# Optimizing a Trainium2 kernel written in Bass

```python
import numpy as np
import jax
import jax.numpy as jnp

def _softmax(x, axis=-1):
    return jax.nn.softmax(x, axis=axis)

def _gelu(x):
    return jax.nn.gelu(x, approximate=True)

def _silu(x):
    return jax.nn.silu(x)

def _sigmoid(x):
    return jax.nn.sigmoid(x)

def _layernorm(x, axis=-1, eps=1e-05):
    m = jnp.mean(x, axis=axis, keepdims=True)
    v = jnp.var(x, axis=axis, keepdims=True)
    return (x - m) / jnp.sqrt(v + eps)

def _scatter_add(tgt, idx, src, axis=0):
    return tgt.at[idx].add(src)

def _segment_sum(src, seg, n):
    return jax.ops.segment_sum(src, seg, n)
kernel_name = 'mk_adaln_d2_jaxref_r8_d5205c'

def setup_inputs(seed: int=0):
    np.random.seed(seed)
    _w = jnp.asarray

    def _L0_attn_setup():
        import jax, jax.numpy as jnp
        import numpy as np
        EMBED = 128
        HEADS = 16
        HEAD_DIM = EMBED // HEADS
        B, T = (2, 256)
        ROPE_THETA = 10000.0

        def _rope(x):
            D = x.shape[-1]
            inv_freq = 1.0 / ROPE_THETA ** (jnp.arange(0, D, 2, dtype=jnp.float32) / D)
            freqs = jnp.arange(x.shape[2], dtype=jnp.float32)[:, None] * inv_freq[None, :]
            cos = jnp.cos(freqs).astype(x.dtype)
            sin = jnp.sin(freqs).astype(x.dtype)
            x1, x2 = (x[..., :D // 2], x[..., D // 2:])
            return jnp.concatenate([x1 * cos - x2 * sin, x2 * cos + x1 * sin], axis=-1)
        key = jax.random.key(seed)
        ks = jax.random.split(key, 5)
        s = 1.0 / np.sqrt(EMBED)
        return {'x': jax.random.normal(ks[0], (B, T, EMBED), dtype=jnp.float32), 'Wq': jax.random.normal(ks[1], (EMBED, EMBED), dtype=jnp.float32) * s, 'bq': jnp.zeros((EMBED,), dtype=jnp.float32), 'Wk': jax.random.normal(ks[2], (EMBED, EMBED), dtype=jnp.float32) * s, 'bk': jnp.zeros((EMBED,), dtype=jnp.float32), 'Wv': jax.random.normal(ks[3], (EMBED, EMBED), dtype=jnp.float32) * s, 'bv': jnp.zeros((EMBED,), dtype=jnp.float32), 'Wo': jax.random.normal(ks[4], (EMBED, EMBED), dtype=jnp.float32) * s, 'bo': jnp.zeros((EMBED,), dtype=jnp.float32)}
    _L0_attn_in = _L0_attn_setup()

    def _L0_ffn_setup():
        import jax, jax.numpy as jnp
        import numpy as np
        TOP_K = 2
        EPS = 1e-05

        def layer_norm(x, g, b):
            mu = jnp.mean(x, axis=-1, keepdims=True)
            var = jnp.mean(jnp.square(x - mu), axis=-1, keepdims=True)
            return (x - mu) * jax.lax.rsqrt(var + EPS) * g + b
        key = jax.random.key(seed)
        ks = jax.random.split(key, 12)
        B, S, D, F, E = (2, 256, 128, 512, 8)
        std = 0.02
        return {'x': jax.random.normal(ks[0], (B, S, D), jnp.float32), 'g1': jnp.ones((D,), jnp.float32), 'be1': jnp.zeros((D,), jnp.float32), 'mix_w': jax.random.normal(ks[1], (D, D), jnp.float32) * std, 'mix_b': jnp.zeros((D,), jnp.float32), 'g2': jnp.ones((D,), jnp.float32), 'be2': jnp.zeros((D,), jnp.float32), 'router_w': jax.random.normal(ks[2], (D, E), jnp.float32) * std, 'w1': jax.random.normal(ks[3], (E, D, F), jnp.float32) * std, 'b1': jnp.zeros((E, F), jnp.float32), 'w2': jax.random.normal(ks[4], (E, F, D), jnp.float32) * std, 'b2': jnp.zeros((E, D), jnp.float32)}
    _L0_ffn_in = _L0_ffn_setup()
    _L0_c = _w((lambda *s: np.random.randn(*s).astype(np.float32) * 0.05)(8, 128))
    _L0_wmod = _w((lambda *s: np.random.randn(*s).astype(np.float32) * 0.05)(128, 6 * 128) * 128 ** (-0.5))

    def _L1_attn_setup():
        import jax, jax.numpy as jnp
        import numpy as np
        B, S, D, H, DOUT = (4, 256, 128, 4, 128)
        key = jax.random.key(seed)
        ks = jax.random.split(key, 11)
        x = jax.random.normal(ks[0], (B, S, D), dtype=jnp.float32)
        phase = jax.random.normal(ks[1], (H, D), dtype=jnp.float32) * 0.02
        sc = 1.0 / np.sqrt(D)
        Wq = jax.random.normal(ks[2], (D, H * D), dtype=jnp.float32) * sc
        bq = jnp.zeros((H * D,), dtype=jnp.float32)
        Wk = jax.random.normal(ks[3], (D, H * D), dtype=jnp.float32) * sc
        bk = jnp.zeros((H * D,), dtype=jnp.float32)
        Wv = jax.random.normal(ks[4], (D, H * D), dtype=jnp.float32) * sc
        bv = jnp.zeros((H * D,), dtype=jnp.float32)
        Wo = jax.random.normal(ks[5], (H * D, DOUT), dtype=jnp.float32) / np.sqrt(H * D)
        bo = jnp.zeros((DOUT,), dtype=jnp.float32)
        return {'x': x, 'phase': phase, 'Wq': Wq, 'bq': bq, 'Wk': Wk, 'bk': bk, 'Wv': Wv, 'bv': bv, 'Wo': Wo, 'bo': bo}
    _L1_attn_in = _L1_attn_setup()

    def _L1_ffn_setup():
        import jax, jax.numpy as jnp
        import numpy as np
        DIM = 128
        DEPTH = 6
        HEADS = 16
        DIM_HEAD = 64
        WINDOW = 32
        INNER = HEADS * DIM_HEAD
        DIM_INNER = int(DIM * 4 * 2 / 3)
        QK_SCALE = 8.0

        def shift_tokens(t):
            a, s = jnp.split(t, 2, -1)
            s = jnp.pad(s, ((0, 0), (1, 0), (0, 0)))[:, :-1]
            return jnp.concatenate([a, s], -1)

        def l2norm(t):
            return t / jnp.maximum(jnp.linalg.norm(t, axis=-1, keepdims=True), 1e-12)

        def rotate_half(x):
            x1, x2 = jnp.split(x, 2, -1)
            return jnp.concatenate([-x2, x1], -1)

        def rotary_tables(n):
            half = jnp.arange(0, DIM_HEAD, 2, dtype=jnp.float32)
            inv_freq = 1.0 / 10000.0 ** (half / DIM_HEAD)
            t = jnp.arange(n, dtype=jnp.float32)
            freqs = t[:, None] * inv_freq[None, :]
            freqs = jnp.concatenate([freqs, freqs], -1)
            base_scale = (half + 0.4 * DIM_HEAD) / (1.4 * DIM_HEAD)
            power = (t - n // 2) / (WINDOW // 2)
            scale = base_scale[None, :] ** power[:, None]
            scale = jnp.concatenate([scale, scale], -1)
            return (freqs, scale)

        def local_attention(q, k, v):
            b, h, n, d = q.shape
            w = WINDOW
            nw = n // w
            bq = q.reshape(b, h, nw, w, d)
            bk = k.reshape(b, h, nw, w, d)
            bv = v.reshape(b, h, nw, w, d)

            def look(t):
                p = jnp.pad(t, ((0, 0), (0, 0), (1, 0), (0, 0), (0, 0)))
                return jnp.concatenate([p[:, :, :nw], p[:, :, 1:]], axis=3)
            bk2, bv2 = (look(bk), look(bv))
            seq = jnp.arange(n).reshape(nw, w)
            seq_p = jnp.pad(seq, ((1, 0), (0, 0)), constant_values=-1)
            jt = jnp.concatenate([seq_p[:nw], seq_p[1:]], axis=1)
            it = seq[:, :, None]
            jb = jt[:, None, :]
            mask = (it < jb) | (it > jb + w) | (jb == -1)
            sim = jnp.einsum('bhwie,bhwje->bhwij', bq, bk2) * QK_SCALE
            sim = jnp.where(mask, -jnp.finfo(sim.dtype).max, sim)
            attn = jax.nn.softmax(sim, -1)
            out = jnp.einsum('bhwij,bhwje->bhwie', attn, bv2)
            return out.reshape(b, h, n, d)

        def attn_layer(x, Wqkv, qs, ksc, Wo):
            b, n, _ = x.shape
            qkv = x @ Wqkv
            q, k, v = jnp.split(qkv, 3, -1)
            sh = lambda t: t.reshape(b, n, HEADS, DIM_HEAD).transpose(0, 2, 1, 3)
            q, k, v = (sh(q), sh(k), sh(v))
            q = l2norm(q) * qs
            k = l2norm(k) * ksc
            freqs, scale = rotary_tables(n)
            cos, sin = (jnp.cos(freqs), jnp.sin(freqs))
            q = q * cos * scale + rotate_half(q) * sin * scale
            inv = 1.0 / scale
            k = k * cos * inv + rotate_half(k) * sin * inv
            out = local_attention(q, k, v)
            out = out.transpose(0, 2, 1, 3).reshape(b, n, INNER)
            return out @ Wo

        def ffn_layer(x, g, bln, W1, b1, W2, b2):
            mu = x.mean(-1, keepdims=True)
            var = ((x - mu) ** 2).mean(-1, keepdims=True)
            xn = (x - mu) / jnp.sqrt(var + 1e-05) * g + bln
            hg = xn @ W1 + b1
            a, gate = jnp.split(hg, 2, -1)
            return a * jax.nn.gelu(gate, approximate=False) @ W2 + b2
        key = jax.random.key(seed)
        ks = jax.random.split(key, 8)
        B, N = (2, 256)
        init = lambda k, shape: jax.random.normal(k, shape, jnp.float32) * 0.02
        return {'x': jax.random.normal(ks[0], (B, N, DIM), jnp.float32), 'Wqkv': init(ks[1], (DEPTH, DIM, 3 * INNER)), 'q_scale': jnp.ones((DEPTH, DIM_HEAD), jnp.float32), 'k_scale': jnp.ones((DEPTH, DIM_HEAD), jnp.float32), 'Wo': init(ks[2], (DEPTH, INNER, DIM)), 'ln_g': jnp.ones((DEPTH, DIM), jnp.float32), 'ln_b': jnp.zeros((DEPTH, DIM), jnp.float32), 'W1': init(ks[3], (DEPTH, DIM, 2 * DIM_INNER)), 'b1': jnp.zeros((DEPTH, 2 * DIM_INNER), jnp.float32), 'W2': init(ks[4], (DEPTH, DIM_INNER, DIM)), 'b2': jnp.zeros((DEPTH, DIM), jnp.float32)}
    _L1_ffn_in = _L1_ffn_setup()
    _L1_c = _w((lambda *s: np.random.randn(*s).astype(np.float32) * 0.05)(8, 128))
    _L1_wmod = _w((lambda *s: np.random.randn(*s).astype(np.float32) * 0.05)(128, 6 * 128) * 128 ** (-0.5))
    _d = {'L0_attn_x': _L0_attn_in['x'], 'L0_attn_Wq': _L0_attn_in['Wq'], 'L0_attn_bq': _L0_attn_in['bq'], 'L0_attn_Wk': _L0_attn_in['Wk'], 'L0_attn_bk': _L0_attn_in['bk'], 'L0_attn_Wv': _L0_attn_in['Wv'], 'L0_attn_bv': _L0_attn_in['bv'], 'L0_attn_Wo': _L0_attn_in['Wo'], 'L0_attn_bo': _L0_attn_in['bo'], 'L0_ffn_g1': _L0_ffn_in['g1'], 'L0_ffn_be1': _L0_ffn_in['be1'], 'L0_ffn_mix_w': _L0_ffn_in['mix_w'], 'L0_ffn_mix_b': _L0_ffn_in['mix_b'], 'L0_ffn_g2': _L0_ffn_in['g2'], 'L0_ffn_be2': _L0_ffn_in['be2'], 'L0_ffn_router_w': _L0_ffn_in['router_w'], 'L0_ffn_w1': _L0_ffn_in['w1'], 'L0_ffn_b1': _L0_ffn_in['b1'], 'L0_ffn_w2': _L0_ffn_in['w2'], 'L0_ffn_b2': _L0_ffn_in['b2'], 'L0_c': _L0_c, 'L0_wmod': _L0_wmod, 'L1_attn_phase': _L1_attn_in['phase'], 'L1_attn_Wq': _L1_attn_in['Wq'], 'L1_attn_bq': _L1_attn_in['bq'], 'L1_attn_Wk': _L1_attn_in['Wk'], 'L1_attn_bk': _L1_attn_in['bk'], 'L1_attn_Wv': _L1_attn_in['Wv'], 'L1_attn_bv': _L1_attn_in['bv'], 'L1_attn_Wo': _L1_attn_in['Wo'], 'L1_attn_bo': _L1_attn_in['bo'], 'L1_ffn_Wqkv': _L1_ffn_in['Wqkv'], 'L1_ffn_q_scale': _L1_ffn_in['q_scale'], 'L1_ffn_k_scale': _L1_ffn_in['k_scale'], 'L1_ffn_Wo': _L1_ffn_in['Wo'], 'L1_ffn_ln_g': _L1_ffn_in['ln_g'], 'L1_ffn_ln_b': _L1_ffn_in['ln_b'], 'L1_ffn_W1': _L1_ffn_in['W1'], 'L1_ffn_b1': _L1_ffn_in['b1'], 'L1_ffn_W2': _L1_ffn_in['W2'], 'L1_ffn_b2': _L1_ffn_in['b2'], 'L1_c': _L1_c, 'L1_wmod': _L1_wmod}
    _x0 = _d['L0_attn_x']
    _d['L0_attn_x'] = jax.random.normal(jax.random.fold_in(jax.random.key(seed), 1), (8, 512, 128), dtype=_x0.dtype)
    del _x0
    return _d

def reference(L0_attn_x, L0_attn_Wq, L0_attn_bq, L0_attn_Wk, L0_attn_bk, L0_attn_Wv, L0_attn_bv, L0_attn_Wo, L0_attn_bo, L0_ffn_g1, L0_ffn_be1, L0_ffn_mix_w, L0_ffn_mix_b, L0_ffn_g2, L0_ffn_be2, L0_ffn_router_w, L0_ffn_w1, L0_ffn_b1, L0_ffn_w2, L0_ffn_b2, L0_c, L0_wmod, L1_attn_phase, L1_attn_Wq, L1_attn_bq, L1_attn_Wk, L1_attn_bk, L1_attn_Wv, L1_attn_bv, L1_attn_Wo, L1_attn_bo, L1_ffn_Wqkv, L1_ffn_q_scale, L1_ffn_k_scale, L1_ffn_Wo, L1_ffn_ln_g, L1_ffn_ln_b, L1_ffn_W1, L1_ffn_b1, L1_ffn_W2, L1_ffn_b2, L1_c, L1_wmod):

    def _L0_attn_ref(x, Wq, bq, Wk, bk, Wv, bv, Wo, bo):
        import jax, jax.numpy as jnp
        import numpy as np
        EMBED = 128
        HEADS = 16
        HEAD_DIM = EMBED // HEADS
        B, T = (2, 256)
        ROPE_THETA = 10000.0

        def _rope(x):
            D = x.shape[-1]
            inv_freq = 1.0 / ROPE_THETA ** (jnp.arange(0, D, 2, dtype=jnp.float32) / D)
            freqs = jnp.arange(x.shape[2], dtype=jnp.float32)[:, None] * inv_freq[None, :]
            cos = jnp.cos(freqs).astype(x.dtype)
            sin = jnp.sin(freqs).astype(x.dtype)
            x1, x2 = (x[..., :D // 2], x[..., D // 2:])
            return jnp.concatenate([x1 * cos - x2 * sin, x2 * cos + x1 * sin], axis=-1)
        Bb, Tt, C = x.shape
        H, D = (HEADS, HEAD_DIM)

        def proj(W, b):
            return (jnp.einsum('btc,oc->bto', x, W) + b).reshape(Bb, Tt, H, D).transpose(0, 2, 1, 3)
        q = _rope(proj(Wq, bq))
        k = _rope(proj(Wk, bk))
        v = proj(Wv, bv)
        scale = jnp.sqrt(jnp.asarray(D, dtype=x.dtype))
        scores = jnp.einsum('bhtd,bhsd->bhts', q, k) / scale
        attn = jax.nn.softmax(scores, axis=-1)
        out = jnp.einsum('bhts,bhsd->bhtd', attn, v)
        out = out.transpose(0, 2, 1, 3).reshape(Bb, Tt, C)
        return jnp.einsum('btc,oc->bto', out, Wo) + bo

    def _L0_ffn_ref(x, g1, be1, mix_w, mix_b, g2, be2, router_w, w1, b1, w2, b2):
        import jax, jax.numpy as jnp
        import numpy as np
        TOP_K = 2
        EPS = 1e-05

        def layer_norm(x, g, b):
            mu = jnp.mean(x, axis=-1, keepdims=True)
            var = jnp.mean(jnp.square(x - mu), axis=-1, keepdims=True)
            return (x - mu) * jax.lax.rsqrt(var + EPS) * g + b
        res = x
        n = layer_norm(x, g1, be1)
        x = res + n + (n @ mix_w + mix_b)
        res = x
        n = layer_norm(x, g2, be2)
        B, S, D = n.shape
        E = w1.shape[0]
        flat = n.reshape(-1, D)
        probs = jax.nn.softmax(flat @ router_w, axis=-1)
        topw, topi = jax.lax.top_k(probs, TOP_K)
        combine = jnp.sum(jax.nn.one_hot(topi, E, dtype=flat.dtype) * topw[..., None], axis=1)
        h = jax.nn.silu(jnp.einsum('td,edf->tef', flat, w1) + b1)
        y = jnp.einsum('tef,efd->ted', h, w2) + b2
        out = jnp.einsum('te,ted->td', combine, y)
        return res + out.reshape(B, S, D)

    def _L1_attn_ref(x, phase, Wq, bq, Wk, bk, Wv, bv, Wo, bo):
        import jax, jax.numpy as jnp
        import numpy as np
        B, S, D, H, DOUT = (4, 256, 128, 4, 128)
        b, s, d = x.shape
        h = phase.shape[0]
        q = (x @ Wq + bq).reshape(b, s, h, d)
        k = (x @ Wk + bk).reshape(b, s, h, d)
        v = (x @ Wv + bv).reshape(b, s, h, d)
        c, sn = (jnp.cos(phase), jnp.sin(phase))
        qr, qi = (q * c, q * sn)
        kr, ki = (k * c, k * sn)
        scale = 1.0 / np.sqrt(d)
        scores = (jnp.einsum('bshd,bsgd->bshg', qr, kr) + jnp.einsum('bshd,bsgd->bshg', qi, ki)) * scale
        attn = jax.nn.softmax(scores, axis=-1)
        out = jnp.einsum('bshg,bsgd->bshd', attn, v)
        out = jnp.swapaxes(out, 1, 2).reshape(b, s, h * d)
        return out @ Wo + bo

    def _L1_ffn_ref(x, Wqkv, q_scale, k_scale, Wo, ln_g, ln_b, W1, b1, W2, b2):
        import jax, jax.numpy as jnp
        import numpy as np
        DIM = 128
        DEPTH = 6
        HEADS = 16
        DIM_HEAD = 64
        WINDOW = 32
        INNER = HEADS * DIM_HEAD
        DIM_INNER = int(DIM * 4 * 2 / 3)
        QK_SCALE = 8.0

        def shift_tokens(t):
            a, s = jnp.split(t, 2, -1)
            s = jnp.pad(s, ((0, 0), (1, 0), (0, 0)))[:, :-1]
            return jnp.concatenate([a, s], -1)

        def l2norm(t):
            return t / jnp.maximum(jnp.linalg.norm(t, axis=-1, keepdims=True), 1e-12)

        def rotate_half(x):
            x1, x2 = jnp.split(x, 2, -1)
            return jnp.concatenate([-x2, x1], -1)

        def rotary_tables(n):
            half = jnp.arange(0, DIM_HEAD, 2, dtype=jnp.float32)
            inv_freq = 1.0 / 10000.0 ** (half / DIM_HEAD)
            t = jnp.arange(n, dtype=jnp.float32)
            freqs = t[:, None] * inv_freq[None, :]
            freqs = jnp.concatenate([freqs, freqs], -1)
            base_scale = (half + 0.4 * DIM_HEAD) / (1.4 * DIM_HEAD)
            power = (t - n // 2) / (WINDOW // 2)
            scale = base_scale[None, :] ** power[:, None]
            scale = jnp.concatenate([scale, scale], -1)
            return (freqs, scale)

        def local_attention(q, k, v):
            b, h, n, d = q.shape
            w = WINDOW
            nw = n // w
            bq = q.reshape(b, h, nw, w, d)
            bk = k.reshape(b, h, nw, w, d)
            bv = v.reshape(b, h, nw, w, d)

            def look(t):
                p = jnp.pad(t, ((0, 0), (0, 0), (1, 0), (0, 0), (0, 0)))
                return jnp.concatenate([p[:, :, :nw], p[:, :, 1:]], axis=3)
            bk2, bv2 = (look(bk), look(bv))
            seq = jnp.arange(n).reshape(nw, w)
            seq_p = jnp.pad(seq, ((1, 0), (0, 0)), constant_values=-1)
            jt = jnp.concatenate([seq_p[:nw], seq_p[1:]], axis=1)
            it = seq[:, :, None]
            jb = jt[:, None, :]
            mask = (it < jb) | (it > jb + w) | (jb == -1)
            sim = jnp.einsum('bhwie,bhwje->bhwij', bq, bk2) * QK_SCALE
            sim = jnp.where(mask, -jnp.finfo(sim.dtype).max, sim)
            attn = jax.nn.softmax(sim, -1)
            out = jnp.einsum('bhwij,bhwje->bhwie', attn, bv2)
            return out.reshape(b, h, n, d)

        def attn_layer(x, Wqkv, qs, ksc, Wo):
            b, n, _ = x.shape
            qkv = x @ Wqkv
            q, k, v = jnp.split(qkv, 3, -1)
            sh = lambda t: t.reshape(b, n, HEADS, DIM_HEAD).transpose(0, 2, 1, 3)
            q, k, v = (sh(q), sh(k), sh(v))
            q = l2norm(q) * qs
            k = l2norm(k) * ksc
            freqs, scale = rotary_tables(n)
            cos, sin = (jnp.cos(freqs), jnp.sin(freqs))
            q = q * cos * scale + rotate_half(q) * sin * scale
            inv = 1.0 / scale
            k = k * cos * inv + rotate_half(k) * sin * inv
            out = local_attention(q, k, v)
            out = out.transpose(0, 2, 1, 3).reshape(b, n, INNER)
            return out @ Wo

        def ffn_layer(x, g, bln, W1, b1, W2, b2):
            mu = x.mean(-1, keepdims=True)
            var = ((x - mu) ** 2).mean(-1, keepdims=True)
            xn = (x - mu) / jnp.sqrt(var + 1e-05) * g + bln
            hg = xn @ W1 + b1
            a, gate = jnp.split(hg, 2, -1)
            return a * jax.nn.gelu(gate, approximate=False) @ W2 + b2
        for i in range(DEPTH):
            x = attn_layer(shift_tokens(x), Wqkv[i], q_scale[i], k_scale[i], Wo[i]) + x
            x = ffn_layer(shift_tokens(x), ln_g[i], ln_b[i], W1[i], b1[i], W2[i], b2[i]) + x
        return x
    x = L0_attn_x
    mod = (_silu(L0_c) @ L0_wmod).reshape(L0_c.shape[0], 6, 1, -1)
    sa, ca, ga, sb, cb, gb = (mod[:, 0], mod[:, 1], mod[:, 2], mod[:, 3], mod[:, 4], mod[:, 5])
    ga = (2 * (ga >= 0) - 1) * jnp.maximum(jnp.abs(ga), 0.25)
    gb = (2 * (gb >= 0) - 1) * jnp.maximum(jnp.abs(gb), 0.25)
    h = _layernorm(x, axis=-1) * (1 + ca) + sa
    x = x + ga * _L0_attn_ref(h, L0_attn_Wq, L0_attn_bq, L0_attn_Wk, L0_attn_bk, L0_attn_Wv, L0_attn_bv, L0_attn_Wo, L0_attn_bo)
    h = _layernorm(x, axis=-1) * (1 + cb) + sb
    x = x + gb * _L0_ffn_ref(h, L0_ffn_g1, L0_ffn_be1, L0_ffn_mix_w, L0_ffn_mix_b, L0_ffn_g2, L0_ffn_be2, L0_ffn_router_w, L0_ffn_w1, L0_ffn_b1, L0_ffn_w2, L0_ffn_b2)
    mod = (_silu(L1_c) @ L1_wmod).reshape(L1_c.shape[0], 6, 1, -1)
    sa, ca, ga, sb, cb, gb = (mod[:, 0], mod[:, 1], mod[:, 2], mod[:, 3], mod[:, 4], mod[:, 5])
    ga = (2 * (ga >= 0) - 1) * jnp.maximum(jnp.abs(ga), 0.25)
    gb = (2 * (gb >= 0) - 1) * jnp.maximum(jnp.abs(gb), 0.25)
    h = _layernorm(x, axis=-1) * (1 + ca) + sa
    x = x + ga * _L1_attn_ref(h, L1_attn_phase, L1_attn_Wq, L1_attn_bq, L1_attn_Wk, L1_attn_bk, L1_attn_Wv, L1_attn_bv, L1_attn_Wo, L1_attn_bo)
    h = _layernorm(x, axis=-1) * (1 + cb) + sb
    x = x + gb * _L1_ffn_ref(h, L1_ffn_Wqkv, L1_ffn_q_scale, L1_ffn_k_scale, L1_ffn_Wo, L1_ffn_ln_g, L1_ffn_ln_b, L1_ffn_W1, L1_ffn_b1, L1_ffn_W2, L1_ffn_b2)
    return x

_drawn_inputs = setup_inputs


def setup_inputs(seed=0):
    import zlib

    import numpy as np

    out = dict(_drawn_inputs(seed))
    spreads = {'L0_attn_bq': (0.0, 0.8),
     'L0_attn_bk': (0.0, 0.8),
     'L0_attn_bv': (0.0, 0.338),
     'L0_attn_bo': (0.0, 0.321),
     'L0_ffn_g1': (1.0, 0.2),
     'L0_ffn_be1': (0.0, 0.321),
     'L0_ffn_mix_b': (0.0, 0.341),
     'L0_ffn_g2': (1.0, 0.6),
     'L0_ffn_be2': (0.0, 0.8),
     'L0_ffn_b1': (0.0, 0.8),
     'L0_ffn_b2': (0.0, 0.8),
     'L1_attn_bq': (0.0, 0.8),
     'L1_attn_bk': (0.0, 0.8),
     'L1_attn_bv': (0.0, 0.554),
     'L1_attn_bo': (0.0, 0.379),
     'L1_ffn_q_scale': (1.0, 0.6),
     'L1_ffn_k_scale': (1.0, 0.6),
     'L1_ffn_ln_g': (1.0, 0.6),
     'L1_ffn_ln_b': (0.0, 0.8),
     'L1_ffn_b1': (0.0, 0.8),
     'L1_ffn_b2': (0.0, 0.8)}
    factors = {'L0_attn_Wq': 2.779,
     'L0_attn_Wk': 2.682,
     'L0_ffn_router_w': 8.0,
     'L0_ffn_w1': 8.0,
     'L0_ffn_w2': 8.0,
     'L1_attn_phase': 64.0,
     'L1_ffn_W1': 8.0,
     'L1_ffn_W2': 8.0}
    for name, (base, spread) in spreads.items():
        noise = np.random.default_rng([zlib.crc32(name.encode()), seed]).standard_normal(out[name].shape)
        drawn = base * np.exp(spread * noise) if base else spread * noise
        out[name] = jnp.asarray(drawn.astype(out[name].dtype))
    for name, factor in factors.items():
        out[name] = (out[name] * factor).astype(out[name].dtype)
    return out
```

```python
from contextlib import ExitStack

import numpy as np

import concourse.bass as bass
from concourse import mybir

F32 = mybir.dt.float32
BF16 = mybir.dt.bfloat16
ACT = mybir.ActivationFunctionType
ALU = mybir.AluOpType
AX_X = mybir.AxisListType.X

B, T, D = 8, 512, 128
P = 128
TT = T // P
EPS = 1e-5
BANK = 512
NEG = -1e30

H0, HD0 = 16, 8
E0, F0 = 8, 512
H1, HD1, TB = 4, 128, 32
DEPTH, H2, HD2, WIN = 6, 16, 64, 32
INNER = H2 * HD2
QK_SCALE = 8.0
DI = 341
PADW = WIN + 1
XW = PADW + T
LN_RANGE = 2.0 ** 20


def constants():
    f = np.float32
    c = {}
    c["ident"] = np.eye(P, dtype=f)
    c["mean"] = np.full((P, P), 1.0 / P, f)
    c["center"] = (np.eye(P) - 1.0 / P).astype(f)
    half = HD0 // 2
    inv = (1.0 / f(10000.0) ** (np.arange(0, HD0, 2, dtype=f) / f(HD0))).astype(f)
    ang = (np.arange(T, dtype=f)[:, None] * inv[None, :]).astype(f)
    d = np.arange(P) % HD0
    c["cos0"] = np.cos(ang).astype(f).T[d % half].copy()
    c["sin0"] = (np.sin(ang).astype(f).T[d % half] * np.where(d < half, -1, 1)[:, None]).astype(f)
    other = np.arange(P) + np.where(d < half, half, -half)
    swap = np.zeros((P, P), f)
    swap[other, np.arange(P)] = 1
    c["swap0"] = swap
    c["headmask0"] = (np.arange(P)[:, None] // HD0 == np.arange(H0)[None, :]).astype(f)
    pick = np.zeros((P, H0, P), f)
    for part in range(3):
        for h in range(H0):
            pick[32 * part + h, h, :] = 1
    c["pick"] = pick.reshape(P, H0 * P)
    c["lower"] = np.broadcast_to(np.tril(np.ones((E0, E0), f), -1).reshape(1, -1), (P, E0 * E0)).copy()
    t = np.arange(P) % TB
    c["mask1"] = np.where(t[:, None] == t[None, :], 0, NEG).astype(f)
    q = (np.arange(P) % WIN)[:, None]
    k = np.arange(2 * WIN)[None, :]
    ok = (q <= k) & (q >= k - WIN)
    first = ok & ((np.arange(P)[:, None] >= 64) | (k >= WIN))
    c["mask2"] = np.concatenate([np.where(ok, 0, NEG), np.where(first, 0, NEG)], 1).astype(f)
    hf = np.arange(0, HD2, 2, dtype=f)
    inv = (1.0 / f(10000.0) ** (hf / f(HD2))).astype(f)
    tok = np.arange(T, dtype=f)
    ang = (tok[:, None] * inv[None, :]).astype(f)
    ang = np.concatenate([ang, ang], 1)
    base = ((hf + f(0.4 * HD2)) / f(1.4 * HD2)).astype(f)
    power = ((tok - T // 2) / f(WIN // 2)).astype(f)
    scale = (base[None, :] ** power[:, None]).astype(f)
    scale = np.concatenate([scale, scale], 1)
    sign = np.where(np.arange(HD2) < HD2 // 2, -1, 1).astype(f)
    cos, sin = np.cos(ang).astype(f), (np.sin(ang) * sign).astype(f)
    co = np.stack([cos * scale, cos / scale], 1).reshape(TT, P, 2, HD2).transpose(1, 0, 2, 3)
    si = np.stack([sin * scale, sin / scale], 1).reshape(TT, P, 2, HD2).transpose(1, 0, 2, 3)
    c["cos2"] = np.ascontiguousarray(co.reshape(P, -1)).astype(f)
    c["sin2"] = np.ascontiguousarray(si.reshape(P, -1)).astype(f)
    return c


def column(v):
    return v.rearrange("(p one) -> p one", one=1)


def across(v, n=P):
    return v.partition_broadcast(n)


class Core:

    def __init__(self, nc, ctx):
        self.nc, self.ctx = nc, ctx

    def sb(self, ctx, name, shape, dt=F32):
        return ctx.enter_context(self.nc.sbuf_tensor(name, shape, dt))

    def ps(self, ctx, name, shape, dt=F32):
        return ctx.enter_context(self.nc.psum_tensor(name, shape, dt))

    def sem(self, name):
        return self.ctx.enter_context(self.nc.semaphore(name))


def prelude(core, A, C):
    nc = core.nc
    loaded, small, cast = core.sem("x_loaded"), core.sem("small_loaded"), core.sem("pick_loaded")
    turned, taken = core.sem("x_turned"), core.sem("x_taken")
    silu_ready, silu_turned, silu_t_ready = core.sem("silu_ready"), core.sem("silu_turned"), core.sem("silu_t_ready")
    mod_done, gate_step = core.sem("mod_done"), core.sem("gate_step")
    w_turned, w_taken = core.sem("w_turned"), core.sem("w_taken")
    bias_turned = core.sem("bias_turned")
    S = core
    with ExitStack() as ctx:
        xt = core.sb(ctx, "x_tokens", [P, B * TT, P])
        cc = core.sb(ctx, "cond", [B, 2, P])
        sc = core.sb(ctx, "cond_silu", [B, 2, P])
        sct = core.sb(ctx, "cond_silu_t", [P, 2, B])
        wmod = core.sb(ctx, "wmod", [P, 2, 6 * P])
        w4 = core.sb(ctx, "w_l0", [P, 4, P])
        sg = core.sb(ctx, "gate_sign", [P, 2 * B])
        ab = core.sb(ctx, "gate_size", [P, 2 * B])
        ra = core.sb(ctx, "gate_raw", [P, 2 * B])
        px = core.ps(ctx, "px", [P, 4, BANK])
        pm = core.ps(ctx, "pm", [P, 2, BANK])
        pw = core.ps(ctx, "pw", [P, 2, BANK])
        names = ["L0_attn_Wq", "L0_attn_Wk", "L0_attn_Wv", "L0_attn_Wo"]
        NSMALL = 7 + 2 + 2 + 4 + 4
        with nc.Block() as block:
            @block.sync
            def _(sp):
                for g in range(4):
                    sp.dma_start(xt[:, 8 * g:8 * g + 8, :],
                                 A["L0_attn_x"].rearrange("b t d -> (b t) d")[1024 * g:1024 * g + 1024, :]
                                 .rearrange("(n p) d -> p n d", p=P)).then_inc(loaded, 16)
                for n, ap in (("L0_attn_bk", S.bq[:, 1:2]), ("L0_attn_bq", S.bq[:, 0:1]), ("L0_attn_bo", S.bo0[:, :])):
                    sp.dma_start(ap, column(A[n])).then_inc(small, 16)
                sp.dma_start(S.bv0[:, :], across(A["L0_attn_bv"])).then_inc(small, 16)
                sp.wait_ge(loaded, 64)
                sp.wait_ge(small, 16 * NSMALL)

            @block.gpsimd
            def _(pool):
                pool.dma_start(S.pick[:, :, :].rearrange("p h m -> p (h m)"), C["pick"]).then_inc(cast, 16)
                pool.dma_start(S.identb[:, :], C["ident"]).then_inc(cast, 16)
                pool.memset(S.xa[:, :, 0:PADW], 0.0)
                pool.memset(S.xb[:, :, 0:PADW], 0.0)
                pool.wait_ge(cast, 32)

            @block.tensor
            def _(pe):
                pe.wait_ge(small, 16 * NSMALL)
                pe.wait_ge(silu_ready, 1)
                for l in range(2):
                    tr = pe.transpose(pm[:, 0, 8 * l:8 * l + 8], sc[:, l, :], S.ident[0:B, 0:B])
                tr.then_inc(silu_turned, 1)
                pe.transpose(pw[:, 0, 0:128], w4[:, 0, :], S.ident[:, :])
                pe.transpose(pw[:, 0, 128:256], w4[:, 1, :], S.ident[:, :])
                pe.transpose(pw[:, 0, 256:384], w4[:, 2, :], S.ident[:, :])
                pe.transpose(pw[:, 0, 384:512], w4[:, 3, :], S.ident[:, :]).then_inc(w_turned, 1)
                pe.matmul(pw[:, 1, 0:128], w4[:, 0, :], S.swap0[:, :], start=True, stop=True)
                pe.matmul(pw[:, 1, 128:256], w4[:, 1, :], S.swap0[:, :], start=True, stop=True)
                pe.matmul(pw[:, 1, 256:258], S.swap0[:, :], S.bq[:, 0:2], start=True, stop=True).then_inc(w_turned, 1)
                pe.wait_ge(silu_t_ready, 1)
                for l in range(2):
                    for j in range(6):
                        at = (l * 6 + j) * B
                        mm = pe.matmul(pm[:, 1, at:at + B], wmod[:, l, P * j:P * j + P], sct[:, l, :],
                                       start=True, stop=True)
                mm.then_inc(mod_done, 1)
                pe.wait_ge(loaded, 64)
                for n in range(B * TT // 4):
                    if n >= 4:
                        pe.wait_ge(taken, n - 3)
                    for c in range(4):
                        tr = pe.transpose(px[:, n % 4, P * c:P * c + P], xt[:, 4 * n + c, :], S.ident[:, :])
                    tr.then_inc(turned, 1)

            @block.scalar
            def _(act):
                for n, ap in (("ident", S.ident), ("mean", S.mean), ("center", S.center), ("cos0", S.cos0),
                              ("sin0", S.sin0), ("swap0", S.swap0), ("headmask0", S.headmask0)):
                    act.dma_start(ap[:, :], C[n]).then_inc(small, 16)
                for l in range(2):
                    act.dma_start(cc[:, l, :], A[f"L{l}_c"]).then_inc(small, 16)
                    act.dma_start(wmod[:, l, :], A[f"L{l}_wmod"]).then_inc(small, 16)
                for i, n in enumerate(names):
                    act.dma_start(w4[:, i, :], A[n]).then_inc(small, 16)
                act.wait_ge(small, 16 * NSMALL)
                act.activation(sc[:, :, :], cc[:, :, :], ACT.Silu).then_inc(silu_ready, 1)
                for n in range(B * TT // 4):
                    act.wait_ge(turned, n + 1)
                    act.activation(S.xr[:, n, :], px[:, n % 4, :], ACT.Identity).then_inc(taken, 1)

            @block.vector
            def _(dve):
                dve.wait_ge(silu_turned, 1)
                dve.tensor_copy(sct[:, :, :].rearrange("p l b -> p (l b)"), pm[:, 0, 0:2 * B]).then_inc(silu_t_ready, 1)
                dve.wait_ge(w_turned, 1)
                dve.tensor_copy(S.w0[:, 0:4, :].rearrange("p n m -> p (n m)"), pw[:, 0, :])
                dve.wait_ge(w_turned, 2)
                dve.tensor_copy(S.w0[:, 4:6, :].rearrange("p n m -> p (n m)"), pw[:, 1, 0:256])
                dve.tensor_copy(S.bq[:, 2:4], pw[:, 1, 256:258])
                dve.wait_ge(mod_done, 1)
                m = pm[:, 1, 0:12 * B].rearrange("p (l j b) -> p l j b", l=2, j=6)
                for j in (0, 3):
                    dve.tensor_copy(S.mod[:, :, j, :], m[:, :, j, :])
                for j in (1, 4):
                    dve.tensor_scalar(S.mod[:, :, j, :], m[:, :, j, :], 1.0, None, ALU.add)
                n = 0
                for j in (2, 5):
                    raw = ra[:, :].rearrange("p (l b) -> p l b", l=2)
                    sgn, size = sg[:, :].rearrange("p (l b) -> p l b", l=2), ab[:, :].rearrange("p (l b) -> p l b", l=2)
                    for ins in (lambda: dve.tensor_scalar(sgn, m[:, :, j, :], 0.0, 2.0, ALU.is_ge, ALU.mult),
                                lambda: dve.tensor_scalar(sgn, sgn, 1.0, None, ALU.subtract),
                                lambda: dve.tensor_copy(raw, m[:, :, j, :]),
                                lambda: dve.scalar_tensor_tensor(out=size, in0=raw, scalar=-1.0, in1=raw, op0=ALU.mult, op1=ALU.max),
                                lambda: dve.tensor_scalar(size, size, 0.25, None, ALU.max),
                                lambda: dve.tensor_tensor(S.mod[:, :, j, :], sgn, size, ALU.mult)):
                        ins().then_inc(gate_step, 1)
                        n += 1
                        dve.wait_ge(gate_step, n)


def norm_stage(core, source, target, scale, shift, batches=B):
    nc, S = core.nc, core
    U = 4
    S.norms += 1
    tag = f"norm{S.norms}"
    centered, squared, var_done, ln_step, rstd_ready, scaled, done = S.norm_sems

    def stage(before):
        with ExitStack() as ctx:
            pc = core.ps(ctx, tag + "_pc", [P, U, BANK])
            pv = core.ps(ctx, tag + "_pv", [P, U, BANK])
            work = core.sb(ctx, tag + "_work", [P, U, T])
            with nc.Block() as block:
                @block.tensor
                def _(pe):
                    for r in range(batches // U):
                        for u in range(U):
                            b = U * r + u
                            if b >= U:
                                pe.wait_ge(scaled, before + b - U + 1)
                            pe.matmul(pc[:, u, :], S.center[:, :], source(b), start=True, stop=True).then_inc(centered, 1)
                        for u in range(U):
                            b = U * r + u
                            pe.wait_ge(squared, before + b + 1)
                            if b >= U:
                                pe.wait_ge(rstd_ready, before + b - U + 1)
                            pe.matmul(pv[:, u, :], S.mean[:, :], work[:, u, :], start=True, stop=True).then_inc(var_done, 1)

                @block.scalar
                def _(act):
                    act.preload_act_table_set("natural_log_exp_and_others")
                    for r in range(batches // U):
                        for u in range(U):
                            b = U * r + u
                            act.wait_ge(centered, before + b + 1)
                            if b >= U:
                                act.wait_ge(done, before + b - U + 1)
                            act.activation(work[:, u, :], pc[:, u, :], ACT.Square).then_inc(squared, 1)
                        for u in range(U):
                            b = U * r + u
                            act.wait_ge(var_done, before + b + 1)
                            act.activation(work[:, u, :], pv[:, u, :], ACT.Ln, bias=S.eps[:, 0:1]).then_inc(ln_step, 1)
                            act.wait_ge(ln_step, before + b + 1)
                            act.activation(work[:, u, :], work[:, u, :], ACT.Exp, scale=-0.5).then_inc(rstd_ready, 1)

                @block.vector
                def _(dve):
                    for b in range(batches):
                        u = b % U
                        dve.wait_ge(rstd_ready, before + b + 1)
                        dve.tensor_tensor(work[:, u, :], pc[:, u, :], work[:, u, :], ALU.mult).then_inc(scaled, 1)
                        dve.wait_ge(scaled, before + b + 1)
                        dve.tensor_scalar(target(b), work[:, u, :], scale(b), shift(b), ALU.mult, ALU.add).then_inc(done, 1)

    return stage


def attention0(core):
    nc, S = core.nc, core
    names = ("proj_done rope_step q_ready v_done v_ready kmask_ready score_done max_ready maxt_done part_step gated "
             "st_done exp_done pv_done o_ready ot_done onorm_step of_done of_ready y_done x_ready hs_ready "
             "start").split()
    sm = {n: core.sem("a0_" + n) for n in names}
    NS = H0 * TT
    GH = 4
    with ExitStack() as ctx:
        hs = core.sb(ctx, "a0_hs", [P, T])
        ta, tb = core.sb(ctx, "a0_ta", [P, 2, T]), core.sb(ctx, "a0_tb", [P, 2, T])
        qk = core.sb(ctx, "a0_qk", [P, 2, T])
        vv = core.sb(ctx, "a0_v", [P, TT, H0, 32])
        km = core.sb(ctx, "a0_km", [P, H0, T])
        mx = core.sb(ctx, "a0_max", [P, TT, H0])
        rem = core.sb(ctx, "a0_rem", [H0, 2, T])
        mid = core.sb(ctx, "a0_mid", [H0, T], BF16)
        mb = core.sb(ctx, "a0_maxparts", [96, T], BF16)
        pt = core.sb(ctx, "a0_probs", [P, 4, T])
        os_ = core.sb(ctx, "a0_o", [P, 2, T])
        rc = core.sb(ctx, "a0_rsum", [P, TT, GH])
        on = core.sb(ctx, "a0_onorm", [P, TT, P])
        of = core.sb(ctx, "a0_of", [P, T])
        tx = core.sb(ctx, "a0_tx", [P, T])
        ring = core.ps(ctx, "a0_ring", [P, 4, BANK])
        og = core.ps(ctx, "a0_og", [P, 2, BANK])
        t1 = core.ps(ctx, "a0_t1", [P, BANK])
        t2 = core.ps(ctx, "a0_t2", [P, BANK])
        with nc.Block() as block:
            def copy_out(act, b, g):
                act.wait_ge(sm["pv_done"], b * NS + 16 * g + 16)
                if g >= 2:
                    act.wait_ge(sm["ot_done"], b * 4 + g - 1)
                act.activation(os_[:, g % 2, :], og[:, g % 2, :], ACT.Identity).then_inc(sm["o_ready"], 1)

            def maxima(dve, b, h):
                for c in range(TT):
                    n = h * TT + c
                    dve.wait_ge(sm["score_done"], b * NS + n + 1)
                    dve.tensor_reduce(mx[:, c, h:h + 1], ring[:, n % 4, :], AX_X, ALU.max, negate=True).then_inc(sm["max_ready"], 1)

            @block.gpsimd
            def _(pool):
                pool.memset(vv[:, :, :, :].rearrange("p c h m -> p (c h m)"), 0.0).then_inc(sm["start"], 1)
                pool.wait_ge(sm["start"], 1)
                pool.memset(vv[:, :, :, HD0:HD0 + 1], 1.0).then_inc(sm["start"], 1)
                pool.memset(mb[:, :], 0.0).then_inc(sm["start"], 1)
                with pool.Fori(0, B) as b:
                    pool.wait_ge(sm["v_done"], b + 1)
                    pool.tensor_copy(hs[:, :], S.h[:, b, :]).then_inc(sm["hs_ready"], 1)

            @block.tensor
            def _(pe):
                pe.sem_inc(sm["v_done"], 1)
                with pe.Fori(0, B) as b:
                    pe.wait_ge(sm["hs_ready"], b + 1)
                    pe.wait_ge(sm["exp_done"], b * NS + 1)
                    for i, w in enumerate((0, 4, 1, 5)):
                        pe.matmul(ring[:, i, :], S.w0[:, w, :], hs[:, :], start=True, stop=True).then_inc(sm["proj_done"], 1)
                    pe.wait_ge(sm["onorm_step"], b * 8 + 1)
                    for c in range(TT):
                        mm = pe.matmul(t1[:, P * c:P * c + P], hs[:, P * c:P * c + P], S.w0[:, 2, :], start=True, stop=True)
                    mm.then_inc(sm["v_done"], 1)
                    for n in range(NS):
                        h, c = n // TT, n % TT
                        if c == 0:
                            pe.wait_ge(sm["kmask_ready"], b * H0 + h + 1)
                        if n >= 4:
                            pe.wait_ge(sm["max_ready"], b * NS + n - 3)
                        pe.matmul(ring[:, n % 4, :], qk[:, 0, P * c:P * c + P], km[:, h, :], start=True,
                                  stop=True).then_inc(sm["score_done"], 1)
                    pe.wait_ge(sm["max_ready"], b * NS + NS)
                    pe.wait_ge(sm["x_ready"], b + 1)
                    for c in range(TT):
                        tr = pe.transpose(t2[0:H0, P * c:P * c + P], mx[:, c, :], S.ident[:, :])
                    tr.then_inc(sm["maxt_done"], 1)
                    pe.wait_ge(sm["part_step"], b * 6 + 6)

                    def scores(n):
                        h, c = n // TT, n % TT
                        if n >= 4:
                            pe.wait_ge(sm["exp_done"], b * NS + n - 2)
                        pe.matmul(ring[:, n % 4, :], km[:, h, P * c:P * c + P], qk[:, 0, :], start=True, stop=False)
                        pe.matmul(ring[:, n % 4, :], S.pick[0:96, h, :], mb[:, :], start=False,
                                  stop=True).then_inc(sm["st_done"], 1)

                    def weighted(n):
                        h, c = n // TT, n % TT
                        g, j = h // GH, h % GH
                        pe.wait_ge(sm["exp_done"], b * NS + n + 2)
                        if g >= 2 and n % (GH * TT) == 0:
                            pe.wait_ge(sm["o_ready"], b * 4 + g - 1)
                        pe.matmul(og[32 * j:32 * j + 32, g % 2, :], vv[:, c, h, :], pt[:, n % 4, :], start=(c == 0),
                                  stop=(c == TT - 1)).then_inc(sm["pv_done"], 1)

                    def turn_out(g):
                        pe.wait_ge(sm["o_ready"], b * 4 + g + 1)
                        if g:
                            pe.wait_ge(sm["onorm_step"], b * 8 + 2 * g + 1)
                        for c in range(TT):
                            tr = pe.transpose(t1[:, P * c:P * c + P], os_[:, g % 2, P * c:P * c + P], S.ident[:, :])
                        tr.then_inc(sm["ot_done"], 1)

                    LAG = 2
                    for n in range(NS + LAG):
                        if n < NS:
                            scores(n)
                        if n >= LAG:
                            weighted(n - LAG)
                        if n % (GH * TT) == 6 and n > GH * TT:
                            turn_out(n // (GH * TT) - 1)
                    turn_out(3)
                    pe.wait_ge(sm["onorm_step"], b * 8 + 9)
                    for c in range(TT):
                        tr = pe.transpose(t2[:, P * c:P * c + P], on[:, c, :], S.ident[:, :])
                    tr.then_inc(sm["of_done"], 1)
                    pe.wait_ge(sm["of_ready"], b + 1)
                    pe.matmul(t2[:, :], S.w0[:, 3, :], of[:, :], start=True, stop=True).then_inc(sm["y_done"], 1)

            @block.scalar
            def _(act):
                act.preload_act_table_set("natural_log_exp_and_others")
                act.sem_inc(sm["exp_done"], 1)
                with act.Fori(0, B) as b:
                    for n in range(NS):
                        act.wait_ge(sm["st_done"], b * NS + n + 1)
                        if n >= 4:
                            act.wait_ge(sm["pv_done"], b * NS + n - 3)
                        act.activation(pt[:, n % 4, :], ring[:, n % 4, :], ACT.Exp,
                                       scale=float(HD0) ** -0.5).then_inc(sm["exp_done"], 1)
                        if n % 16 == 5 and n > 16:
                            copy_out(act, b, n // 16 - 1)
                    copy_out(act, b, 3)
                    act.wait_ge(sm["of_done"], b + 1)
                    act.activation(of[:, :], t2[:, :], ACT.Identity).then_inc(sm["of_ready"], 1)

            @block.vector
            def _(dve):
                dve.sem_inc(sm["onorm_step"], 1)
                dve.sem_inc(sm["x_ready"], 1)
                dve.wait_ge(sm["start"], 3)
                with dve.Fori(0, B) as b:
                    for i in range(2):
                        dve.wait_ge(sm["proj_done"], b * 4 + 2 * i + 1)
                        dve.scalar_tensor_tensor(out=ta[:, i, :], in0=ring[:, 2 * i, :], scalar=S.bq[:, i:i + 1],
                                                 in1=S.cos0[:, :], op0=ALU.add, op1=ALU.mult).then_inc(sm["rope_step"], 1)
                        dve.wait_ge(sm["proj_done"], b * 4 + 2 * i + 2)
                        dve.scalar_tensor_tensor(out=tb[:, i, :], in0=ring[:, 2 * i + 1, :], scalar=S.bq[:, 2 + i:3 + i],
                                                 in1=S.sin0[:, :], op0=ALU.add, op1=ALU.mult).then_inc(sm["rope_step"], 1)
                        dve.wait_ge(sm["rope_step"], b * 4 + 2 * i + 2)
                        dve.tensor_tensor(qk[:, i, :], ta[:, i, :], tb[:, i, :], ALU.add).then_inc(sm["q_ready"], 1)
                    dve.wait_ge(sm["v_done"], b + 2)
                    dve.tensor_tensor(vv[:, :, :, 0:HD0], t1[:, :].rearrange("p (c h d) -> p c h d", c=TT, h=H0),
                                      S.bv0[:, :].rearrange("p (h d) -> p h d", h=H0).unsqueeze(1).broadcast_to([P, TT, H0, HD0]),
                                      ALU.add).then_inc(sm["v_ready"], 1)
                    dve.wait_ge(sm["q_ready"], b * 2 + 2)
                    for h in range(H0):
                        dve.tensor_scalar(km[:, h, :], qk[:, 1, :], S.headmask0[:, h:h + 1], None,
                                          ALU.mult).then_inc(sm["kmask_ready"], 1)
                        if h:
                            maxima(dve, b, h - 1)
                    maxima(dve, b, H0 - 1)
                    dve.wait_ge(sm["maxt_done"], b + 1)
                    k = b * 6
                    dve.tensor_copy(mb[0:H0, :], t2[0:H0, :]).then_inc(sm["part_step"], 1)
                    dve.wait_ge(sm["part_step"], k + 1)
                    dve.tensor_tensor(rem[:, 0, :], t2[0:H0, :], mb[0:H0, :], ALU.subtract).then_inc(sm["part_step"], 1)
                    dve.wait_ge(sm["part_step"], k + 2)
                    dve.tensor_copy(mid[:, :], rem[:, 0, :]).then_inc(sm["part_step"], 1)
                    dve.wait_ge(sm["part_step"], k + 3)
                    dve.tensor_copy(mb[32:32 + H0, :], mid[:, :]).then_inc(sm["part_step"], 1)
                    dve.tensor_tensor(rem[:, 1, :], rem[:, 0, :], mid[:, :], ALU.subtract).then_inc(sm["part_step"], 1)
                    dve.wait_ge(sm["part_step"], k + 5)
                    dve.tensor_copy(mb[64:64 + H0, :], rem[:, 1, :]).then_inc(sm["part_step"], 1)
                    for g in range(4):
                        dve.wait_ge(sm["ot_done"], b * 4 + g + 1)
                        t = t1[:, :].rearrange("p (c j m) -> p c j m", c=TT, j=GH)
                        dve.reciprocal(rc[:, :, :], t[:, :, :, HD0]).then_inc(sm["onorm_step"], 1)
                        dve.wait_ge(sm["onorm_step"], b * 8 + 2 * g + 2)
                        o = on[:, :, GH * HD0 * g:GH * HD0 * (g + 1)].rearrange("p c (j d) -> p c j d", j=GH)
                        dve.tensor_tensor(o, t[:, :, :, 0:HD0], rc[:, :, :].unsqueeze(3).broadcast_to([P, TT, GH, HD0]),
                                          ALU.mult).then_inc(sm["onorm_step"], 1)
                    dve.wait_ge(sm["y_done"], b + 1)
                    dve.tensor_scalar(tx[:, :], t2[:, :], S.bo0[:, 0:1], S.mod[:, 0, 2, bass.ds(b, 1)], ALU.add,
                                      ALU.mult).then_inc(sm["gated"], 1)
                    dve.wait_ge(sm["gated"], b + 1)
                    dve.tensor_tensor(S.xr[:, b, :], S.xr[:, b, :], tx[:, :], ALU.add).then_inc(sm["x_ready"], 1)


def mix_stage(core, A):
    nc, S = core.nc, core
    loaded, mixed, step, done = core.sem("mix_loaded"), core.sem("mix_done"), core.sem("mix_step"), core.sem("mix_added")
    with ExitStack() as ctx:
        w = core.sb(ctx, "mix_w", [P, P])
        bias = core.sb(ctx, "mix_b", [P, 1])
        tmp = core.sb(ctx, "mix_tmp", [P, 4, T])
        pm = core.ps(ctx, "mix_ps", [P, 4, BANK])
        with nc.Block() as block:
            @block.sync
            def _(sp):
                sp.dma_start(w[:, :], A["L0_ffn_mix_w"]).then_inc(loaded, 16)
                sp.dma_start(bias[:, :], column(A["L0_ffn_mix_b"])).then_inc(loaded, 16)

            @block.tensor
            def _(pe):
                pe.wait_ge(loaded, 32)
                for b in range(B):
                    if b >= 4:
                        pe.wait_ge(step, b - 3)
                    pe.matmul(pm[:, b % 4, :], w[:, :], S.xa[:, b, PADW:], start=True, stop=True).then_inc(mixed, 1)

            @block.vector
            def _(dve):
                dve.wait_ge(loaded, 32)
                for b in range(B):
                    dve.wait_ge(mixed, b + 1)
                    dve.scalar_tensor_tensor(out=tmp[:, b % 4, :], in0=pm[:, b % 4, :], scalar=bias[:, 0:1],
                                             in1=S.xa[:, b, PADW:], op0=ALU.add, op1=ALU.add).then_inc(step, 1)
                    dve.wait_ge(step, b + 1)
                    dve.tensor_tensor(S.h[:, b, :], S.h[:, b, :], tmp[:, b % 4, :], ALU.add).then_inc(done, 1)


def router_stage(core, A, comb, b1t, b2t):
    nc, S = core.nc, core
    loaded = core.sem("rt_loaded")
    logits, biases, step = core.sem("rt_logits"), core.sem("rt_biases"), core.sem("rt_step")
    exp_done, turned, taken = core.sem("rt_exp"), core.sem("rt_turned"), core.sem("rt_taken")
    zeroed = core.sem("rt_zeroed")
    N = B * TT
    with ExitStack() as ctx:
        w = core.sb(ctx, "rt_w", [P, E0])
        b1 = core.sb(ctx, "rt_b1", [4 * E0, P])
        b2 = core.sb(ctx, "rt_b2", [E0, P])
        low = core.sb(ctx, "rt_lower", [P, E0 * E0])
        pr = core.sb(ctx, "rt_probs", [P, N, E0])
        mx, sm = core.sb(ctx, "rt_max", [P, N]), core.sb(ctx, "rt_sum", [P, N])
        gt, eq = core.sb(ctx, "rt_gt", [P, N, E0 * E0]), core.sb(ctx, "rt_eq", [P, N, E0 * E0])
        rank = core.sb(ctx, "rt_rank", [P, N, E0])
        part = core.sb(ctx, "rt_part", [P, 2, N, E0], BF16)
        parts = core.sb(ctx, "rt_parts", [P, N, 96])
        pl = core.ps(ctx, "rt_pl", [P, BANK])
        pb = core.ps(ctx, "rt_pb", [P, BANK])
        pt = core.ps(ctx, "rt_pt", [P, 4, BANK])
        with nc.Block() as block:
            @block.sync
            def _(sp):
                sp.dma_start(w[:, :], A["L0_ffn_router_w"]).then_inc(loaded, 16)
                sp.dma_start(b1[:, :], A["L0_ffn_b1"].rearrange("e (c p) -> (e c) p", p=P)).then_inc(loaded, 16)
                sp.dma_start(b2[:, :], A["L0_ffn_b2"]).then_inc(loaded, 16)
                sp.dma_start(low[:, :], A["lower"]).then_inc(loaded, 16)

            @block.tensor
            def _(pe):
                pe.wait_ge(loaded, 64)
                for n in range(N):
                    b, c = n // TT, n % TT
                    mm = pe.matmul(pl[:, E0 * n:E0 * n + E0], S.xa[:, b, PADW + P * c:PADW + P * c + P], w[:, :],
                                   start=True, stop=True)
                mm.then_inc(logits, 1)
                pe.transpose(pb[:, 0:32], b1[:, :], S.ident[0:32, 0:32])
                pe.transpose(pb[:, 32:40], b2[:, :], S.ident[0:8, 0:8]).then_inc(biases, 1)
                pe.wait_ge(step, 19)
                for b in range(B):
                    if b >= 4:
                        pe.wait_ge(taken, b - 3)
                    for c in range(TT):
                        tr = pe.transpose(pt[0:96, b % 4, P * c:P * c + P], parts[:, TT * b + c, :], S.ident[:, :])
                    tr.then_inc(turned, 1)

            @block.scalar
            def _(act):
                act.preload_act_table_set("natural_log_exp_and_others")
                act.wait_ge(step, 2)
                act.activation(pr[:, :, :], pr[:, :, :], ACT.Exp).then_inc(exp_done, 1)
                for b in range(B):
                    act.wait_ge(turned, b + 1)
                    act.activation(comb[:, b, :], pt[0:96, b % 4, :], ACT.Identity).then_inc(taken, 1)

            @block.gpsimd
            def _(pool):
                pool.memset(parts[:, :, :], 0.0).then_inc(zeroed, 1)

            @block.vector
            def _(dve):
                n = 0

                def ordered(ins):
                    nonlocal n
                    n += 1
                    ins.then_inc(step, 1)
                    dve.wait_ge(step, n)

                lg = pl[:, 0:N * E0].rearrange("p (n e) -> p n e", e=E0)

                def wide(ap):
                    return ap[:, :].unsqueeze(2).broadcast_to([P, N, E0])

                def pairs(ap):
                    return ap[:, :, :].rearrange("p n (e o) -> p n e o", e=E0)

                def by_expert():
                    return pr[:, :, :].unsqueeze(3).broadcast_to([P, N, E0, E0])

                def by_other():
                    return pr[:, :, :].unsqueeze(2).broadcast_to([P, N, E0, E0])

                dve.wait_ge(logits, 1)
                ordered(dve.tensor_reduce(mx[:, :], lg, AX_X, ALU.max))
                ordered(dve.tensor_tensor(pr[:, :, :], lg, wide(mx), ALU.subtract))
                dve.wait_ge(exp_done, 1)
                ordered(dve.tensor_reduce(sm[:, :], pr[:, :, :], AX_X, ALU.add))
                ordered(dve.reciprocal(sm[:, :], sm[:, :]))
                ordered(dve.tensor_tensor(pr[:, :, :], pr[:, :, :], wide(sm), ALU.mult))
                ordered(dve.tensor_tensor(pairs(gt), by_other(), by_expert(), ALU.is_gt))
                ordered(dve.tensor_tensor(pairs(eq), by_other(), by_expert(), ALU.is_equal))
                dve.wait_ge(loaded, 64)
                ordered(dve.tensor_tensor(eq[:, :, :], eq[:, :, :], low[:, :].unsqueeze(1).broadcast_to([P, N, E0 * E0]),
                                          ALU.mult))
                ordered(dve.tensor_tensor(gt[:, :, :], gt[:, :, :], eq[:, :, :], ALU.add))
                ordered(dve.tensor_reduce(rank[:, :, :], pairs(gt), AX_X, ALU.add))
                ordered(dve.tensor_scalar(rank[:, :, :], rank[:, :, :], 2.0, None, ALU.is_lt))
                ordered(dve.tensor_tensor(pr[:, :, :], pr[:, :, :], rank[:, :, :], ALU.mult))
                dve.wait_ge(zeroed, 1)
                ordered(dve.tensor_copy(part[:, 0, :, :], pr[:, :, :]))
                ordered(dve.tensor_copy(parts[:, :, 0:E0], part[:, 0, :, :]))
                ordered(dve.tensor_tensor(pr[:, :, :], pr[:, :, :], part[:, 0, :, :], ALU.subtract))
                ordered(dve.tensor_copy(part[:, 1, :, :], pr[:, :, :]))
                ordered(dve.tensor_copy(parts[:, :, 32:32 + E0], part[:, 1, :, :]))
                ordered(dve.tensor_tensor(pr[:, :, :], pr[:, :, :], part[:, 1, :, :], ALU.subtract))
                ordered(dve.tensor_copy(parts[:, :, 64:64 + E0], pr[:, :, :]))
                dve.wait_ge(biases, 1)
                dve.tensor_copy(b1t[:, :], pb[:, 0:32])
                dve.tensor_copy(b2t[:, :], pb[:, 32:40])


def experts_stage(core, comb, w1, w2, b1t, b2t):
    nc, S = core.nc, core
    FC = F0 // P
    NH = E0 * FC
    sm = {n: core.sem("ex_" + n) for n in "h_done h_ready y_done c_done c_ready y_ready acc_ready x_ready".split()}
    with ExitStack() as ctx:
        hs = core.sb(ctx, "ex_hs", [P, 2 * FC, T])
        cs = core.sb(ctx, "ex_cs", [P, 2, T])
        ys = core.sb(ctx, "ex_ys", [P, 2, T])
        acc = core.sb(ctx, "ex_acc", [P, T])
        ph = core.ps(ctx, "ex_ph", [P, 4, BANK])
        py = core.ps(ctx, "ex_py", [P, 2, BANK])
        pc = core.ps(ctx, "ex_pc", [P, 2, BANK])
        with nc.Block() as block:
            @block.tensor
            def _(pe):
                pe.wait_ge(S.experts_loaded, 32)
                with pe.Fori(0, B) as b:
                    def up(e):
                        for f in range(FC):
                            n = e * FC + f
                            pe.wait_ge(sm["h_ready"], b * NH + n + 1)
                            pe.matmul(ph[:, n % 4, :], w1[:, e, P * f:P * f + P], S.xa[:, b, PADW:], start=True,
                                      stop=True).then_inc(sm["h_done"], 1)
                        pe.wait_ge(sm["c_ready"], b * E0 + e + 1)
                        pe.matmul(pc[:, e % 2, :], S.pick[0:96, e, :], comb[:, b, :], start=True,
                                  stop=True).then_inc(sm["c_done"], 1)

                    def down(e):
                        pe.wait_ge(sm["y_ready"], b * E0 + e + 1)
                        for f in range(FC):
                            n = e * FC + f
                            pe.wait_ge(sm["h_ready"], b * NH + n + 5)
                            mm = pe.matmul(py[:, e % 2, :], w2[:, e, f, :], hs[:, n % (2 * FC), :], start=(f == 0),
                                           stop=(f == FC - 1))
                        mm.then_inc(sm["y_done"], 1)

                    for e in range(E0 + 1):
                        if e < E0:
                            up(e)
                        if e:
                            down(e - 1)

            @block.scalar
            def _(act):
                act.preload_act_table_set("silu_and_others")
                act.sem_inc(sm["h_ready"], 4)
                act.sem_inc(sm["c_ready"], 2)
                with act.Fori(0, B) as b:
                    for e in range(E0):
                        act.wait_ge(sm["y_done"], b * E0 + e + 1)
                        for f in range(FC):
                            n = e * FC + f
                            act.wait_ge(sm["h_done"], b * NH + n + 1)
                            act.activation(hs[:, n % (2 * FC), :], ph[:, n % 4, :], ACT.Silu,
                                           bias=b1t[:, n:n + 1]).then_inc(sm["h_ready"], 1)
                        act.wait_ge(sm["c_done"], b * E0 + e + 1)
                        act.wait_ge(sm["y_ready"], b * E0 + e + 1)
                        act.activation(cs[:, e % 2, :], pc[:, e % 2, :], ACT.Identity).then_inc(sm["c_ready"], 1)

            @block.vector
            def _(dve):
                dve.sem_inc(sm["y_ready"], 2)
                dve.sem_inc(sm["y_done"], 2)
                dve.sem_inc(sm["x_ready"], 1)
                with dve.Fori(0, B) as b:
                    for e in range(E0):
                        dve.wait_ge(sm["y_done"], b * E0 + e + 3)
                        dve.wait_ge(sm["c_ready"], b * E0 + e + 3)
                        dve.wait_ge(sm["acc_ready"], b * E0 + e + 1)
                        dve.scalar_tensor_tensor(out=ys[:, e % 2, :], in0=py[:, e % 2, :], scalar=b2t[:, e:e + 1],
                                                 in1=cs[:, e % 2, :], op0=ALU.add, op1=ALU.mult).then_inc(sm["y_ready"], 1)
                    dve.wait_ge(sm["acc_ready"], b * E0 + E0 + 2)
                    dve.scalar_tensor_tensor(out=S.xr[:, b, :], in0=acc[:, :], scalar=S.mod[:, 0, 5, bass.ds(b, 1)],
                                             in1=S.xr[:, b, :], op0=ALU.mult, op1=ALU.add).then_inc(sm["x_ready"], 1)

            @block.gpsimd
            def _(pool):
                pool.sem_inc(sm["acc_ready"], 2)
                with pool.Fori(0, B) as b:
                    pool.wait_ge(sm["x_ready"], b + 1)
                    for e in range(E0):
                        pool.wait_ge(sm["y_ready"], b * E0 + e + 3)
                        if e:
                            pool.wait_ge(sm["acc_ready"], b * E0 + e + 2)
                        pool.tensor_tensor(acc[:, :], acc[:, :] if e else S.h[:, b, :], ys[:, e % 2, :],
                                           ALU.add).then_inc(sm["acc_ready"], 1)


def ffn0(core, A, C):
    nc, S = core.nc, core
    with ExitStack() as ctx:
        w1 = core.sb(ctx, "moe_w1", [P, E0, F0])
        w2 = core.sb(ctx, "moe_w2", [P, E0, F0 // P, P])
        comb = core.sb(ctx, "moe_comb", [96, B, T], BF16)
        b1t, b2t = core.sb(ctx, "moe_b1", [P, 32]), core.sb(ctx, "moe_b2", [P, 8])
        gb = core.sb(ctx, "moe_norms", [P, 4])
        S.experts_loaded, gains = core.sem("experts_loaded"), core.sem("gains_loaded")
        with nc.Block() as block:
            @block.sync
            def _(sp):
                for i, n in enumerate(("g1", "be1", "g2", "be2")):
                    sp.dma_start(gb[:, i:i + 1], column(A["L0_ffn_" + n])).then_inc(gains, 16)
                sp.dma_start(w1[:, :, :], A["L0_ffn_w1"].rearrange("e d f -> d e f")).then_inc(S.experts_loaded, 16)
                sp.dma_start(w2[:, :, :, :], A["L0_ffn_w2"].rearrange("e (c p) d -> p e c d", p=P)).then_inc(S.experts_loaded, 16)
                sp.wait_ge(gains, 64)
        norm_stage(core, lambda b: S.xr[:, b, :], lambda b: S.h[:, b, :],
                   lambda b: S.mod[:, 0, 4, b:b + 1], lambda b: S.mod[:, 0, 3, b:b + 1])(B)
        norm_stage(core, lambda b: S.h[:, b, :], lambda b: S.xa[:, b, PADW:], lambda b: gb[:, 0:1], lambda b: gb[:, 1:2])(2 * B)
        mix_stage(core, A)
        norm_stage(core, lambda b: S.h[:, b, :], lambda b: S.xa[:, b, PADW:], lambda b: gb[:, 2:3], lambda b: gb[:, 3:4])(3 * B)
        router_stage(core, {**A, "lower": C["lower"]}, comb, b1t, b2t)
        experts_stage(core, comb, w1, w2, b1t, b2t)


def attention1(core, A, C):
    nc, S = core.nc, core
    sm = {n: core.sem("a1_" + n) for n in ("loaded loaded_cast trig_step trig_ready sin_done hs_ready proj_done act_ready dve_ready s_done v_done "
                                           "max_ready sub_ready exp_done sum_ready rsum_ready norm_ready t_done t_ready "
                                           "v_ready o_done o_ready y_done gated x_ready start setup").split()}
    NB = T // TB
    NG = NB // 4
    SCALE = float(HD1) ** -0.5
    TWO_PI = 2 * np.pi
    TP_HI = float(np.float32(6.28125))
    TP_LO = float(TWO_PI - 6.28125)
    MAGIC = 1.5 * 2.0 ** 23
    with ExitStack() as ctx:
        wq, wk, wv = (core.sb(ctx, "a1_w" + n, [P, H1 * HD1]) for n in "qkv")
        wo = core.sb(ctx, "a1_wo", [P, H1, P])
        bqk = core.sb(ctx, "a1_bqk", [P, 2, H1])
        bo = core.sb(ctx, "a1_bo", [P, 1])
        bv = core.sb(ctx, "a1_bv", [P, HD1])
        mask = core.sb(ctx, "a1_mask", [P, P], BF16)
        mask4 = core.sb(ctx, "a1_mask4", [P, 4, P], BF16)
        ph = core.sb(ctx, "a1_phase", [P, H1])
        rnd = core.sb(ctx, "a1_round", [P, 2, H1])
        red = core.sb(ctx, "a1_reduced", [P, 2, H1])
        trig = core.sb(ctx, "a1_trig", [P, 2, H1])
        tbias = core.sb(ctx, "a1_tbias", [P, 2, H1])
        hs = core.sb(ctx, "a1_hs", [P, T])
        qp = core.sb(ctx, "a1_q", [P, 2, NB, H1, TB])
        kp = core.sb(ctx, "a1_k", [P, 2, NB, H1, TB])
        vs = core.sb(ctx, "a1_v", [P, 2, 4, HD1])
        pr = core.sb(ctx, "a1_p", [P, 2, 4, P])
        pn = core.sb(ctx, "a1_pn", [P, 2, 4, P])
        at = core.sb(ctx, "a1_pt", [P, 2, 4, P])
        mx, su, rs = (core.sb(ctx, "a1_" + n, [P, 2, 4]) for n in ("max", "sum", "rsum"))
        ot = core.sb(ctx, "a1_o", [P, H1, T])
        tx = core.sb(ctx, "a1_tx", [P, T])
        ring = core.ps(ctx, "a1_ring", [P, 4, BANK])
        ps = core.ps(ctx, "a1_s", [P, 2, BANK])
        po = core.ps(ctx, "a1_po", [P, BANK])
        py = core.ps(ctx, "a1_py", [P, BANK])
        with nc.Block() as block:
            @block.sync
            def _(sp):
                for n, ap in (("L1_attn_Wq", wq), ("L1_attn_Wk", wk), ("L1_attn_Wv", wv)):
                    sp.dma_start(ap[:, :], A[n]).then_inc(sm["loaded"], 16)
                sp.dma_start(wo[:, :, :], A["L1_attn_Wo"].rearrange("(h d) o -> d h o", d=HD1)).then_inc(sm["loaded"], 16)
                with nc.allow_non_contiguous_dma("small vectors turned onto the partitions"):
                    sp.dma_start(bqk[:, 0, :], A["L1_attn_bq"].rearrange("(h d) -> d h", d=HD1)).then_inc(sm["loaded"], 16)
                    sp.dma_start(bqk[:, 1, :], A["L1_attn_bk"].rearrange("(h d) -> d h", d=HD1)).then_inc(sm["loaded"], 16)
                    sp.dma_start(ph[:, :], A["L1_attn_phase"].rearrange("h d -> d h")).then_inc(sm["loaded"], 16)
                sp.dma_start(bo[:, :], column(A["L1_attn_bo"])).then_inc(sm["loaded"], 16)
                for g in range(H1):
                    sp.dma_start(bv[TB * g:TB * g + TB, :],
                                 A["L1_attn_bv"][HD1 * g:HD1 * g + HD1].partition_broadcast(TB)).then_inc(sm["loaded"], 16)

            NLOAD = 16 * 12

            @block.gpsimd
            def _(pool):
                pool.dma_start(mask[:, :], C["mask1"]).then_inc(sm["loaded_cast"], 16)
                pool.wait_ge(sm["loaded_cast"], 16)
                with pool.Fori(0, B) as b:
                    pool.wait_ge(sm["v_done"], b * NG + 1)
                    pool.tensor_copy(hs[:, :], S.h[:, b, :]).then_inc(sm["hs_ready"], 1)
                    for g in range(NG):
                        pool.wait_ge(sm["rsum_ready"], b * NG + g + 1)
                        pool.wait_ge(sm["t_done"], b * NG + g + 1)
                        pool.tensor_tensor(pn[:, g % 2, :, :], pr[:, g % 2, :, :],
                                           rs[:, g % 2, :].unsqueeze(2).broadcast_to([P, 4, P]),
                                           ALU.mult).then_inc(sm["norm_ready"], 1)

            @block.tensor
            def _(pe):
                pe.wait_ge(sm["loaded"], NLOAD)
                pe.wait_ge(sm["setup"], 1)
                pe.sem_inc(sm["v_done"], 1)
                pe.sem_inc(sm["t_done"], 2)
                with pe.Fori(0, B) as b:
                    pe.wait_ge(sm["hs_ready"], b + 1)
                    for n in range(2 * H1):
                        h, k = n // 2, n % 2
                        w = wk if k else wq
                        if h >= 2:
                            pe.wait_ge(sm["dve_ready" if k else "act_ready"], b * 2 * H1 + 2 * (h - 1))
                        elif k:
                            pe.wait_ge(sm["t_ready"], b * NG + 1)
                        else:
                            pe.wait_ge(sm["v_ready"], b * NG + 1)
                        pe.matmul(ring[:, 2 * k + h % 2, :], w[:, HD1 * h:HD1 * h + HD1], hs[:, :], start=True,
                                  stop=True).then_inc(sm["proj_done"], 1)

                    def scores(g):
                        pe.wait_ge(sm["sub_ready"], b * NG + g + 1)
                        if g == 0:
                            pe.wait_ge(sm["act_ready"], b * 2 * H1 + 2 * H1)
                            pe.wait_ge(sm["dve_ready"], b * 2 * H1 + 2 * H1)
                        pe.matmul(ps[:, g % 2, :], S.identb[:, :], mask4[:, :, :].rearrange("p n m -> p (n m)"), start=True,
                                  stop=False, skip_group_check=True)
                        for i in range(4):
                            for part in range(2):
                                mm = pe.matmul(ps[:, g % 2, P * i:P * i + P],
                                               qp[:, part, 4 * g + i, :, :].rearrange("p h t -> p (h t)"),
                                               kp[:, part, 4 * g + i, :, :].rearrange("p h t -> p (h t)"),
                                               start=False, stop=(part == 1), skip_group_check=True)
                        mm.then_inc(sm["s_done"], 1)
                        if g >= 2:
                            pe.wait_ge(sm["v_ready"], b * NG + g)
                        for h in range(H1):
                            for i in range(4):
                                at_ = TB * (4 * g + i)
                                mm = pe.matmul(ring[TB * h:TB * h + TB, g % 2, P * i:P * i + P], hs[:, at_:at_ + TB],
                                               wv[:, HD1 * h:HD1 * h + HD1], start=True, stop=True)
                        mm.then_inc(sm["v_done"], 1)

                    def turn(g):
                        pe.wait_ge(sm["norm_ready"], b * NG + g + 3)
                        if g >= 2:
                            pe.wait_ge(sm["t_ready"], b * NG + g)
                        for i in range(4):
                            tr = pe.transpose(ring[:, 2 + g % 2, P * i:P * i + P], pn[:, g % 2, i, :], S.ident[:, :])
                        tr.then_inc(sm["t_done"], 1)

                    def weighted(g):
                        pe.wait_ge(sm["t_ready"], b * NG + g + 2)
                        pe.wait_ge(sm["v_ready"], b * NG + g + 2)
                        pe.wait_ge(sm["o_ready"], b * NG + g + 1)
                        for i in range(4):
                            mm = pe.matmul(po[:, P * i:P * i + P], vs[:, g % 2, i, :], at[:, g % 2, i, :], start=True, stop=True)
                        mm.then_inc(sm["o_done"], 1)

                    for s in range(NG + 2):
                        if s < NG:
                            scores(s)
                        if 1 <= s <= NG:
                            turn(s - 1)
                        if s >= 2:
                            weighted(s - 2)
                    pe.wait_ge(sm["o_ready"], b * NG + NG + 1)
                    pe.wait_ge(sm["x_ready"], b + 1)
                    for j in range(H1):
                        mm = pe.matmul(py[:, :], wo[:, j, :], ot[:, :, :].rearrange("p h (r j) -> p h r j", j=H1)[:, :, :, j],
                                       start=(j == 0), stop=(j == H1 - 1))
                    mm.then_inc(sm["y_done"], 1)

            @block.scalar
            def _(act):
                act.sem_inc(sm["t_ready"], 1)
                act.wait_ge(sm["trig_ready"], 1)
                act.activation(trig[:, :, :], red[:, :, :], ACT.Sin).then_inc(sm["sin_done"], 1)
                act.wait_ge(sm["setup"], 1)
                act.preload_act_table_set("natural_log_exp_and_others")
                with act.Fori(0, B) as b:
                    for h in range(H1):
                        act.wait_ge(sm["proj_done"], b * 2 * H1 + 2 * h + 1)
                        if h == 0:
                            act.wait_ge(sm["s_done"], b * NG + 1)
                        for part in range(2):
                            act.activation(qp[:, part, :, h, :], ring[:, h % 2, :].rearrange("p (n t) -> p n t", t=TB),
                                           ACT.Identity, bias=tbias[:, part, h:h + 1],
                                           scale=trig[:, part, h:h + 1]).then_inc(sm["act_ready"], 1)
                    for s in range(NG + 1):
                        if s < NG:
                            act.wait_ge(sm["sub_ready"], b * NG + s + 3)
                            act.activation(pr[:, s % 2, :, :], pr[:, s % 2, :, :], ACT.Exp, scale=SCALE).then_inc(sm["exp_done"], 1)
                        if s:
                            g = s - 1
                            act.wait_ge(sm["t_done"], b * NG + g + 3)
                            act.wait_ge(sm["o_done"], b * NG + g + 1)
                            act.activation(at[:, g % 2, :, :].rearrange("p n m -> p (n m)"), ring[:, 2 + g % 2, :],
                                           ACT.Identity).then_inc(sm["t_ready"], 1)

            @block.vector
            def _(dve):
                dve.sem_inc(sm["v_ready"], 1)
                dve.sem_inc(sm["sub_ready"], 2)
                dve.sem_inc(sm["o_ready"], 1)
                dve.sem_inc(sm["x_ready"], 1)
                dve.sem_inc(sm["s_done"], 1)
                dve.sem_inc(sm["o_done"], 2)
                dve.sem_inc(sm["norm_ready"], 2)
                dve.sem_inc(sm["y_done"], 1)
                dve.wait_ge(sm["loaded"], NLOAD)
                n = 0

                def ordered(ins):
                    nonlocal n
                    n += 1
                    ins.then_inc(sm["trig_step"], 1)
                    dve.wait_ge(sm["trig_step"], n)

                for part in range(2):
                    ordered(dve.tensor_scalar(rnd[:, part, :], ph[:, :], 1.0 / TWO_PI, 0.25 if part == 0 else 0.0,
                                              ALU.mult, ALU.add))
                    ordered(dve.tensor_scalar(rnd[:, part, :], rnd[:, part, :], MAGIC, None, ALU.add))
                    ordered(dve.tensor_scalar(rnd[:, part, :], rnd[:, part, :], MAGIC, None, ALU.subtract))
                    ordered(dve.scalar_tensor_tensor(out=red[:, part, :], in0=rnd[:, part, :], scalar=-TP_HI, in1=ph[:, :],
                                                     op0=ALU.mult, op1=ALU.add))
                    ordered(dve.scalar_tensor_tensor(out=red[:, part, :], in0=rnd[:, part, :], scalar=-TP_LO,
                                                     in1=red[:, part, :], op0=ALU.mult, op1=ALU.add))
                    if part == 0:
                        ordered(dve.tensor_scalar(red[:, part, :], red[:, part, :], float(np.pi / 2), None, ALU.add))
                    ordered(dve.tensor_scalar(red[:, part, :], red[:, part, :], 3.1415925, -3.1415925, ALU.min, ALU.max))
                dve.sem_inc(sm["trig_ready"], 1)
                dve.wait_ge(sm["sin_done"], 1)
                for part in range(2):
                    ordered(dve.tensor_tensor(tbias[:, part, :], trig[:, part, :], bqk[:, 0, :], ALU.mult))
                dve.wait_ge(sm["loaded_cast"], 16)
                dve.tensor_copy(mask4[:, :, :], mask[:, :].unsqueeze(1).broadcast_to([P, 4, P])).then_inc(sm["setup"], 1)
                with dve.Fori(0, B) as b:
                    for h in range(H1):
                        dve.wait_ge(sm["proj_done"], b * 2 * H1 + 2 * h + 2)
                        for part in range(2):
                            dve.tensor_scalar(kp[:, part, :, h, :], ring[:, 2 + h % 2, :].rearrange("p (n t) -> p n t", t=TB),
                                              bqk[:, 1, h:h + 1], trig[:, part, h:h + 1], ALU.add,
                                              ALU.mult).then_inc(sm["dve_ready"], 1)
                    for s in range(NG + 2):
                        if s < NG:
                            g, i = s, s % 2
                            dve.wait_ge(sm["s_done"], b * NG + g + 2)
                            S4 = ps[:, i, :].rearrange("p (n m) -> p n m", m=P)
                            dve.tensor_reduce(mx[:, i, :], S4, AX_X, ALU.max).then_inc(sm["max_ready"], 1)
                            dve.wait_ge(sm["max_ready"], b * NG + g + 1)
                            dve.wait_ge(sm["norm_ready"], b * NG + g + 1)
                            dve.tensor_tensor(pr[:, i, :, :], S4, mx[:, i, :].unsqueeze(2).broadcast_to([P, 4, P]),
                                              ALU.subtract).then_inc(sm["sub_ready"], 1)
                            dve.wait_ge(sm["v_done"], b * NG + g + 2)
                            if g >= 2:
                                dve.wait_ge(sm["o_done"], b * NG + g + 1)
                            dve.tensor_tensor(vs[:, i, :, :], ring[:, i, :].rearrange("p (n m) -> p n m", m=HD1),
                                              bv[:, :].unsqueeze(1).broadcast_to([P, 4, HD1]), ALU.add).then_inc(sm["v_ready"], 1)
                            dve.wait_ge(sm["exp_done"], b * NG + g + 1)
                            dve.tensor_reduce(su[:, i, :], pr[:, i, :, :], AX_X, ALU.add).then_inc(sm["sum_ready"], 1)
                            dve.wait_ge(sm["sum_ready"], b * NG + g + 1)
                            dve.reciprocal(rs[:, i, :], su[:, i, :]).then_inc(sm["rsum_ready"], 1)
                        if s >= 2:
                            g = s - 2
                            dve.wait_ge(sm["o_done"], b * NG + g + 3)
                            if g == 0:
                                dve.wait_ge(sm["y_done"], b + 1)
                            dve.tensor_copy(ot[:, :, P * g:P * g + P].rearrange("p h (n t) -> p n h t", t=TB),
                                            po[:, :].rearrange("p (n h t) -> p n h t", n=4, h=H1)).then_inc(sm["o_ready"], 1)
                    dve.wait_ge(sm["y_done"], b + 2)
                    dve.tensor_scalar(tx[:, :], py[:, :], bo[:, 0:1], S.mod[:, 1, 2, bass.ds(b, 1)], ALU.add,
                                      ALU.mult).then_inc(sm["gated"], 1)
                    dve.wait_ge(sm["gated"], b + 1)
                    dve.tensor_tensor(S.xr[:, b, :], S.xr[:, b, :], tx[:, :], ALU.add).then_inc(sm["x_ready"], 1)


NPAIR = H2 // 2
NT = B * TT
NW = P // WIN


class LocalAttention:

    NAMES = ("proj_done sq_ready ss_ready ssmax_ready ln_step rn_ready cos_ready sin_ready add_ready qkn_ready "
             "turn_done q_taken k_taken s_done max_ready sub_ready exp_ready sum_ready rsum_ready pn_ready "
             "v_done v_taken pt_done pt_taken o_done o_taken y_done x_ready table_step table_ready").split()

    def __init__(self, core, ctx):
        self.core = core
        self.sm = {n: core.sem("la_" + n) for n in self.NAMES}
        self.xs_ready = [core.sem("la_xs%d_ready" % i) for i in range(TT)]
        sb = lambda name, shape, dt=F32: core.sb(ctx, "la_" + name, shape, dt)
        self.wqkv = sb("wqkv", [P, 3 * INNER])
        self.wo = sb("wo", [P, NPAIR, P])
        self.qks = sb("qks", [P, 2, HD2])
        self.rope = sb("rope", [P, 2, TT, 2, HD2])
        self.cs = sb("cs", [P, 2, TT, 2, HD2])
        self.maskf = sb("maskf", [P, 2, 2 * WIN], BF16)
        self.mask = sb("mask", [P, 2, NPAIR, 2 * WIN], BF16)
        self.xs = sb("xs", [P, 4, P + WIN])
        self.work = sb("work", [P, 3, 2, INNER])
        self.sq, self.t1, self.t2 = (self.work[:, i, :, :] for i in range(3))
        self.ss = sb("ss", [P, 2, H2])
        self.rn = sb("rn", [P, 2, H2])
        self.qkn = sb("qkn", [P, 2, INNER])
        self.kt = sb("kt", [P, 2, NPAIR, P + WIN])
        self.qb = sb("qb", [P, NPAIR, NW, 2 * WIN])
        self.pr = sb("pr", [P, 2, NPAIR, 2 * WIN])
        self.pn = sb("pn", [P, 2, NPAIR, 2 * WIN])
        self.mx, self.su, self.rs = (sb(n, [P, 2, NPAIR]) for n in ("max", "sum", "rsum"))
        self.pb = sb("pb", [P, 2, NPAIR // 2, 4, 2, WIN])
        self.vs = sb("vs", [P, NW, NPAIR // 2, P])
        self.os = sb("os", [P, NPAIR, P])

    def setup(self, A, C):
        nc, S, sm = self.core.nc, self.core, self.sm
        loaded, cast, ready = S.sem("la_tables"), S.sem("la_masks"), S.sem("la_zeroed")
        with nc.Block() as block:
            @block.sync
            def _(sp):
                for i, n in enumerate(("cos2", "sin2")):
                    sp.dma_start(self.rope[:, i, :, :, :].rearrange("p t k d -> p (t k d)"), C[n]).then_inc(loaded, 16)
                sp.wait_ge(loaded, 32)

            @block.gpsimd
            def _(pool):
                pool.dma_start(self.maskf[:, :, :].rearrange("p n m -> p (n m)"), C["mask2"]).then_inc(cast, 16)
                pool.memset(self.qb[:, :, :, :].rearrange("p a b c -> p (a b c)"), 0.0)
                pool.memset(self.pb[:, :, :, :, :, :].rearrange("p a b c d e -> p (a b c d e)"), 0.0)
                pool.memset(self.kt[:, 0, :, 0:WIN], 0.0)
                pool.wait_ge(cast, 16)

            @block.vector
            def _(dve):
                dve.wait_ge(cast, 16)
                dve.tensor_copy(self.mask[:, :, :, :], self.maskf[:, :, :].unsqueeze(2).broadcast_to([P, 2, NPAIR, 2 * WIN])).then_inc(ready, 1)
                for n in ("qkn_ready", "cos_ready", "o_taken", "add_ready"):
                    dve.sem_inc(sm[n], 2)
                for n in ("proj_done", "s_done", "pt_done", "o_done", "y_done", "pt_taken", "x_ready", "sin_ready", "ssmax_ready",
                          "rn_ready", "pn_ready", "v_taken", "turn_done"):
                    dve.sem_inc(sm[n], 4)

    def layer(self, layer, weights_count, src, dst, A):
        nc, S, sm = self.core.nc, self.core, self.sm
        me = self

        def G(n):
            return layer * NT + n

        def steps(eng, before, step, after):
            before()
            with eng.Fori(0, B - 1) as b:
                for i in range(TT):
                    step(b * TT + i, b, i, True, True, True)
            for i in range(TT):
                step((B - 1) * TT + i, B - 1, i, i < TT - 3, i < TT - 2, i < TT - 1)
            after()

        with ExitStack() as ctx:
            pa = S.ps(ctx, "la_pa", [P, 4, BANK])
            ring = S.ps(ctx, "la_ring", [P, 4, BANK])
            with nc.Block() as block:
                @block.tensor
                def _(pe):
                    def project(n, b, i):
                        pe.wait_ge(me.xs_ready[i], 32 * (layer * B + b) + 32)
                        pe.wait_ge(sm["sin_ready"], 2 * G(n) + 4)
                        for k in range(4):
                            mm = pe.matmul(pa[:, k, :], me.xs[:, i, WIN:], me.wqkv[:, BANK * k:BANK * k + BANK], start=True, stop=True)
                            if k % 2:
                                mm.then_inc(sm["proj_done"], 1)

                    def score(n, i, steady):
                        s = i % 2
                        for u in range(4):
                            if u % 2 == 0:
                                pe.wait_ge(sm["qkn_ready"], 2 * G(n) + u // 2 + 1 + 2)
                            if steady:
                                if u < 2:
                                    pe.wait_ge(sm["sub_ready"], 2 * G(n - 1) + u + 1)
                                    pe.wait_ge(sm["o_taken"], 2 * (G(n) - 2) + u + 1 + 2)
                                elif u == 2:
                                    pe.wait_ge(sm["x_ready"], G(n) - 2 + 1 + 4)
                                else:
                                    pe.wait_ge(sm["pt_taken"], 4 * (G(n) - 2) + 4 + 4)
                            for j in range(4):
                                at = (u % 2) * BANK + P * j
                                tr = pe.transpose(ring[:, u, P * j:P * j + P], me.qkn[:, u // 2, at:at + P], S.ident[:, :])
                            tr.then_inc(sm["turn_done"], 1)
                        for u in range(2):
                            pe.wait_ge(sm["q_taken"], 4 * G(n) + 4)
                            pe.wait_ge(sm["k_taken"], 2 * G(n) + 2)
                            first = 1 if (i == 0 and u == 0) else 0
                            pe.matmul(ring[:, u, :], S.identb[:, :], me.mask[:, first, :, :].rearrange("p n m -> p (n m)"),
                                      start=True, stop=False, skip_group_check=True)
                            for w in (2 * u, 2 * u + 1):
                                r = 64 * (w % 2)
                                for p in range(NPAIR):
                                    mm = pe.matmul(ring[r:r + 64, u, 64 * p:64 * p + 64], me.qb[:, p, w, :],
                                                   me.kt[:, s, p, WIN * w:WIN * w + 64], start=False, stop=True,
                                                   skip_group_check=True)
                            mm.then_inc(sm["s_done"], 1)

                    def weigh(n, i, follows):
                        wv = me.wqkv[:, 2 * INNER:3 * INNER].rearrange("p (j r m) -> p j r m", r=2, m=P)
                        for w in range(NW):
                            if w < 2:
                                if follows:
                                    pe.wait_ge(sm["k_taken"], 2 * G(n + 1) + 1 + w)
                                else:
                                    pe.wait_ge(sm["x_ready"] if w == 0 else sm["pt_taken"],
                                               G(n - 1) + 1 + 4 if w == 0 else 4 * G(n - 1) + 4 + 4)
                            else:
                                pe.wait_ge(sm["v_taken"], 4 * G(n) + w - 1 + 4)
                            for r in range(2):
                                mm = pe.matmul(ring[64 * r:64 * r + 64, 2 + w % 2, :], me.xs[:, i, WIN * w:WIN * w + 64],
                                               wv[:, :, r, :], start=True, stop=True)
                            mm.then_inc(sm["v_done"], 1)
                        for u in range(2):
                            pe.wait_ge(sm["v_taken"], 4 * G(n) + 3 + u + 4)
                            pe.wait_ge(sm["pn_ready"], 2 * G(n) + u + 1 + 4)
                            for j in range(NPAIR // 2):
                                tr = pe.transpose(ring[:, 2 + u, P * j:P * j + P],
                                                  me.pn[:, u, 2 * j:2 * j + 2, :].rearrange("p a k -> p (a k)"), S.ident[:, :])
                            tr.then_inc(sm["pt_done"], 1)
                        pe.wait_ge(sm["pt_taken"], 4 * G(n) + 4 + 4)
                        for half in range(2):
                            if follows:
                                pe.wait_ge(sm["sub_ready"], 2 * G(n + 1) + half + 1)
                            for h in range(2):
                                for j in (2 * half, 2 * half + 1):
                                    for w in range(NW):
                                        o = ring[64 * h:64 * h + 64, half, :].rearrange("p (a r t) -> p a r t", a=2, r=2)
                                        mm = pe.matmul(o[:, j % 2, :, WIN * w:WIN * w + WIN], me.vs[:, w, j, 64 * h:64 * h + 64],
                                                       me.pb[:, w // 2, j, 2 * (w % 2) + h, :, :], start=True, stop=True)
                            mm.then_inc(sm["o_done"], 1)
                        for p in range(NPAIR):
                            if p % 4 == 0:
                                pe.wait_ge(sm["o_taken"], 2 * G(n) + p // 4 + 1 + 2)
                            mm = pe.matmul(ring[:, 2, 0:P], me.wo[:, p, :], me.os[:, p, :], start=(p == 0), stop=(p == NPAIR - 1))
                        mm.then_inc(sm["y_done"], 1)

                    def before():
                        pe.wait_ge(S.weights_a, weights_count)
                        project(0, 0, 0)
                        project(1, 0, 1)
                        score(0, 0, False)

                    def step(n, b, i, more3, more2, more1):
                        if more2:
                            project(n + 2, b + 1 if i + 2 >= TT else b, (i + 2) % TT)
                        if more1:
                            score(n + 1, (i + 1) % 4, True)
                        weigh(n, i, more1)

                    steps(pe, before, step, lambda: None)

                @block.sync
                def _(sp):
                    def shift(b, i):
                        for half in range(2):
                            r, at = slice(64 * half, 64 * half + 64), P * i + 1 - half
                            sp.dma_start(me.xs[r, i, :], src[r, b, at:at + P + WIN]).then_inc(me.xs_ready[i], 16)

                    def before():
                        for i in range(3):
                            shift(0, i)

                    def step(n, b, i, more3, more2, more1):
                        if more3:
                            sp.wait_ge(sm["y_done"], G(n) + 4)
                            shift(b + 1 if i + 3 >= TT else b, (i + 3) % TT)

                    steps(sp, before, step, lambda: None)

                @block.gpsimd
                def _(pool):
                    def rotate(n):
                        for k in range(2):
                            pool.wait_ge(sm["cos_ready"], 2 * G(n) + k + 1 + 2)
                            pool.wait_ge(sm["sin_ready"], 2 * G(n) + k + 1 + 4)
                            pool.tensor_tensor(me.t1[:, k, :], me.t1[:, k, :], me.t2[:, k, :], ALU.add).then_inc(sm["add_ready"], 1)
                            pool.wait_ge(sm["add_ready"], 2 * G(n) + k + 1 + 2)
                            pool.wait_ge(sm["rn_ready"], 2 * G(n) + k + 1 + 4)
                            pool.wait_ge(sm["turn_done"], 4 * G(n) + 4 if k else 4 * G(n) + 2)
                            pool.tensor_tensor(me.qkn[:, k, :].rearrange("p (h d) -> p h d", h=H2),
                                               me.t1[:, k, :].rearrange("p (h d) -> p h d", h=H2),
                                               me.rn[:, k, :].unsqueeze(2).broadcast_to([P, H2, HD2]),
                                               ALU.mult).then_inc(sm["qkn_ready"], 1)

                    def normalize(n):
                        for u in range(2):
                            pool.wait_ge(sm["rsum_ready"], 2 * G(n) + u + 1)
                            pool.wait_ge(sm["pt_done"], 2 * G(n) + u - 1 + 4)
                            pool.tensor_tensor(me.pn[:, u, :, :], me.pr[:, u, :, :],
                                               me.rs[:, u, :].unsqueeze(2).broadcast_to([P, NPAIR, 2 * WIN]),
                                               ALU.mult).then_inc(sm["pn_ready"], 1)

                    def before():
                        rotate(0)
                        rotate(1)
                        normalize(0)

                    def step(n, b, i, more3, more2, more1):
                        if more2:
                            rotate(n + 2)
                        if more1:
                            normalize(n + 1)

                    steps(pool, before, step, lambda: None)

                @block.scalar
                def _(act):
                    def squares(n):
                        for k in range(2):
                            act.wait_ge(sm["proj_done"], 2 * G(n) + k + 1 + 4)
                            act.wait_ge(sm["ssmax_ready"], 2 * G(n) + k - 1 + 4)
                            act.activation(me.sq[:, k, :], pa[:, 2 * k:2 * k + 2, :].rearrange("p a b -> p (a b)"),
                                           ACT.Square).then_inc(sm["sq_ready"], 1)
                        for k in range(2):
                            act.wait_ge(sm["ssmax_ready"], 2 * G(n) + k + 1 + 4)
                            act.wait_ge(sm["qkn_ready"], 2 * G(n) + k - 1 + 2)
                            act.activation(me.rn[:, k, :], me.ss[:, k, :], ACT.Ln, scale=LN_RANGE).then_inc(sm["ln_step"], 1)
                            act.wait_ge(sm["ln_step"], 2 * G(n) + k + 1)
                            act.activation(me.rn[:, k, :], me.rn[:, k, :], ACT.Exp, scale=-0.5,
                                           bias=S.half_range[:, 0:1]).then_inc(sm["rn_ready"], 1)

                    def take_q(n):
                        for u in range(2):
                            act.wait_ge(sm["turn_done"], 4 * G(n) + u + 1 + 4)
                            act.wait_ge(sm["s_done"], 2 * G(n) + 4)
                            for half in range(2):
                                r = slice(64 * half, 64 * half + 64)
                                act.activation(me.qb[r, 4 * u:4 * u + 4, :, WIN * half:WIN * half + WIN],
                                               ring[r, u, :].rearrange("p (a w t) -> p a w t", a=4, w=NW),
                                               ACT.Identity).then_inc(sm["q_taken"], 1)

                    def exps(n):
                        for u in range(2):
                            act.wait_ge(sm["sub_ready"], 2 * G(n) + u + 1)
                            act.activation(me.pr[:, u, :, :], me.pr[:, u, :, :], ACT.Exp, scale=QK_SCALE).then_inc(sm["exp_ready"], 1)

                    def take_v(n):
                        for w in range(NW):
                            act.wait_ge(sm["v_done"], 4 * G(n) + w + 1)
                            act.wait_ge(sm["o_done"], 2 * G(n) + 4)
                            act.activation(me.vs[:, w, :, :].rearrange("p j m -> p (j m)"), ring[:, 2 + w % 2, :],
                                           ACT.Identity).then_inc(sm["v_taken"], 1)

                    def take_weighted(n):
                        for u in range(2):
                            act.wait_ge(sm["pt_done"], 2 * G(n) + u + 1 + 4)
                            for half in range(2):
                                r = slice(64 * half, 64 * half + 64)
                                act.activation(me.pb[r, u, :, :, half, :],
                                               ring[r, 2 + u, :].rearrange("p (j x t) -> p j x t", j=4, x=4),
                                               ACT.Identity).then_inc(sm["pt_taken"], 1)
                        for half in range(2):
                            act.wait_ge(sm["o_done"], 2 * G(n) + half + 1 + 4)
                            act.wait_ge(sm["y_done"], G(n) + 4)
                            act.activation(me.os[:, 4 * half:4 * half + 4, :].rearrange("p a t -> p (a t)"), ring[:, half, :],
                                           ACT.Identity).then_inc(sm["o_taken"], 1)

                    def before():
                        act.preload_act_table_set("natural_log_exp_and_others")
                        squares(0)
                        squares(1)
                        take_q(0)
                        exps(0)

                    def step(n, b, i, more3, more2, more1):
                        if more2:
                            squares(n + 2)
                        if more1:
                            take_q(n + 1)
                            exps(n + 1)
                        take_v(n)
                        take_weighted(n)

                    steps(act, before, step, lambda: None)

                @block.vector
                def _(dve):
                    def tables():
                        dve.wait_ge(S.weights_a, weights_count)
                        scales = me.qks[:, :, :]
                        cos, sin = me.cs[:, 0, :, :, :], me.cs[:, 1, :, :, :]
                        dve.tensor_tensor(cos, me.rope[:, 0, :, :, :], scales.unsqueeze(1).broadcast_to([P, TT, 2, HD2]), ALU.mult)
                        hd = HD2 // 2
                        for half in range(2):
                            to, other = slice(hd * half, hd * half + hd), slice(hd * (1 - half), hd * (1 - half) + hd)
                            ins = dve.tensor_tensor(sin[:, :, :, to], me.rope[:, 1, :, :, to],
                                                    scales[:, :, other].unsqueeze(1).broadcast_to([P, TT, 2, hd]), ALU.mult)
                        ins.then_inc(sm["table_step"], 1)
                        dve.wait_ge(sm["table_step"], layer + 1)

                    def rope(n, i):
                        hd = HD2 // 2
                        for k in range(2):
                            dve.wait_ge(sm["sq_ready"], 2 * G(n) + k + 1)
                            dve.tensor_reduce(me.ss[:, k, :], me.sq[:, k, :].rearrange("p (h d) -> p h d", h=H2), AX_X,
                                              ALU.add).then_inc(sm["ss_ready"], 1)
                            dve.wait_ge(sm["ss_ready"], 2 * G(n) + k + 1)
                            dve.wait_ge(sm["rn_ready"], 2 * G(n) + k - 1 + 4)
                            dve.tensor_scalar(me.ss[:, k, :], me.ss[:, k, :], 1e-24, None, ALU.max).then_inc(sm["ssmax_ready"], 1)
                        for k in range(2):
                            raw = pa[:, 2 * k:2 * k + 2, :].rearrange("p a (h d) -> p (a h) d", d=HD2)
                            dve.wait_ge(sm["add_ready"], 2 * G(n) + k - 1 + 2)
                            dve.wait_ge(sm["qkn_ready"], 2 * G(n) + k - 1 + 2)
                            dve.tensor_tensor(me.t1[:, k, :].rearrange("p (h d) -> p h d", h=H2), raw,
                                              me.cs[:, 0, i, k, :].unsqueeze(1).broadcast_to([P, H2, HD2]),
                                              ALU.mult).then_inc(sm["cos_ready"], 1)
                            t2 = me.t2[:, k, :].rearrange("p (h d) -> p h d", h=H2)
                            for half in range(2):
                                to, other = slice(hd * half, hd * half + hd), slice(hd * (1 - half), hd * (1 - half) + hd)
                                ins = dve.tensor_tensor(t2[:, :, to], raw[:, :, other],
                                                        me.cs[:, 1, i, k, to].unsqueeze(1).broadcast_to([P, H2, hd]), ALU.mult)
                            ins.then_inc(sm["sin_ready"], 1)

                    def take_k(n, i):
                        s = i % 2
                        for u in range(2):
                            dve.wait_ge(sm["turn_done"], 4 * G(n) + 2 + u + 1 + 4)
                            bank = ring[:, 2 + u, :].rearrange("p (a t) -> p a t", a=4)
                            dve.tensor_copy(me.kt[:, s, 4 * u:4 * u + 4, WIN:], bank)
                            dve.tensor_copy(me.kt[:, 1 - s, 4 * u:4 * u + 4, 0:WIN], bank[:, :, P - WIN:]).then_inc(sm["k_taken"], 1)

                    def softmax(n):
                        for u in range(2):
                            dve.wait_ge(sm["s_done"], 2 * G(n) + u + 1 + 4)
                            sc = ring[:, u, :].rearrange("p (a k) -> p a k", a=NPAIR)
                            dve.tensor_reduce(me.mx[:, u, :], sc, AX_X, ALU.max).then_inc(sm["max_ready"], 1)
                            dve.wait_ge(sm["max_ready"], 2 * G(n) + u + 1)
                            dve.wait_ge(sm["pn_ready"], 2 * G(n) + u - 1 + 4)
                            dve.tensor_tensor(me.pr[:, u, :, :], sc, me.mx[:, u, :].unsqueeze(2).broadcast_to([P, NPAIR, 2 * WIN]),
                                              ALU.subtract).then_inc(sm["sub_ready"], 1)
                        for u in range(2):
                            dve.wait_ge(sm["exp_ready"], 2 * G(n) + u + 1)
                            dve.tensor_reduce(me.su[:, u, :], me.pr[:, u, :, :], AX_X, ALU.add).then_inc(sm["sum_ready"], 1)
                            dve.wait_ge(sm["sum_ready"], 2 * G(n) + u + 1)
                            dve.reciprocal(me.rs[:, u, :], me.su[:, u, :]).then_inc(sm["rsum_ready"], 1)

                    def add_x(n, b, i):
                        dve.wait_ge(sm["y_done"], G(n) + 1 + 4)
                        at = slice(PADW + P * i, PADW + P * i + P)
                        dve.tensor_tensor(dst[:, b, at], ring[:, 2, 0:P], src[:, b, at], ALU.add).then_inc(sm["x_ready"], 1)

                    def before():
                        tables()
                        rope(0, 0)
                        rope(1, 1)
                        take_k(0, 0)
                        softmax(0)

                    def step(n, b, i, more3, more2, more1):
                        if more2:
                            rope(n + 2, (i + 2) % 4)
                        if more1:
                            take_k(n + 1, (i + 1) % 4)
                            softmax(n + 1)
                        add_x(n, b, i)

                    steps(dve, before, step, lambda: None)


def ffn_layer(core, F, layer, src, dst):
    nc, S, sm = core.nc, core, F.sm
    NC = 3
    sizes = [P, P, DI - 2 * P]
    with ExitStack() as ctx:
        pa = core.ps(ctx, "ff_pa", [P, NC, BANK])
        pg = core.ps(ctx, "ff_pg", [P, NC, BANK])
        py = core.ps(ctx, "ff_py", [P, 2, BANK])
        with nc.Block() as block:
            def loop(eng, one):
                with eng.Fori(0, B // 2) as r:
                    for u in range(2):
                        one(r * 2 + u, u)

            def G(b):
                return layer * B + b

            @block.tensor
            def _(pe):
                def one(b, u):
                    for c in range(NC):
                        pe.wait_ge(sm["gelu_ready"], NC * G(b) + c + 1)
                        pe.matmul(pg[0:sizes[c], c, :], F.w1[:, DI + P * c:DI + P * c + sizes[c]], S.h[:, b, :], start=True,
                                  stop=True).then_inc(sm["gate_done"], 1)
                        pe.wait_ge(sm["h_ready"], NC * G(b) + c + 1)
                        pe.matmul(pa[0:sizes[c], c, :], F.w1[:, P * c:P * c + sizes[c]], S.h[:, b, :], start=True,
                                  stop=True).then_inc(sm["a_done"], 1)
                    pe.wait_ge(sm["x_ready"], G(b) + 1)
                    for c in range(NC):
                        pe.wait_ge(sm["h_ready"], NC * G(b) + c + 4)
                        mm = pe.matmul(py[:, u, :], F.w2[0:sizes[c], c, :], F.hs[0:sizes[c], u, c, :], start=(c == 0),
                                       stop=(c == NC - 1))
                    mm.then_inc(sm["y_done"], 1)

                loop(pe, one)

            @block.scalar
            def _(act):
                def one(b, u):
                    for c in range(NC):
                        act.wait_ge(sm["gate_done"], NC * G(b) + c + 1)
                        act.wait_ge(sm["h_ready"], NC * G(b) + c + 1)
                        act.activation(F.gl[0:sizes[c], c, :], pg[0:sizes[c], c, :], ACT.Gelu,
                                       bias=F.b1[0:sizes[c], 3 + c:4 + c]).then_inc(sm["gelu_ready"], 1)

                act.preload_act_table_set("gelu_and_others")
                loop(act, one)

            @block.vector
            def _(dve):
                def one(b, u):
                    dve.wait_ge(sm["y_done"], G(b) + 1)
                    for c in range(NC):
                        dve.wait_ge(sm["a_done"], NC * G(b) + c + 1)
                        dve.wait_ge(sm["gelu_ready"], NC * G(b) + c + 4)
                        dve.scalar_tensor_tensor(out=F.hs[0:sizes[c], u, c, :], in0=pa[0:sizes[c], c, :],
                                                 scalar=F.b1[0:sizes[c], c:c + 1], in1=F.gl[0:sizes[c], c, :],
                                                 op0=ALU.add, op1=ALU.mult).then_inc(sm["h_ready"], 1)
                    dve.wait_ge(sm["y_done"], G(b) + 3)
                    dve.scalar_tensor_tensor(out=dst[:, b, PADW:], in0=py[:, u, :], scalar=F.b2[:, 0:1],
                                             in1=src[:, b, PADW:], op0=ALU.add, op1=ALU.add).then_inc(sm["x_ready"], 1)

                loop(dve, one)


class FeedForward:

    def __init__(self, core, ctx, work):
        self.sm = {n: core.sem("ff_" + n) for n in "gate_done a_done gelu_ready h_ready y_done x_ready shifted".split()}
        sb = lambda name, shape: core.sb(ctx, "ff_" + name, shape)
        self.w1, self.w2 = sb("w1", [P, 2 * DI]), sb("w2", [P, 3, P])
        self.b1, self.b2, self.lnp = sb("b1", [P, 6]), sb("b2", [P, 1]), sb("ln", [P, 2])
        flat = work[:, :, :, :].rearrange("p a b c -> p (a b c)")
        self.hs = flat[:, 0:6 * T].rearrange("p (u c t) -> p u c t", u=2, c=3)
        self.gl = flat[:, 6 * T:9 * T].rearrange("p (c t) -> p c t", c=3)


def shift_stage(core, F, layer, src):
    nc, S = core.nc, core
    with nc.Block() as block:
        @block.vector
        def _(dve):
            for b in range(B):
                dve.tensor_copy(S.h[0:64, b, :], src[0:64, b, PADW:])

        @block.scalar
        def _(act):
            for b in range(B):
                act.activation(S.h[64:P, b, :], src[64:P, b, PADW - 1:PADW - 1 + T], ACT.Identity)


def local_layers(core, A, C):
    nc, S = core.nc, core
    S.weights_a, S.weights_f = core.sem("weights_a"), core.sem("weights_f")
    added = core.sem("final_added")
    with ExitStack() as ctx:
        L = LocalAttention(core, ctx)
        F = FeedForward(core, ctx, L.work)

        def load_attention(sp, l):
            sp.dma_start(L.wqkv[:, :], A["L1_ffn_Wqkv"][l]).then_inc(S.weights_a, 16)
            sp.dma_start(L.wo[:, :, :], A["L1_ffn_Wo"][l].rearrange("(a p) d -> p a d", p=P)).then_inc(S.weights_a, 16)
            sp.dma_start(L.qks[:, 0, :], A["L1_ffn_q_scale"][l].partition_broadcast(P)).then_inc(S.weights_a, 16)
            sp.dma_start(L.qks[:, 1, :], A["L1_ffn_k_scale"][l].partition_broadcast(P)).then_inc(S.weights_a, 16)

        def load_feedforward(sp, l):
            sp.dma_start(F.w1[:, :], A["L1_ffn_W1"][l]).then_inc(S.weights_f, 16)
            sp.dma_start(F.w2[:, 0:2, :], A["L1_ffn_W2"][l][0:2 * P, :].rearrange("(a p) d -> p a d", p=P)).then_inc(S.weights_f, 16)
            sp.dma_start(F.w2[0:DI - 2 * P, 2, :], A["L1_ffn_W2"][l][2 * P:DI, :]).then_inc(S.weights_f, 16)
            for c in range(2):
                sp.dma_start(F.b1[:, 3 * c:3 * c + 2], A["L1_ffn_b1"][l][DI * c:DI * c + 2 * P].rearrange("(a p) -> p a", p=P)).then_inc(S.weights_f, 16)
                sp.dma_start(F.b1[0:DI - 2 * P, 3 * c + 2:3 * c + 3], column(A["L1_ffn_b1"][l][DI * c + 2 * P:DI * c + DI])).then_inc(S.weights_f, 16)
            for ap, n in ((F.b2[:, 0:1], "b2"), (F.lnp[:, 0:1], "ln_g"), (F.lnp[:, 1:2], "ln_b")):
                sp.dma_start(ap, column(A["L1_ffn_" + n][l])).then_inc(S.weights_f, 16)

        norm_stage(S, lambda b: S.xr[:, b, :], lambda b: S.xa[:, b, PADW:],
                   lambda b: S.mod[:, 1, 4, b:b + 1], lambda b: S.mod[:, 1, 3, b:b + 1])(5 * B)
        L.setup(A, C)
        norm = norm_stage(core, lambda b: S.h[:, b, :], lambda b: S.h[:, b, :], lambda b: F.lnp[:, 0:1], lambda b: F.lnp[:, 1:2])
        with nc.Block() as block:
            @block.sync
            def _(sp):
                load_attention(sp, 0)

            @block.vector
            def _(dve):
                for n, k in (("gelu_ready", 3), ("h_ready", 3), ("x_ready", 2), ("y_done", 2)):
                    dve.sem_inc(F.sm[n], k)
        with nc.Fori(0, DEPTH) as layer:
            with nc.Block() as block:
                @block.sync
                def _(sp):
                    with nc.allow_non_contiguous_dma("small vectors turned onto the partitions"):
                        load_feedforward(sp, layer)
            L.layer(layer, 64 * layer + 64, S.xa, S.xb, A)
            with nc.Block() as block:
                @block.sync
                def _(sp):
                    sp.wait_ge(S.weights_f, 160 * layer + 160)
                    load_attention(sp, (layer + 1) % DEPTH)
            shift_stage(core, F, layer, S.xb)
            norm((layer + 6) * B)
            ffn_layer(core, F, layer, S.xb, S.xa)
        with nc.Block() as block:
            @block.sync
            def _(sp):
                sp.wait_ge(S.weights_a, 64 * DEPTH + 64)

            @block.vector
            def _(dve):
                for b in range(B):
                    dve.scalar_tensor_tensor(out=S.xr[:, b, :], in0=S.xa[:, b, PADW:], scalar=S.mod[:, 1, 5, b:b + 1],
                                             in1=S.xr[:, b, :], op0=ALU.mult, op1=ALU.add)


def program(nc, A, C, out):
    with ExitStack() as ctx:
        nc.disable_value_cache = True
        S = Core(nc, ctx)
        S.xr = S.sb(ctx, "xr", [P, B, T])
        S.h = S.sb(ctx, "h", [P, B, T])
        S.xa = S.sb(ctx, "xa", [P, B, XW])
        S.xb = S.sb(ctx, "xb", [P, B, XW])
        S.ident, S.mean, S.center = (S.sb(ctx, n, [P, P]) for n in ("ident", "mean", "center"))
        S.identb = S.sb(ctx, "identb", [P, P], BF16)
        S.mod = S.sb(ctx, "mod", [P, 2, 6, B])
        S.eps = S.sb(ctx, "eps", [P, 1])
        S.half_range = S.sb(ctx, "half_range", [P, 1])
        l0 = ctx.enter_context(ExitStack())
        S.cos0, S.sin0 = (S.sb(l0, n, [P, T]) for n in ("cos0", "sin0"))
        S.swap0, S.headmask0 = S.sb(l0, "swap0", [P, P]), S.sb(l0, "headmask0", [P, H0])
        S.pick = S.sb(l0, "pick", [P, H0, P], BF16)
        S.bq = S.sb(l0, "bq", [P, 4])
        S.bo0 = S.sb(l0, "bo0", [P, 1])
        S.bv0 = S.sb(l0, "bv0", [P, P])
        S.w0 = S.sb(l0, "w0", [P, 6, P])
        S.norms = 0
        S.norm_sems = [S.sem("norm_" + n) for n in ("centered", "squared", "var", "ln", "rstd", "scaled", "done")]
        S.constants_set = S.sem("constants_set")
        with nc.Block() as block:
            @block.vector
            def _(dve):
                dve.memset(S.eps[:, :], EPS).then_inc(S.constants_set, 1)
                dve.memset(S.half_range[:, :], float(0.5 * np.log(LN_RANGE))).then_inc(S.constants_set, 1)
                dve.wait_ge(S.constants_set, 2)
        prelude(S, A, C)
        norm_stage(S, lambda b: S.xr[:, b, :], lambda b: S.h[:, b, :],
                   lambda b: S.mod[:, 0, 1, b:b + 1], lambda b: S.mod[:, 0, 0, b:b + 1])(0)
        attention0(S)
        ffn0(S, A, C)
        l0.close()
        norm_stage(S, lambda b: S.xr[:, b, :], lambda b: S.h[:, b, :],
                   lambda b: S.mod[:, 1, 1, b:b + 1], lambda b: S.mod[:, 1, 0, b:b + 1])(4 * B)
        attention1(S, A, C)
        local_layers(S, A, C)
        store(S, out, S.xr)


def store(core, out, src):
    nc, S = core.nc, core
    turned, taken, stored = core.sem("out_turned"), core.sem("out_taken"), core.sem("out_stored")
    with ExitStack() as ctx:
        px = core.ps(ctx, "out_px", [P, 4, BANK])
        xt = core.sb(ctx, "out_tokens", [P, B, T])
        with nc.Block() as block:
            @block.tensor
            def _(pe):
                for n in range(B):
                    if n >= 4:
                        pe.wait_ge(taken, n - 3)
                    for c in range(TT):
                        tr = pe.transpose(px[:, n % 4, P * c:P * c + P], src[:, n, P * c:P * c + P], S.ident[:, :])
                    tr.then_inc(turned, 1)

            @block.scalar
            def _(act):
                for n in range(B):
                    act.wait_ge(turned, n + 1)
                    act.activation(xt[:, n, :], px[:, n % 4, :], ACT.Identity).then_inc(taken, 1)

            @block.sync
            def _(sp):
                for n in range(B):
                    sp.wait_ge(taken, n + 1)
                    sp.dma_start(out[n].rearrange("(c p) d -> p c d", p=P),
                                 xt[:, n, :].rearrange("p (c d) -> p c d", c=TT)).then_inc(stored, 16)
                sp.wait_ge(stored, 16 * B)


INPUTS = ['L0_attn_x', 'L0_attn_Wq', 'L0_attn_bq', 'L0_attn_Wk', 'L0_attn_bk', 'L0_attn_Wv', 'L0_attn_bv', 'L0_attn_Wo',
          'L0_attn_bo', 'L0_ffn_g1', 'L0_ffn_be1', 'L0_ffn_mix_w', 'L0_ffn_mix_b', 'L0_ffn_g2', 'L0_ffn_be2',
          'L0_ffn_router_w', 'L0_ffn_w1', 'L0_ffn_b1', 'L0_ffn_w2', 'L0_ffn_b2', 'L0_c', 'L0_wmod', 'L1_attn_phase',
          'L1_attn_Wq', 'L1_attn_bq', 'L1_attn_Wk', 'L1_attn_bk', 'L1_attn_Wv', 'L1_attn_bv', 'L1_attn_Wo', 'L1_attn_bo',
          'L1_ffn_Wqkv', 'L1_ffn_q_scale', 'L1_ffn_k_scale', 'L1_ffn_Wo', 'L1_ffn_ln_g', 'L1_ffn_ln_b', 'L1_ffn_W1',
          'L1_ffn_b1', 'L1_ffn_W2', 'L1_ffn_b2', 'L1_c', 'L1_wmod']


def kernel(**inputs):
    import concourse.bacc as bacc
    from concourse.bass_utils import run_bass_kernel_spmd

    nc = bacc.Bacc("TRN2", target_bir_lowering=False, num_devices=1)
    arrays, args, tables = {}, {}, {}
    for name in INPUTS:
        a = np.ascontiguousarray(inputs[name])
        arrays[f"in_{name}"] = a
        args[name] = nc.dram_tensor(f"in_{name}", a.shape, mybir.dt.from_np(a.dtype), kind="ExternalInput").ap()
    for name, a in constants().items():
        a = np.ascontiguousarray(a)
        arrays[f"const_{name}"] = a
        tables[name] = nc.dram_tensor(f"const_{name}", a.shape, mybir.dt.from_np(a.dtype), kind="ExternalInput").ap()
    out = nc.dram_tensor("out", (B, T, D), F32, kind="ExternalOutput").ap()
    program(nc, args, tables, out)
    r = run_bass_kernel_spmd(nc, [arrays], core_ids=[0])
    return r.results[0]["out"]
```

```python
from contextlib import ExitStack

import numpy as np

import concourse.bass as bass
from concourse import mybir

F32 = mybir.dt.float32
BF16 = mybir.dt.bfloat16
ACT = mybir.ActivationFunctionType
ALU = mybir.AluOpType
AX_X = mybir.AxisListType.X

B, T, D = 8, 512, 128
P = 128
TT = T // P
EPS = 1e-5
BANK = 512
NEG = -1e30

H0, HD0 = 16, 8
E0, F0 = 8, 512
H1, HD1, TB = 4, 128, 32
DEPTH, H2, HD2, WIN = 6, 16, 64, 32
INNER = H2 * HD2
QK_SCALE = 8.0
DI = 341
PADW = WIN + 1
XW = PADW + T
LN_RANGE = 2.0 ** 20


def constants():
    f = np.float32
    c = {}
    c["ident"] = np.eye(P, dtype=f)
    c["mean"] = np.full((P, P), 1.0 / P, f)
    c["center"] = (np.eye(P) - 1.0 / P).astype(f)
    half = HD0 // 2
    inv = (1.0 / f(10000.0) ** (np.arange(0, HD0, 2, dtype=f) / f(HD0))).astype(f)
    ang = (np.arange(T, dtype=f)[:, None] * inv[None, :]).astype(f)
    d = np.arange(P) % HD0
    c["cos0"] = np.cos(ang).astype(f).T[d % half].copy()
    c["sin0"] = (np.sin(ang).astype(f).T[d % half] * np.where(d < half, -1, 1)[:, None]).astype(f)
    other = np.arange(P) + np.where(d < half, half, -half)
    swap = np.zeros((P, P), f)
    swap[other, np.arange(P)] = 1
    c["swap0"] = swap
    pick = np.zeros((P, E0, P), f)
    for part in range(3):
        for h in range(E0):
            pick[32 * part + h, h, :] = 1
    c["pick"] = pick.reshape(P, E0 * P)
    c["lower"] = np.broadcast_to(np.tril(np.ones((E0, E0), f), -1).reshape(1, -1), (P, E0 * E0)).copy()
    t = np.arange(P) % TB
    c["mask1"] = np.where(t[:, None] == t[None, :], 0, NEG).astype(f)
    q = (np.arange(P) % WIN)[:, None]
    k = np.arange(2 * WIN)[None, :]
    ok = (q <= k) & (q >= k - WIN)
    first = ok & ((np.arange(P)[:, None] >= 64) | (k >= WIN))
    c["mask2"] = np.concatenate([np.where(ok, 0, NEG), np.where(first, 0, NEG)], 1).astype(f)
    hf = np.arange(0, HD2, 2, dtype=f)
    inv = (1.0 / f(10000.0) ** (hf / f(HD2))).astype(f)
    tok = np.arange(T, dtype=f)
    ang = (tok[:, None] * inv[None, :]).astype(f)
    ang = np.concatenate([ang, ang], 1)
    base = ((hf + f(0.4 * HD2)) / f(1.4 * HD2)).astype(f)
    power = ((tok - T // 2) / f(WIN // 2)).astype(f)
    scale = (base[None, :] ** power[:, None]).astype(f)
    scale = np.concatenate([scale, scale], 1)
    sign = np.where(np.arange(HD2) < HD2 // 2, -1, 1).astype(f)
    cos, sin = np.cos(ang).astype(f), (np.sin(ang) * sign).astype(f)
    co = np.stack([cos * scale, cos / scale], 1).reshape(TT, P, 2, HD2).transpose(1, 0, 2, 3)
    si = np.stack([sin * scale, sin / scale], 1).reshape(TT, P, 2, HD2).transpose(1, 0, 2, 3)
    c["cos2"] = np.ascontiguousarray(co.reshape(P, -1)).astype(f)
    c["sin2"] = np.ascontiguousarray(si.reshape(P, -1)).astype(f)
    return c


def column(v):
    return v.rearrange("(p one) -> p one", one=1)


def across(v, n=P):
    return v.partition_broadcast(n)


class Core:

    def __init__(self, nc, ctx):
        self.nc, self.ctx = nc, ctx

    def sb(self, ctx, name, shape, dt=F32):
        return ctx.enter_context(self.nc.sbuf_tensor(name, shape, dt))

    def ps(self, ctx, name, shape, dt=F32):
        return ctx.enter_context(self.nc.psum_tensor(name, shape, dt))

    def sem(self, name):
        return self.ctx.enter_context(self.nc.semaphore(name))


def prelude(core, A, C):
    nc = core.nc
    loaded, small, cast = core.sem("x_loaded"), core.sem("small_loaded"), core.sem("pick_loaded")
    turned, taken = core.sem("x_turned"), core.sem("x_taken")
    silu_ready, silu_turned, silu_t_ready = core.sem("silu_ready"), core.sem("silu_turned"), core.sem("silu_t_ready")
    mod_done, gate_step = core.sem("mod_done"), core.sem("gate_step")
    w_turned, w_taken = core.sem("w_turned"), core.sem("w_taken")
    bias_turned = core.sem("bias_turned")
    S = core
    with ExitStack() as ctx:
        xt = core.sb(ctx, "x_tokens", [P, B * TT, P])
        cc = core.sb(ctx, "cond", [B, 2, P])
        sc = core.sb(ctx, "cond_silu", [B, 2, P])
        sct = core.sb(ctx, "cond_silu_t", [P, 2, B])
        wmod = core.sb(ctx, "wmod", [P, 2, 6 * P])
        w4 = core.sb(ctx, "w_l0", [P, 4, P])
        sg = core.sb(ctx, "gate_sign", [P, 2 * B])
        ab = core.sb(ctx, "gate_size", [P, 2 * B])
        ra = core.sb(ctx, "gate_raw", [P, 2 * B])
        px = core.ps(ctx, "px", [P, 4, BANK])
        pm = core.ps(ctx, "pm", [P, 2, BANK])
        pw = core.ps(ctx, "pw", [P, 2, BANK])
        names = ["L0_attn_Wq", "L0_attn_Wk", "L0_attn_Wv", "L0_attn_Wo"]
        NSMALL = 6 + 2 + 2 + 4 + 4
        with nc.Block() as block:
            @block.sync
            def _(sp):
                for g in range(4):
                    sp.dma_start(xt[:, 8 * g:8 * g + 8, :],
                                 A["L0_attn_x"].rearrange("b t d -> (b t) d")[1024 * g:1024 * g + 1024, :]
                                 .rearrange("(n p) d -> p n d", p=P)).then_inc(loaded, 16)
                for n, ap in (("L0_attn_bk", S.bq[:, 1:2]), ("L0_attn_bq", S.bq[:, 0:1]), ("L0_attn_bo", S.bo0[:, :])):
                    sp.dma_start(ap, column(A[n])).then_inc(small, 16)
                sp.dma_start(S.bv0[:, :], across(A["L0_attn_bv"])).then_inc(small, 16)
                sp.wait_ge(loaded, 64)
                sp.wait_ge(small, 16 * NSMALL)

            @block.gpsimd
            def _(pool):
                pool.dma_start(S.pick[:, :, :].rearrange("p h m -> p (h m)"), C["pick"]).then_inc(cast, 16)
                pool.dma_start(S.identb[:, :], C["ident"]).then_inc(cast, 16)
                pool.memset(S.xa[:, :, 0:PADW], 0.0)
                pool.memset(S.xb[:, :, 0:PADW], 0.0)
                pool.wait_ge(cast, 32)

            @block.tensor
            def _(pe):
                pe.wait_ge(small, 16 * NSMALL)
                pe.wait_ge(silu_ready, 1)
                for l in range(2):
                    tr = pe.transpose(pm[:, 0, 8 * l:8 * l + 8], sc[:, l, :], S.ident[0:B, 0:B])
                tr.then_inc(silu_turned, 1)
                pe.transpose(pw[:, 0, 0:128], w4[:, 0, :], S.ident[:, :])
                pe.transpose(pw[:, 0, 128:256], w4[:, 1, :], S.ident[:, :])
                pe.transpose(pw[:, 0, 256:384], w4[:, 2, :], S.ident[:, :])
                pe.transpose(pw[:, 0, 384:512], w4[:, 3, :], S.ident[:, :]).then_inc(w_turned, 1)
                pe.matmul(pw[:, 1, 0:128], w4[:, 0, :], S.swap0[:, :], start=True, stop=True)
                pe.matmul(pw[:, 1, 128:256], w4[:, 1, :], S.swap0[:, :], start=True, stop=True)
                pe.matmul(pw[:, 1, 256:258], S.swap0[:, :], S.bq[:, 0:2], start=True, stop=True).then_inc(w_turned, 1)
                pe.wait_ge(silu_t_ready, 1)
                for l in range(2):
                    for j in range(6):
                        at = (l * 6 + j) * B
                        mm = pe.matmul(pm[:, 1, at:at + B], wmod[:, l, P * j:P * j + P], sct[:, l, :],
                                       start=True, stop=True)
                mm.then_inc(mod_done, 1)
                pe.wait_ge(loaded, 64)
                for n in range(B * TT // 4):
                    if n >= 4:
                        pe.wait_ge(taken, n - 3)
                    for c in range(4):
                        tr = pe.transpose(px[:, n % 4, P * c:P * c + P], xt[:, 4 * n + c, :], S.ident[:, :])
                    tr.then_inc(turned, 1)

            @block.scalar
            def _(act):
                for n, ap in (("ident", S.ident), ("mean", S.mean), ("center", S.center), ("cos0", S.cos0),
                              ("sin0", S.sin0), ("swap0", S.swap0)):
                    act.dma_start(ap[:, :], C[n]).then_inc(small, 16)
                for l in range(2):
                    act.dma_start(cc[:, l, :], A[f"L{l}_c"]).then_inc(small, 16)
                    act.dma_start(wmod[:, l, :], A[f"L{l}_wmod"]).then_inc(small, 16)
                for i, n in enumerate(names):
                    act.dma_start(w4[:, i, :], A[n]).then_inc(small, 16)
                act.wait_ge(small, 16 * NSMALL)
                act.activation(sc[:, :, :], cc[:, :, :], ACT.Silu).then_inc(silu_ready, 1)
                for n in range(B * TT // 4):
                    act.wait_ge(turned, n + 1)
                    act.activation(S.xr[:, n, :], px[:, n % 4, :], ACT.Identity).then_inc(taken, 1)

            @block.vector
            def _(dve):
                dve.wait_ge(silu_turned, 1)
                dve.tensor_copy(sct[:, :, :].rearrange("p l b -> p (l b)"), pm[:, 0, 0:2 * B]).then_inc(silu_t_ready, 1)
                dve.wait_ge(w_turned, 1)
                dve.tensor_copy(S.w0[:, 0:4, :].rearrange("p n m -> p (n m)"), pw[:, 0, :])
                dve.wait_ge(w_turned, 2)
                dve.tensor_copy(S.w0[:, 4:6, :].rearrange("p n m -> p (n m)"), pw[:, 1, 0:256])
                dve.tensor_copy(S.bq[:, 2:4], pw[:, 1, 256:258])
                dve.wait_ge(mod_done, 1)
                m = pm[:, 1, 0:12 * B].rearrange("p (l j b) -> p l j b", l=2, j=6)
                for j in (0, 3):
                    dve.tensor_copy(S.mod[:, :, j, :], m[:, :, j, :])
                for j in (1, 4):
                    dve.tensor_scalar(S.mod[:, :, j, :], m[:, :, j, :], 1.0, None, ALU.add)
                n = 0
                for j in (2, 5):
                    raw = ra[:, :].rearrange("p (l b) -> p l b", l=2)
                    sgn, size = sg[:, :].rearrange("p (l b) -> p l b", l=2), ab[:, :].rearrange("p (l b) -> p l b", l=2)
                    for ins in (lambda: dve.tensor_scalar(sgn, m[:, :, j, :], 0.0, 2.0, ALU.is_ge, ALU.mult),
                                lambda: dve.tensor_scalar(sgn, sgn, 1.0, None, ALU.subtract),
                                lambda: dve.tensor_copy(raw, m[:, :, j, :]),
                                lambda: dve.scalar_tensor_tensor(out=size, in0=raw, scalar=-1.0, in1=raw, op0=ALU.mult, op1=ALU.max),
                                lambda: dve.tensor_scalar(size, size, 0.25, None, ALU.max),
                                lambda: dve.tensor_tensor(S.mod[:, :, j, :], sgn, size, ALU.mult)):
                        ins().then_inc(gate_step, 1)
                        n += 1
                        dve.wait_ge(gate_step, n)


def norm_stage(core, source, target, scale, shift, batches=B):
    nc, S = core.nc, core
    U = 4
    S.norms += 1
    tag = f"norm{S.norms}"
    centered, squared, var_done, ln_step, rstd_ready, scaled, done = S.norm_sems

    def stage(before):
        with ExitStack() as ctx:
            pc = core.ps(ctx, tag + "_pc", [P, U, BANK])
            pv = core.ps(ctx, tag + "_pv", [P, U, BANK])
            work = core.sb(ctx, tag + "_work", [P, U, T])
            with nc.Block() as block:
                @block.tensor
                def _(pe):
                    for r in range(batches // U):
                        for u in range(U):
                            b = U * r + u
                            if b >= U:
                                pe.wait_ge(scaled, before + b - U + 1)
                            pe.matmul(pc[:, u, :], S.center[:, :], source(b), start=True, stop=True).then_inc(centered, 1)
                        for u in range(U):
                            b = U * r + u
                            pe.wait_ge(squared, before + b + 1)
                            if b >= U:
                                pe.wait_ge(rstd_ready, before + b - U + 1)
                            pe.matmul(pv[:, u, :], S.mean[:, :], work[:, u, :], start=True, stop=True).then_inc(var_done, 1)

                @block.scalar
                def _(act):
                    act.preload_act_table_set("natural_log_exp_and_others")
                    for r in range(batches // U):
                        for u in range(U):
                            b = U * r + u
                            act.wait_ge(centered, before + b + 1)
                            if b >= U:
                                act.wait_ge(done, before + b - U + 1)
                            act.activation(work[:, u, :], pc[:, u, :], ACT.Square).then_inc(squared, 1)
                        for u in range(U):
                            b = U * r + u
                            act.wait_ge(var_done, before + b + 1)
                            act.activation(work[:, u, :], pv[:, u, :], ACT.Ln, bias=S.eps[:, 0:1]).then_inc(ln_step, 1)
                            act.wait_ge(ln_step, before + b + 1)
                            act.activation(work[:, u, :], work[:, u, :], ACT.Exp, scale=-0.5).then_inc(rstd_ready, 1)

                @block.vector
                def _(dve):
                    for b in range(batches):
                        u = b % U
                        dve.wait_ge(rstd_ready, before + b + 1)
                        dve.tensor_tensor(work[:, u, :], pc[:, u, :], work[:, u, :], ALU.mult).then_inc(scaled, 1)
                        dve.wait_ge(scaled, before + b + 1)
                        dve.tensor_scalar(target(b), work[:, u, :], scale(b), shift(b), ALU.mult, ALU.add).then_inc(done, 1)

    return stage


def attention0(core):
    nc, S = core.nc, core
    names = ("proj_done rope_step q_ready parts_step v_done v_ready rep_done rep_taken score_done max_ready maxt_done "
             "part_step rows_ready gated st_done exp_done pv_done o_ready ot_done onorm_step of_done of_ready y_done "
             "x_ready hs_ready zeroed sel_ready").split()
    sm = {n: core.sem("a0_" + n) for n in names}
    NS = H0 * TT
    NE = NS // 2
    GH = 4
    NP = 3
    KR = NP * NP * HD0
    NPT = 6
    HH = H0 // 2
    MR = 96
    KM = MR + NP
    with ExitStack() as ctx:
        hs = core.sb(ctx, "a0_hs", [P, T])
        ta, tb = core.sb(ctx, "a0_ta", [P, 2, T]), core.sb(ctx, "a0_tb", [P, 2, T])
        qk = core.sb(ctx, "a0_qk", [P, 2, T])
        rest = core.sb(ctx, "a0_rest", [P, 2, T])
        parts = core.sb(ctx, "a0_parts", [P, NP, 2, T], BF16)
        sel = core.sb(ctx, "a0_sel", [P, 2, NP, H0, KR], BF16)
        qs = core.sb(ctx, "a0_stacked", [P, 2, H0, T], BF16)
        vv = core.sb(ctx, "a0_v", [P, TT, H0, 32])
        mx = core.sb(ctx, "a0_max", [P, 2, TT, HH])
        rem = core.sb(ctx, "a0_rem", [HH, 2, T])
        mid = core.sb(ctx, "a0_mid", [HH, T], BF16)
        mb = core.sb(ctx, "a0_maxparts", [96, T], BF16)
        pt = core.sb(ctx, "a0_probs", [P, NPT, T])
        os_ = core.sb(ctx, "a0_o", [P, 2, T])
        rc = core.sb(ctx, "a0_rsum", [P, TT, GH])
        on = core.sb(ctx, "a0_onorm", [P, TT, P])
        of = core.sb(ctx, "a0_of", [P, T])
        tx = core.sb(ctx, "a0_tx", [P, T])
        ring = core.ps(ctx, "a0_ring", [P, 4, BANK])
        og = core.ps(ctx, "a0_og", [P, 2, BANK])
        t1 = core.ps(ctx, "a0_t1", [P, BANK])
        t2 = core.ps(ctx, "a0_t2", [P, BANK])
        with nc.Block() as block:
            def sequences(eng, one):
                with eng.Fori(0, B - 1) as b:
                    one(b, False)
                one(B - 1, True)

            def head_of(n):
                return n // (GH * TT), n // GH % TT, n % GH

            @block.gpsimd
            def _(pool):
                pool.memset(vv[:, :, :, :].rearrange("p c h m -> p (c h m)"), 0.0).then_inc(sm["zeroed"], 1)
                pool.wait_ge(sm["zeroed"], 1)
                pool.memset(vv[:, :, :, HD0:HD0 + 1], 1.0).then_inc(sm["zeroed"], 1)
                pool.wait_ge(sm["zeroed"], 2)
                pool.tensor_copy(hs[:, :], S.h[:, 0, :]).then_inc(sm["hs_ready"], 1)
                with pool.Fori(0, B - 1) as b:
                    pool.wait_ge(sm["v_done"], b + 1)
                    pool.tensor_copy(hs[:, :], S.h[:, b + 1, :]).then_inc(sm["hs_ready"], 1)

            @block.sync
            def _(sp):
                def rows(b, last):
                    for half in range(2):
                        sp.wait_ge(sm["part_step"], b * 12 + 6 * half + 6)
                        if half:
                            sp.wait_ge(sm["rows_ready"], (2 * b + 1) * 16 * NP)
                        for i in range(NP):
                            sp.dma_start(qs[MR + i:MR + i + 1, 0, HH * half:HH * half + HH, :],
                                         mb[32 * i:32 * i + HH, :]).then_inc(sm["rows_ready"], 16)

                sequences(sp, rows)

            @block.tensor
            def _(pe):
                def project(b, i):
                    if i == 0:
                        pe.wait_ge(sm["hs_ready"], b + 1)
                    else:
                        pe.wait_ge(sm["rope_step"], b * 4 + i)
                    pe.matmul(t2[:, :], S.w0[:, (0, 4, 1, 5)[i], :], hs[:, :], start=True, stop=True).then_inc(sm["proj_done"], 1)

                def one(b, last):
                    pe.wait_ge(sm["onorm_step"], b * 8 + 1)
                    for c in range(TT):
                        mm = pe.matmul(t1[:, P * c:P * c + P], hs[:, P * c:P * c + P], S.w0[:, 2, :], start=True, stop=True)
                    mm.then_inc(sm["v_done"], 1)

                    def stack(h):
                        if h == 0:
                            pe.wait_ge(sm["parts_step"], b * 4 + 4)
                            pe.wait_ge(sm["o_ready"], b * 4 + 1)
                        else:
                            pe.wait_ge(sm["rep_taken"], (b * H0 + h) * 2 - 1)
                        for x in range(2):
                            if h and x:
                                pe.wait_ge(sm["rep_taken"], (b * H0 + h) * 2)
                            for i in range(NP):
                                mm = pe.matmul(og[0:KR, x, :], sel[:, x, i, h, :], parts[:, i, x, :], start=(i == 0),
                                               stop=(i == NP - 1))
                            mm.then_inc(sm["rep_done"], 1)

                    def largest(h):
                        pe.wait_ge(sm["rep_taken"], (b * H0 + h) * 2 + 2)
                        for c in range(TT):
                            n = h * TT + c
                            if n >= 4 and n % 2 == 0:
                                pe.wait_ge(sm["max_ready"], b * NE + (n - 4) // 2 + 1)
                            pe.matmul(ring[:, n % 4, :], qs[0:KR, 0, h, P * c:P * c + P], qs[0:KR, 1, h, :], start=True,
                                      stop=True).then_inc(sm["score_done"], 1)

                    pe.wait_ge(sm["exp_done"], b * NE + 1)

                    def turn_maxima(half):
                        pe.wait_ge(sm["max_ready"], b * NE + NE // 2 * (half + 1))
                        if half == 0:
                            pe.wait_ge(sm["x_ready"], b + 1)
                        else:
                            pe.wait_ge(sm["part_step"], b * 12 + 6)
                        for c in range(TT):
                            tr = pe.transpose(t2[0:HH, P * c:P * c + P], mx[:, half, c, :], S.ident[:, :])
                        tr.then_inc(sm["maxt_done"], 1)

                    for h in range(H0 + 1):
                        if h < H0:
                            stack(h)
                        if h:
                            largest(h - 1)
                        if h == HH + 2:
                            turn_maxima(0)
                    turn_maxima(1)

                    def scores(n):
                        g, c, j = head_of(n)
                        if n in (0, NS // 2):
                            pe.wait_ge(sm["rows_ready"], (2 * b + n // (NS // 2) + 1) * 16 * NP)
                        if n >= 4 and n % 2 == 0:
                            pe.wait_ge(sm["exp_done"], b * NE + (n - 4) // 2 + 2)
                        pe.matmul(ring[:, n % 4, :], qs[0:KM, 1, GH * g + j, P * c:P * c + P], qs[0:KM, 0, GH * g + j, :],
                                  start=True, stop=True).then_inc(sm["st_done"], 1)

                    def weighted(n):
                        g, c, j = head_of(n)
                        pe.wait_ge(sm["exp_done"], b * NE + n // 2 + 2)
                        if n == 0:
                            pe.wait_ge(sm["v_ready"], b + 1)
                        if g >= 2 and n % (GH * TT) == 0:
                            pe.wait_ge(sm["o_ready"], b * 4 + g)
                        pe.matmul(og[32 * j:32 * j + 32, g % 2, :], vv[:, c, GH * g + j, :], pt[:, n % NPT, :], start=(c == 0),
                                  stop=(c == TT - 1)).then_inc(sm["pv_done"], 1)

                    def turn_out(g):
                        pe.wait_ge(sm["o_ready"], b * 4 + g + 2)
                        if g:
                            pe.wait_ge(sm["onorm_step"], b * 8 + 2 * g + 1)
                        for c in range(TT):
                            tr = pe.transpose(t1[:, P * c:P * c + P], os_[:, g % 2, P * c:P * c + P], S.ident[:, :])
                        tr.then_inc(sm["ot_done"], 1)

                    LAG = NPT
                    for n in range(0, NS + LAG, 2):
                        if n >= LAG:
                            weighted(n - LAG)
                            weighted(n - LAG + 1)
                        if n < NS:
                            scores(n)
                            scores(n + 1)
                        if n % (GH * TT) == 8 and n > GH * TT:
                            turn_out(n // (GH * TT) - 1)
                        if n == 16:
                            pe.wait_ge(sm["part_step"], b * 12 + 8)
                        if not last and n in (16, 20, 24, 28):
                            project(b + 1, n // 4 - 4)
                    turn_out(3)
                    pe.wait_ge(sm["onorm_step"], b * 8 + 9)
                    if not last:
                        pe.wait_ge(sm["rope_step"], b * 4 + 8)
                    for c in range(TT):
                        tr = pe.transpose(t2[:, P * c:P * c + P], on[:, c, :], S.ident[:, :])
                    tr.then_inc(sm["of_done"], 1)
                    pe.wait_ge(sm["of_ready"], b + 1)
                    pe.matmul(t2[:, :], S.w0[:, 3, :], of[:, :], start=True, stop=True).then_inc(sm["y_done"], 1)

                for i in range(4):
                    project(0, i)
                pe.wait_ge(sm["sel_ready"], 9)
                sequences(pe, one)

            @block.scalar
            def _(act):
                def one(b, last):
                    def copy_out(g):
                        act.wait_ge(sm["pv_done"], b * NS + GH * TT * (g + 1))
                        if g >= 2:
                            act.wait_ge(sm["ot_done"], b * 4 + g - 1)
                        act.activation(os_[:, g % 2, :], og[:, g % 2, :], ACT.Identity).then_inc(sm["o_ready"], 1)

                    for h in range(H0):
                        for x in range(2):
                            act.wait_ge(sm["rep_done"], (b * H0 + h) * 2 + x + 1)
                            act.activation(qs[0:KR, x, h, :], og[0:KR, x, :], ACT.Identity).then_inc(sm["rep_taken"], 1)
                    for m in range(NE):
                        act.wait_ge(sm["st_done"], b * NS + 2 * m + 2)
                        if 2 * m >= NPT:
                            act.wait_ge(sm["pv_done"], b * NS + 2 * m - NPT + 2)
                        s, to = 2 * m % 4, 2 * m % NPT
                        act.activation(pt[:, to:to + 2, :], ring[:, s:s + 2, :], ACT.Exp,
                                       scale=float(HD0) ** -0.5).then_inc(sm["exp_done"], 1)
                        if m % 8 == 3 and m > 8:
                            copy_out(m // 8 - 1)
                    copy_out(3)
                    act.wait_ge(sm["of_done"], b + 1)
                    act.activation(of[:, :], t2[:, :], ACT.Identity).then_inc(sm["of_ready"], 1)

                act.preload_act_table_set("natural_log_exp_and_others")
                act.sem_inc(sm["exp_done"], 1)
                act.sem_inc(sm["o_ready"], 1)
                act.wait_ge(sm["sel_ready"], 9)
                sequences(act, one)

            @block.vector
            def _(dve):
                def prepare(b):
                    for i in range(2):
                        for half, (table, out) in enumerate(((S.cos0, ta), (S.sin0, tb))):
                            dve.wait_ge(sm["proj_done"], b * 4 + 2 * i + half + 1)
                            at = 2 * half + i
                            dve.scalar_tensor_tensor(out=out[:, i, :], in0=t2[:, :], scalar=S.bq[:, at:at + 1], in1=table[:, :],
                                                     op0=ALU.add, op1=ALU.mult).then_inc(sm["rope_step"], 1)
                    dve.wait_ge(sm["rope_step"], b * 4 + 4)
                    dve.tensor_tensor(qk[:, :, :], ta[:, :, :], tb[:, :, :], ALU.add).then_inc(sm["q_ready"], 1)
                    dve.wait_ge(sm["q_ready"], b + 1)
                    dve.tensor_copy(parts[:, 0, :, :], qk[:, :, :]).then_inc(sm["parts_step"], 1)
                    dve.wait_ge(sm["parts_step"], b * 4 + 1)
                    dve.tensor_tensor(rest[:, :, :], qk[:, :, :], parts[:, 0, :, :], ALU.subtract).then_inc(sm["parts_step"], 1)
                    dve.wait_ge(sm["parts_step"], b * 4 + 2)
                    dve.tensor_copy(parts[:, 1, :, :], rest[:, :, :]).then_inc(sm["parts_step"], 1)
                    dve.wait_ge(sm["parts_step"], b * 4 + 3)
                    dve.tensor_tensor(parts[:, 2, :, :], rest[:, :, :], parts[:, 1, :, :], ALU.subtract).then_inc(sm["parts_step"], 1)

                def one(b, last):
                    dve.wait_ge(sm["v_done"], b + 1)
                    dve.tensor_tensor(vv[:, :, :, 0:HD0], t1[:, :].rearrange("p (c h d) -> p c h d", c=TT, h=H0),
                                      S.bv0[:, :].rearrange("p (h d) -> p h d", h=H0).unsqueeze(1).broadcast_to([P, TT, H0, HD0]),
                                      ALU.add).then_inc(sm["v_ready"], 1)
                    def maxima(h):
                        for c in (0, 2):
                            m = h * TT + c
                            dve.wait_ge(sm["score_done"], b * NS + m + 2)
                            dve.tensor_reduce(mx[:, h // HH, c:c + 2, h % HH], ring[:, m % 4:m % 4 + 2, :], AX_X, ALU.max,
                                              negate=True).then_inc(sm["max_ready"], 1)

                    def split_maxima(half):
                        dve.wait_ge(sm["maxt_done"], 2 * b + half + 1)
                        if half:
                            dve.wait_ge(sm["rows_ready"], (2 * b + 1) * 16 * NP)
                        k = b * 12 + 6 * half
                        dve.tensor_copy(mb[0:HH, :], t2[0:HH, :]).then_inc(sm["part_step"], 1)
                        dve.wait_ge(sm["part_step"], k + 1)
                        dve.tensor_tensor(rem[:, 0, :], t2[0:HH, :], mb[0:HH, :], ALU.subtract).then_inc(sm["part_step"], 1)
                        dve.wait_ge(sm["part_step"], k + 2)
                        dve.tensor_copy(mid[:, :], rem[:, 0, :]).then_inc(sm["part_step"], 1)
                        dve.wait_ge(sm["part_step"], k + 3)
                        dve.tensor_copy(mb[32:32 + HH, :], mid[:, :]).then_inc(sm["part_step"], 1)
                        dve.tensor_tensor(rem[:, 1, :], rem[:, 0, :], mid[:, :], ALU.subtract).then_inc(sm["part_step"], 1)
                        dve.wait_ge(sm["part_step"], k + 5)
                        dve.tensor_copy(mb[64:64 + HH, :], rem[:, 1, :]).then_inc(sm["part_step"], 1)

                    for h in range(H0):
                        maxima(h)
                        if h == HH + 2:
                            split_maxima(0)
                    split_maxima(1)
                    if not last:
                        prepare(b + 1)
                    for g in range(4):
                        dve.wait_ge(sm["ot_done"], b * 4 + g + 1)
                        t = t1[:, :].rearrange("p (c j m) -> p c j m", c=TT, j=GH)
                        dve.reciprocal(rc[:, :, :], t[:, :, :, HD0]).then_inc(sm["onorm_step"], 1)
                        dve.wait_ge(sm["onorm_step"], b * 8 + 2 * g + 2)
                        o = on[:, :, GH * HD0 * g:GH * HD0 * (g + 1)].rearrange("p c (j d) -> p c j d", j=GH)
                        dve.tensor_tensor(o, t[:, :, :, 0:HD0], rc[:, :, :].unsqueeze(3).broadcast_to([P, TT, GH, HD0]),
                                          ALU.mult).then_inc(sm["onorm_step"], 1)
                    dve.wait_ge(sm["y_done"], b + 1)
                    dve.tensor_scalar(tx[:, :], t2[:, :], S.bo0[:, 0:1], S.mod[:, 0, 2, bass.ds(b, 1)], ALU.add,
                                      ALU.mult).then_inc(sm["gated"], 1)
                    dve.wait_ge(sm["gated"], b + 1)
                    dve.tensor_tensor(S.xr[:, b, :], S.xr[:, b, :], tx[:, :], ALU.add).then_inc(sm["x_ready"], 1)

                dve.sem_inc(sm["onorm_step"], 1)
                dve.sem_inc(sm["x_ready"], 1)
                dve.memset(sel[:, :, :, :, :].rearrange("p x i h m -> p (x i h m)"), 0.0).then_inc(sm["sel_ready"], 1)
                dve.wait_ge(sm["sel_ready"], 1)
                heads = S.identb[:, :].rearrange("p (h d) -> p h d", h=H0).unsqueeze(2).broadcast_to([P, H0, NP, HD0])
                for i in range(NP):
                    for x in range(2):
                        block_rows = sel[:, x, i, :, :].rearrange("p h (a c d) -> p h a c d", a=NP, c=NP)
                        rows = block_rows[:, :, i, :, :] if x == 0 else block_rows[:, :, :, i, :]
                        dve.tensor_copy(rows, heads).then_inc(sm["sel_ready"], 1)
                dve.memset(qs[64:P, :, :, :].rearrange("p x h t -> p (x h t)"), 0.0).then_inc(sm["sel_ready"], 1)
                prepare(0)
                dve.wait_ge(sm["sel_ready"], 8)
                dve.memset(qs[MR:KM, 1, :, :].rearrange("p h t -> p (h t)"), 1.0).then_inc(sm["sel_ready"], 1)
                dve.wait_ge(sm["zeroed"], 2)
                sequences(dve, one)


def mix_stage(core, A):
    nc, S = core.nc, core
    loaded, mixed, step, done = core.sem("mix_loaded"), core.sem("mix_done"), core.sem("mix_step"), core.sem("mix_added")
    with ExitStack() as ctx:
        w = core.sb(ctx, "mix_w", [P, P])
        bias = core.sb(ctx, "mix_b", [P, 1])
        tmp = core.sb(ctx, "mix_tmp", [P, 4, T])
        pm = core.ps(ctx, "mix_ps", [P, 4, BANK])
        with nc.Block() as block:
            @block.sync
            def _(sp):
                sp.dma_start(w[:, :], A["L0_ffn_mix_w"]).then_inc(loaded, 16)
                sp.dma_start(bias[:, :], column(A["L0_ffn_mix_b"])).then_inc(loaded, 16)

            @block.tensor
            def _(pe):
                pe.wait_ge(loaded, 32)
                for b in range(B):
                    if b >= 4:
                        pe.wait_ge(step, b - 3)
                    pe.matmul(pm[:, b % 4, :], w[:, :], S.xa[:, b, PADW:], start=True, stop=True).then_inc(mixed, 1)

            @block.vector
            def _(dve):
                dve.wait_ge(loaded, 32)
                for b in range(B):
                    dve.wait_ge(mixed, b + 1)
                    dve.scalar_tensor_tensor(out=tmp[:, b % 4, :], in0=pm[:, b % 4, :], scalar=bias[:, 0:1],
                                             in1=S.xa[:, b, PADW:], op0=ALU.add, op1=ALU.add).then_inc(step, 1)
                    dve.wait_ge(step, b + 1)
                    dve.tensor_tensor(S.h[:, b, :], S.h[:, b, :], tmp[:, b % 4, :], ALU.add).then_inc(done, 1)


def router_stage(core, A, comb, b1t, b2t):
    nc, S = core.nc, core
    loaded = core.sem("rt_loaded")
    logits, biases, step = core.sem("rt_logits"), core.sem("rt_biases"), core.sem("rt_step")
    exp_done, turned, taken = core.sem("rt_exp"), core.sem("rt_turned"), core.sem("rt_taken")
    zeroed = core.sem("rt_zeroed")
    N = B * TT
    with ExitStack() as ctx:
        w = core.sb(ctx, "rt_w", [P, E0])
        b1 = core.sb(ctx, "rt_b1", [4 * E0, P])
        b2 = core.sb(ctx, "rt_b2", [E0, P])
        low = core.sb(ctx, "rt_lower", [P, E0 * E0])
        pr = core.sb(ctx, "rt_probs", [P, N, E0])
        mx, sm = core.sb(ctx, "rt_max", [P, N]), core.sb(ctx, "rt_sum", [P, N])
        gt, eq = core.sb(ctx, "rt_gt", [P, N, E0 * E0]), core.sb(ctx, "rt_eq", [P, N, E0 * E0])
        rank = core.sb(ctx, "rt_rank", [P, N, E0])
        part = core.sb(ctx, "rt_part", [P, 2, N, E0], BF16)
        parts = core.sb(ctx, "rt_parts", [P, N, 96])
        pl = core.ps(ctx, "rt_pl", [P, BANK])
        pb = core.ps(ctx, "rt_pb", [P, BANK])
        pt = core.ps(ctx, "rt_pt", [P, 4, BANK])
        with nc.Block() as block:
            @block.sync
            def _(sp):
                sp.dma_start(w[:, :], A["L0_ffn_router_w"]).then_inc(loaded, 16)
                sp.dma_start(b1[:, :], A["L0_ffn_b1"].rearrange("e (c p) -> (e c) p", p=P)).then_inc(loaded, 16)
                sp.dma_start(b2[:, :], A["L0_ffn_b2"]).then_inc(loaded, 16)
                sp.dma_start(low[:, :], A["lower"]).then_inc(loaded, 16)

            @block.tensor
            def _(pe):
                pe.wait_ge(loaded, 64)
                for n in range(N):
                    b, c = n // TT, n % TT
                    mm = pe.matmul(pl[:, E0 * n:E0 * n + E0], S.xa[:, b, PADW + P * c:PADW + P * c + P], w[:, :],
                                   start=True, stop=True)
                mm.then_inc(logits, 1)
                pe.transpose(pb[:, 0:32], b1[:, :], S.ident[0:32, 0:32])
                pe.transpose(pb[:, 32:40], b2[:, :], S.ident[0:8, 0:8]).then_inc(biases, 1)
                pe.wait_ge(step, 19)
                for b in range(B):
                    if b >= 4:
                        pe.wait_ge(taken, b - 3)
                    for c in range(TT):
                        tr = pe.transpose(pt[0:96, b % 4, P * c:P * c + P], parts[:, TT * b + c, :], S.ident[:, :])
                    tr.then_inc(turned, 1)

            @block.scalar
            def _(act):
                act.preload_act_table_set("natural_log_exp_and_others")
                act.wait_ge(step, 2)
                act.activation(pr[:, :, :], pr[:, :, :], ACT.Exp).then_inc(exp_done, 1)
                for b in range(B):
                    act.wait_ge(turned, b + 1)
                    act.activation(comb[:, b, :], pt[0:96, b % 4, :], ACT.Identity).then_inc(taken, 1)

            @block.gpsimd
            def _(pool):
                pool.memset(parts[:, :, :], 0.0).then_inc(zeroed, 1)

            @block.vector
            def _(dve):
                n = 0

                def ordered(ins):
                    nonlocal n
                    n += 1
                    ins.then_inc(step, 1)
                    dve.wait_ge(step, n)

                lg = pl[:, 0:N * E0].rearrange("p (n e) -> p n e", e=E0)

                def wide(ap):
                    return ap[:, :].unsqueeze(2).broadcast_to([P, N, E0])

                def pairs(ap):
                    return ap[:, :, :].rearrange("p n (e o) -> p n e o", e=E0)

                def by_expert():
                    return pr[:, :, :].unsqueeze(3).broadcast_to([P, N, E0, E0])

                def by_other():
                    return pr[:, :, :].unsqueeze(2).broadcast_to([P, N, E0, E0])

                dve.wait_ge(logits, 1)
                ordered(dve.tensor_reduce(mx[:, :], lg, AX_X, ALU.max))
                ordered(dve.tensor_tensor(pr[:, :, :], lg, wide(mx), ALU.subtract))
                dve.wait_ge(exp_done, 1)
                ordered(dve.tensor_reduce(sm[:, :], pr[:, :, :], AX_X, ALU.add))
                ordered(dve.reciprocal(sm[:, :], sm[:, :]))
                ordered(dve.tensor_tensor(pr[:, :, :], pr[:, :, :], wide(sm), ALU.mult))
                ordered(dve.tensor_tensor(pairs(gt), by_other(), by_expert(), ALU.is_gt))
                ordered(dve.tensor_tensor(pairs(eq), by_other(), by_expert(), ALU.is_equal))
                dve.wait_ge(loaded, 64)
                ordered(dve.tensor_tensor(eq[:, :, :], eq[:, :, :], low[:, :].unsqueeze(1).broadcast_to([P, N, E0 * E0]),
                                          ALU.mult))
                ordered(dve.tensor_tensor(gt[:, :, :], gt[:, :, :], eq[:, :, :], ALU.add))
                ordered(dve.tensor_reduce(rank[:, :, :], pairs(gt), AX_X, ALU.add))
                ordered(dve.tensor_scalar(rank[:, :, :], rank[:, :, :], 2.0, None, ALU.is_lt))
                ordered(dve.tensor_tensor(pr[:, :, :], pr[:, :, :], rank[:, :, :], ALU.mult))
                dve.wait_ge(zeroed, 1)
                ordered(dve.tensor_copy(part[:, 0, :, :], pr[:, :, :]))
                ordered(dve.tensor_copy(parts[:, :, 0:E0], part[:, 0, :, :]))
                ordered(dve.tensor_tensor(pr[:, :, :], pr[:, :, :], part[:, 0, :, :], ALU.subtract))
                ordered(dve.tensor_copy(part[:, 1, :, :], pr[:, :, :]))
                ordered(dve.tensor_copy(parts[:, :, 32:32 + E0], part[:, 1, :, :]))
                ordered(dve.tensor_tensor(pr[:, :, :], pr[:, :, :], part[:, 1, :, :], ALU.subtract))
                ordered(dve.tensor_copy(parts[:, :, 64:64 + E0], pr[:, :, :]))
                dve.wait_ge(biases, 1)
                dve.tensor_copy(b1t[:, :], pb[:, 0:32])
                dve.tensor_copy(b2t[:, :], pb[:, 32:40])


def experts_stage(core, comb, w1, w2, b1t, b2t):
    nc, S = core.nc, core
    FC = F0 // P
    NH = E0 * FC
    sm = {n: core.sem("ex_" + n) for n in "h_done h_ready y_done c_done c_ready y_ready acc_ready x_ready".split()}
    with ExitStack() as ctx:
        hs = core.sb(ctx, "ex_hs", [P, 2 * FC, T])
        cs = core.sb(ctx, "ex_cs", [P, 2, T])
        ys = core.sb(ctx, "ex_ys", [P, 2, T])
        acc = core.sb(ctx, "ex_acc", [P, T])
        ph = core.ps(ctx, "ex_ph", [P, 4, BANK])
        py = core.ps(ctx, "ex_py", [P, 2, BANK])
        pc = core.ps(ctx, "ex_pc", [P, 2, BANK])
        with nc.Block() as block:
            @block.tensor
            def _(pe):
                pe.wait_ge(S.experts_loaded, 32)
                with pe.Fori(0, B) as b:
                    def up(e):
                        for f in range(FC):
                            n = e * FC + f
                            pe.wait_ge(sm["h_ready"], b * NH + n + 1)
                            pe.matmul(ph[:, n % 4, :], w1[:, e, P * f:P * f + P], S.xa[:, b, PADW:], start=True,
                                      stop=True).then_inc(sm["h_done"], 1)
                        pe.wait_ge(sm["c_ready"], b * E0 + e + 1)
                        pe.matmul(pc[:, e % 2, :], S.pick[0:96, e, :], comb[:, b, :], start=True,
                                  stop=True).then_inc(sm["c_done"], 1)

                    def down(e):
                        pe.wait_ge(sm["y_ready"], b * E0 + e + 1)
                        for f in range(FC):
                            n = e * FC + f
                            pe.wait_ge(sm["h_ready"], b * NH + n + 5)
                            mm = pe.matmul(py[:, e % 2, :], w2[:, e, f, :], hs[:, n % (2 * FC), :], start=(f == 0),
                                           stop=(f == FC - 1))
                        mm.then_inc(sm["y_done"], 1)

                    for e in range(E0 + 1):
                        if e < E0:
                            up(e)
                        if e:
                            down(e - 1)

            @block.scalar
            def _(act):
                act.preload_act_table_set("silu_and_others")
                act.sem_inc(sm["h_ready"], 4)
                act.sem_inc(sm["c_ready"], 2)
                with act.Fori(0, B) as b:
                    for e in range(E0):
                        act.wait_ge(sm["y_done"], b * E0 + e + 1)
                        for f in range(FC):
                            n = e * FC + f
                            act.wait_ge(sm["h_done"], b * NH + n + 1)
                            act.activation(hs[:, n % (2 * FC), :], ph[:, n % 4, :], ACT.Silu,
                                           bias=b1t[:, n:n + 1]).then_inc(sm["h_ready"], 1)
                        act.wait_ge(sm["c_done"], b * E0 + e + 1)
                        act.wait_ge(sm["y_ready"], b * E0 + e + 1)
                        act.activation(cs[:, e % 2, :], pc[:, e % 2, :], ACT.Identity).then_inc(sm["c_ready"], 1)

            @block.vector
            def _(dve):
                dve.sem_inc(sm["y_ready"], 2)
                dve.sem_inc(sm["y_done"], 2)
                dve.sem_inc(sm["x_ready"], 1)
                with dve.Fori(0, B) as b:
                    for e in range(E0):
                        dve.wait_ge(sm["y_done"], b * E0 + e + 3)
                        dve.wait_ge(sm["c_ready"], b * E0 + e + 3)
                        dve.wait_ge(sm["acc_ready"], b * E0 + e + 1)
                        dve.scalar_tensor_tensor(out=ys[:, e % 2, :], in0=py[:, e % 2, :], scalar=b2t[:, e:e + 1],
                                                 in1=cs[:, e % 2, :], op0=ALU.add, op1=ALU.mult).then_inc(sm["y_ready"], 1)
                    dve.wait_ge(sm["acc_ready"], b * E0 + E0 + 2)
                    dve.scalar_tensor_tensor(out=S.xr[:, b, :], in0=acc[:, :], scalar=S.mod[:, 0, 5, bass.ds(b, 1)],
                                             in1=S.xr[:, b, :], op0=ALU.mult, op1=ALU.add).then_inc(sm["x_ready"], 1)

            @block.gpsimd
            def _(pool):
                pool.sem_inc(sm["acc_ready"], 2)
                with pool.Fori(0, B) as b:
                    pool.wait_ge(sm["x_ready"], b + 1)
                    for e in range(E0):
                        pool.wait_ge(sm["y_ready"], b * E0 + e + 3)
                        if e:
                            pool.wait_ge(sm["acc_ready"], b * E0 + e + 2)
                        pool.tensor_tensor(acc[:, :], acc[:, :] if e else S.h[:, b, :], ys[:, e % 2, :],
                                           ALU.add).then_inc(sm["acc_ready"], 1)


def ffn0(core, A, C):
    nc, S = core.nc, core
    with ExitStack() as ctx:
        w1 = core.sb(ctx, "moe_w1", [P, E0, F0])
        w2 = core.sb(ctx, "moe_w2", [P, E0, F0 // P, P])
        comb = core.sb(ctx, "moe_comb", [96, B, T], BF16)
        b1t, b2t = core.sb(ctx, "moe_b1", [P, 32]), core.sb(ctx, "moe_b2", [P, 8])
        gb = core.sb(ctx, "moe_norms", [P, 4])
        S.experts_loaded, gains = core.sem("experts_loaded"), core.sem("gains_loaded")
        with nc.Block() as block:
            @block.sync
            def _(sp):
                for i, n in enumerate(("g1", "be1", "g2", "be2")):
                    sp.dma_start(gb[:, i:i + 1], column(A["L0_ffn_" + n])).then_inc(gains, 16)
                sp.dma_start(w1[:, :, :], A["L0_ffn_w1"].rearrange("e d f -> d e f")).then_inc(S.experts_loaded, 16)
                sp.dma_start(w2[:, :, :, :], A["L0_ffn_w2"].rearrange("e (c p) d -> p e c d", p=P)).then_inc(S.experts_loaded, 16)
                sp.wait_ge(gains, 64)
        norm_stage(core, lambda b: S.xr[:, b, :], lambda b: S.h[:, b, :],
                   lambda b: S.mod[:, 0, 4, b:b + 1], lambda b: S.mod[:, 0, 3, b:b + 1])(B)
        norm_stage(core, lambda b: S.h[:, b, :], lambda b: S.xa[:, b, PADW:], lambda b: gb[:, 0:1], lambda b: gb[:, 1:2])(2 * B)
        mix_stage(core, A)
        norm_stage(core, lambda b: S.h[:, b, :], lambda b: S.xa[:, b, PADW:], lambda b: gb[:, 2:3], lambda b: gb[:, 3:4])(3 * B)
        router_stage(core, {**A, "lower": C["lower"]}, comb, b1t, b2t)
        experts_stage(core, comb, w1, w2, b1t, b2t)


def attention1(core, A, C):
    nc, S = core.nc, core
    sm = {n: core.sem("a1_" + n) for n in ("loaded loaded_cast trig_step trig_ready sin_done hs_ready proj_done act_ready dve_ready s_done v_done "
                                           "max_ready sub_ready exp_done sum_ready rsum_ready norm_ready t_done t_ready "
                                           "v_ready o_done o_ready y_done gated x_ready start setup").split()}
    NB = T // TB
    NG = NB // 4
    SCALE = float(HD1) ** -0.5
    TWO_PI = 2 * np.pi
    TP_HI = float(np.float32(6.28125))
    TP_LO = float(TWO_PI - 6.28125)
    MAGIC = 1.5 * 2.0 ** 23
    with ExitStack() as ctx:
        wq, wk, wv = (core.sb(ctx, "a1_w" + n, [P, H1 * HD1]) for n in "qkv")
        wo = core.sb(ctx, "a1_wo", [P, H1, P])
        bqk = core.sb(ctx, "a1_bqk", [P, 2, H1])
        bo = core.sb(ctx, "a1_bo", [P, 1])
        bv = core.sb(ctx, "a1_bv", [P, HD1])
        mask = core.sb(ctx, "a1_mask", [P, P], BF16)
        mask4 = core.sb(ctx, "a1_mask4", [P, 4, P], BF16)
        ph = core.sb(ctx, "a1_phase", [P, H1])
        rnd = core.sb(ctx, "a1_round", [P, 2, H1])
        red = core.sb(ctx, "a1_reduced", [P, 2, H1])
        trig = core.sb(ctx, "a1_trig", [P, 2, H1])
        tbias = core.sb(ctx, "a1_tbias", [P, 2, H1])
        hs = core.sb(ctx, "a1_hs", [P, T])
        qp = core.sb(ctx, "a1_q", [P, 2, NB, H1, TB])
        kp = core.sb(ctx, "a1_k", [P, 2, NB, H1, TB])
        vs = core.sb(ctx, "a1_v", [P, 2, 4, HD1])
        pr = core.sb(ctx, "a1_p", [P, 2, 4, P])
        pn = core.sb(ctx, "a1_pn", [P, 2, 4, P])
        at = core.sb(ctx, "a1_pt", [P, 2, 4, P])
        mx, su, rs = (core.sb(ctx, "a1_" + n, [P, 2, 4]) for n in ("max", "sum", "rsum"))
        ot = core.sb(ctx, "a1_o", [P, H1, T])
        tx = core.sb(ctx, "a1_tx", [P, T])
        ring = core.ps(ctx, "a1_ring", [P, 4, BANK])
        ps = core.ps(ctx, "a1_s", [P, 2, BANK])
        po = core.ps(ctx, "a1_po", [P, BANK])
        py = core.ps(ctx, "a1_py", [P, BANK])
        with nc.Block() as block:
            @block.sync
            def _(sp):
                for n, ap in (("L1_attn_Wq", wq), ("L1_attn_Wk", wk), ("L1_attn_Wv", wv)):
                    sp.dma_start(ap[:, :], A[n]).then_inc(sm["loaded"], 16)
                sp.dma_start(wo[:, :, :], A["L1_attn_Wo"].rearrange("(h d) o -> d h o", d=HD1)).then_inc(sm["loaded"], 16)
                with nc.allow_non_contiguous_dma("small vectors turned onto the partitions"):
                    sp.dma_start(bqk[:, 0, :], A["L1_attn_bq"].rearrange("(h d) -> d h", d=HD1)).then_inc(sm["loaded"], 16)
                    sp.dma_start(bqk[:, 1, :], A["L1_attn_bk"].rearrange("(h d) -> d h", d=HD1)).then_inc(sm["loaded"], 16)
                    sp.dma_start(ph[:, :], A["L1_attn_phase"].rearrange("h d -> d h")).then_inc(sm["loaded"], 16)
                sp.dma_start(bo[:, :], column(A["L1_attn_bo"])).then_inc(sm["loaded"], 16)
                for g in range(H1):
                    sp.dma_start(bv[TB * g:TB * g + TB, :],
                                 A["L1_attn_bv"][HD1 * g:HD1 * g + HD1].partition_broadcast(TB)).then_inc(sm["loaded"], 16)

            NLOAD = 16 * 12

            @block.gpsimd
            def _(pool):
                pool.dma_start(mask[:, :], C["mask1"]).then_inc(sm["loaded_cast"], 16)
                pool.wait_ge(sm["loaded_cast"], 16)
                with pool.Fori(0, B) as b:
                    pool.wait_ge(sm["v_done"], b * NG + 1)
                    pool.tensor_copy(hs[:, :], S.h[:, b, :]).then_inc(sm["hs_ready"], 1)
                    for g in range(NG):
                        pool.wait_ge(sm["rsum_ready"], b * NG + g + 1)
                        pool.wait_ge(sm["t_done"], b * NG + g + 1)
                        pool.tensor_tensor(pn[:, g % 2, :, :], pr[:, g % 2, :, :],
                                           rs[:, g % 2, :].unsqueeze(2).broadcast_to([P, 4, P]),
                                           ALU.mult).then_inc(sm["norm_ready"], 1)

            @block.tensor
            def _(pe):
                pe.wait_ge(sm["loaded"], NLOAD)
                pe.wait_ge(sm["setup"], 1)
                pe.sem_inc(sm["v_done"], 1)
                pe.sem_inc(sm["t_done"], 2)
                with pe.Fori(0, B) as b:
                    pe.wait_ge(sm["hs_ready"], b + 1)
                    for n in range(2 * H1):
                        h, k = n // 2, n % 2
                        w = wk if k else wq
                        if h >= 2:
                            pe.wait_ge(sm["dve_ready" if k else "act_ready"], b * 2 * H1 + 2 * (h - 1))
                        elif k:
                            pe.wait_ge(sm["t_ready"], b * NG + 1)
                        else:
                            pe.wait_ge(sm["v_ready"], b * NG + 1)
                        pe.matmul(ring[:, 2 * k + h % 2, :], w[:, HD1 * h:HD1 * h + HD1], hs[:, :], start=True,
                                  stop=True).then_inc(sm["proj_done"], 1)

                    def scores(g):
                        pe.wait_ge(sm["sub_ready"], b * NG + g + 1)
                        if g == 0:
                            pe.wait_ge(sm["act_ready"], b * 2 * H1 + 2 * H1)
                            pe.wait_ge(sm["dve_ready"], b * 2 * H1 + 2 * H1)
                        pe.matmul(ps[:, g % 2, :], S.identb[:, :], mask4[:, :, :].rearrange("p n m -> p (n m)"), start=True,
                                  stop=False, skip_group_check=True)
                        for i in range(4):
                            for part in range(2):
                                mm = pe.matmul(ps[:, g % 2, P * i:P * i + P],
                                               qp[:, part, 4 * g + i, :, :].rearrange("p h t -> p (h t)"),
                                               kp[:, part, 4 * g + i, :, :].rearrange("p h t -> p (h t)"),
                                               start=False, stop=(part == 1), skip_group_check=True)
                        mm.then_inc(sm["s_done"], 1)
                        if g >= 2:
                            pe.wait_ge(sm["v_ready"], b * NG + g)
                        for h in range(H1):
                            for i in range(4):
                                at_ = TB * (4 * g + i)
                                mm = pe.matmul(ring[TB * h:TB * h + TB, g % 2, P * i:P * i + P], hs[:, at_:at_ + TB],
                                               wv[:, HD1 * h:HD1 * h + HD1], start=True, stop=True)
                        mm.then_inc(sm["v_done"], 1)

                    def turn(g):
                        pe.wait_ge(sm["norm_ready"], b * NG + g + 3)
                        if g >= 2:
                            pe.wait_ge(sm["t_ready"], b * NG + g)
                        for i in range(4):
                            tr = pe.transpose(ring[:, 2 + g % 2, P * i:P * i + P], pn[:, g % 2, i, :], S.ident[:, :])
                        tr.then_inc(sm["t_done"], 1)

                    def weighted(g):
                        pe.wait_ge(sm["t_ready"], b * NG + g + 2)
                        pe.wait_ge(sm["v_ready"], b * NG + g + 2)
                        pe.wait_ge(sm["o_ready"], b * NG + g + 1)
                        for i in range(4):
                            mm = pe.matmul(po[:, P * i:P * i + P], vs[:, g % 2, i, :], at[:, g % 2, i, :], start=True, stop=True)
                        mm.then_inc(sm["o_done"], 1)

                    for s in range(NG + 2):
                        if s < NG:
                            scores(s)
                        if 1 <= s <= NG:
                            turn(s - 1)
                        if s >= 2:
                            weighted(s - 2)
                    pe.wait_ge(sm["o_ready"], b * NG + NG + 1)
                    pe.wait_ge(sm["x_ready"], b + 1)
                    for j in range(H1):
                        mm = pe.matmul(py[:, :], wo[:, j, :], ot[:, :, :].rearrange("p h (r j) -> p h r j", j=H1)[:, :, :, j],
                                       start=(j == 0), stop=(j == H1 - 1))
                    mm.then_inc(sm["y_done"], 1)

            @block.scalar
            def _(act):
                act.sem_inc(sm["t_ready"], 1)
                act.wait_ge(sm["trig_ready"], 1)
                act.activation(trig[:, :, :], red[:, :, :], ACT.Sin).then_inc(sm["sin_done"], 1)
                act.wait_ge(sm["setup"], 1)
                act.preload_act_table_set("natural_log_exp_and_others")
                with act.Fori(0, B) as b:
                    for h in range(H1):
                        act.wait_ge(sm["proj_done"], b * 2 * H1 + 2 * h + 1)
                        if h == 0:
                            act.wait_ge(sm["s_done"], b * NG + 1)
                        for part in range(2):
                            act.activation(qp[:, part, :, h, :], ring[:, h % 2, :].rearrange("p (n t) -> p n t", t=TB),
                                           ACT.Identity, bias=tbias[:, part, h:h + 1],
                                           scale=trig[:, part, h:h + 1]).then_inc(sm["act_ready"], 1)
                    for s in range(NG + 1):
                        if s < NG:
                            act.wait_ge(sm["sub_ready"], b * NG + s + 3)
                            act.activation(pr[:, s % 2, :, :], pr[:, s % 2, :, :], ACT.Exp, scale=SCALE).then_inc(sm["exp_done"], 1)
                        if s:
                            g = s - 1
                            act.wait_ge(sm["t_done"], b * NG + g + 3)
                            act.wait_ge(sm["o_done"], b * NG + g + 1)
                            act.activation(at[:, g % 2, :, :].rearrange("p n m -> p (n m)"), ring[:, 2 + g % 2, :],
                                           ACT.Identity).then_inc(sm["t_ready"], 1)

            @block.vector
            def _(dve):
                dve.sem_inc(sm["v_ready"], 1)
                dve.sem_inc(sm["sub_ready"], 2)
                dve.sem_inc(sm["o_ready"], 1)
                dve.sem_inc(sm["x_ready"], 1)
                dve.sem_inc(sm["s_done"], 1)
                dve.sem_inc(sm["o_done"], 2)
                dve.sem_inc(sm["norm_ready"], 2)
                dve.sem_inc(sm["y_done"], 1)
                dve.wait_ge(sm["loaded"], NLOAD)
                n = 0

                def ordered(ins):
                    nonlocal n
                    n += 1
                    ins.then_inc(sm["trig_step"], 1)
                    dve.wait_ge(sm["trig_step"], n)

                for part in range(2):
                    ordered(dve.tensor_scalar(rnd[:, part, :], ph[:, :], 1.0 / TWO_PI, 0.25 if part == 0 else 0.0,
                                              ALU.mult, ALU.add))
                    ordered(dve.tensor_scalar(rnd[:, part, :], rnd[:, part, :], MAGIC, None, ALU.add))
                    ordered(dve.tensor_scalar(rnd[:, part, :], rnd[:, part, :], MAGIC, None, ALU.subtract))
                    ordered(dve.scalar_tensor_tensor(out=red[:, part, :], in0=rnd[:, part, :], scalar=-TP_HI, in1=ph[:, :],
                                                     op0=ALU.mult, op1=ALU.add))
                    ordered(dve.scalar_tensor_tensor(out=red[:, part, :], in0=rnd[:, part, :], scalar=-TP_LO,
                                                     in1=red[:, part, :], op0=ALU.mult, op1=ALU.add))
                    if part == 0:
                        ordered(dve.tensor_scalar(red[:, part, :], red[:, part, :], float(np.pi / 2), None, ALU.add))
                    ordered(dve.tensor_scalar(red[:, part, :], red[:, part, :], 3.1415925, -3.1415925, ALU.min, ALU.max))
                dve.sem_inc(sm["trig_ready"], 1)
                dve.wait_ge(sm["sin_done"], 1)
                for part in range(2):
                    ordered(dve.tensor_tensor(tbias[:, part, :], trig[:, part, :], bqk[:, 0, :], ALU.mult))
                dve.wait_ge(sm["loaded_cast"], 16)
                dve.tensor_copy(mask4[:, :, :], mask[:, :].unsqueeze(1).broadcast_to([P, 4, P])).then_inc(sm["setup"], 1)
                with dve.Fori(0, B) as b:
                    for h in range(H1):
                        dve.wait_ge(sm["proj_done"], b * 2 * H1 + 2 * h + 2)
                        for part in range(2):
                            dve.tensor_scalar(kp[:, part, :, h, :], ring[:, 2 + h % 2, :].rearrange("p (n t) -> p n t", t=TB),
                                              bqk[:, 1, h:h + 1], trig[:, part, h:h + 1], ALU.add,
                                              ALU.mult).then_inc(sm["dve_ready"], 1)
                    for s in range(NG + 2):
                        if s < NG:
                            g, i = s, s % 2
                            dve.wait_ge(sm["s_done"], b * NG + g + 2)
                            S4 = ps[:, i, :].rearrange("p (n m) -> p n m", m=P)
                            dve.tensor_reduce(mx[:, i, :], S4, AX_X, ALU.max).then_inc(sm["max_ready"], 1)
                            dve.wait_ge(sm["max_ready"], b * NG + g + 1)
                            dve.wait_ge(sm["norm_ready"], b * NG + g + 1)
                            dve.tensor_tensor(pr[:, i, :, :], S4, mx[:, i, :].unsqueeze(2).broadcast_to([P, 4, P]),
                                              ALU.subtract).then_inc(sm["sub_ready"], 1)
                            dve.wait_ge(sm["v_done"], b * NG + g + 2)
                            if g >= 2:
                                dve.wait_ge(sm["o_done"], b * NG + g + 1)
                            dve.tensor_tensor(vs[:, i, :, :], ring[:, i, :].rearrange("p (n m) -> p n m", m=HD1),
                                              bv[:, :].unsqueeze(1).broadcast_to([P, 4, HD1]), ALU.add).then_inc(sm["v_ready"], 1)
                            dve.wait_ge(sm["exp_done"], b * NG + g + 1)
                            dve.tensor_reduce(su[:, i, :], pr[:, i, :, :], AX_X, ALU.add).then_inc(sm["sum_ready"], 1)
                            dve.wait_ge(sm["sum_ready"], b * NG + g + 1)
                            dve.reciprocal(rs[:, i, :], su[:, i, :]).then_inc(sm["rsum_ready"], 1)
                        if s >= 2:
                            g = s - 2
                            dve.wait_ge(sm["o_done"], b * NG + g + 3)
                            if g == 0:
                                dve.wait_ge(sm["y_done"], b + 1)
                            dve.tensor_copy(ot[:, :, P * g:P * g + P].rearrange("p h (n t) -> p n h t", t=TB),
                                            po[:, :].rearrange("p (n h t) -> p n h t", n=4, h=H1)).then_inc(sm["o_ready"], 1)
                    dve.wait_ge(sm["y_done"], b + 2)
                    dve.tensor_scalar(tx[:, :], py[:, :], bo[:, 0:1], S.mod[:, 1, 2, bass.ds(b, 1)], ALU.add,
                                      ALU.mult).then_inc(sm["gated"], 1)
                    dve.wait_ge(sm["gated"], b + 1)
                    dve.tensor_tensor(S.xr[:, b, :], S.xr[:, b, :], tx[:, :], ALU.add).then_inc(sm["x_ready"], 1)


NPAIR = H2 // 2
NT = B * TT
NW = P // WIN


class LocalAttention:

    NAMES = ("proj_done sq_ready ss_ready ssmax_ready ln_step rn_ready cos_ready sin_ready add_ready qkn_ready "
             "turn_done q_taken k_taken s_done max_ready sub_ready exp_ready sum_ready rsum_ready pn_ready "
             "v_done v_taken pt_done pt_taken o_done o_taken y_done x_ready table_step table_ready").split()

    def __init__(self, core, ctx):
        self.core = core
        self.sm = {n: core.sem("la_" + n) for n in self.NAMES}
        self.xs_ready = [core.sem("la_xs%d_ready" % i) for i in range(TT)]
        sb = lambda name, shape, dt=F32: core.sb(ctx, "la_" + name, shape, dt)
        self.wqkv = sb("wqkv", [P, 3 * INNER])
        self.wo = sb("wo", [P, NPAIR, P])
        self.qks = sb("qks", [P, 2, HD2])
        self.rope = sb("rope", [P, 2, TT, 2, HD2])
        self.cs = sb("cs", [P, 2, TT, 2, HD2])
        self.maskf = sb("maskf", [P, 2, 2 * WIN], BF16)
        self.mask = sb("mask", [P, 2, NPAIR, 2 * WIN], BF16)
        self.xs = sb("xs", [P, 4, P + WIN])
        self.work = sb("work", [P, 3, 2, INNER])
        self.sq, self.t1, self.t2 = (self.work[:, i, :, :] for i in range(3))
        self.ss = sb("ss", [P, 2, H2])
        self.rn = sb("rn", [P, 2, H2])
        self.qkn = sb("qkn", [P, 2, INNER])
        self.kt = sb("kt", [P, 2, NPAIR, P + WIN])
        self.qb = sb("qb", [P, NPAIR, NW, 2 * WIN])
        self.pr = sb("pr", [P, 2, NPAIR, 2 * WIN])
        self.pn = sb("pn", [P, 2, NPAIR, 2 * WIN])
        self.mx, self.su, self.rs = (sb(n, [P, 2, NPAIR]) for n in ("max", "sum", "rsum"))
        self.pb = sb("pb", [P, 2, NPAIR // 2, 4, 2, WIN])
        self.vs = sb("vs", [P, NW, NPAIR // 2, P])
        self.os = sb("os", [P, NPAIR, P])

    def setup(self, A, C):
        nc, S, sm = self.core.nc, self.core, self.sm
        loaded, cast, ready = S.sem("la_tables"), S.sem("la_masks"), S.sem("la_zeroed")
        with nc.Block() as block:
            @block.sync
            def _(sp):
                for i, n in enumerate(("cos2", "sin2")):
                    sp.dma_start(self.rope[:, i, :, :, :].rearrange("p t k d -> p (t k d)"), C[n]).then_inc(loaded, 16)
                sp.wait_ge(loaded, 32)

            @block.gpsimd
            def _(pool):
                pool.dma_start(self.maskf[:, :, :].rearrange("p n m -> p (n m)"), C["mask2"]).then_inc(cast, 16)
                pool.memset(self.qb[:, :, :, :].rearrange("p a b c -> p (a b c)"), 0.0)
                pool.memset(self.pb[:, :, :, :, :, :].rearrange("p a b c d e -> p (a b c d e)"), 0.0)
                pool.memset(self.kt[:, 0, :, 0:WIN], 0.0)
                pool.wait_ge(cast, 16)

            @block.vector
            def _(dve):
                dve.wait_ge(cast, 16)
                dve.tensor_copy(self.mask[:, :, :, :], self.maskf[:, :, :].unsqueeze(2).broadcast_to([P, 2, NPAIR, 2 * WIN])).then_inc(ready, 1)
                for n in ("qkn_ready", "cos_ready", "o_taken", "add_ready"):
                    dve.sem_inc(sm[n], 2)
                for n in ("proj_done", "s_done", "pt_done", "o_done", "y_done", "pt_taken", "x_ready", "sin_ready", "ssmax_ready",
                          "rn_ready", "pn_ready", "v_taken", "turn_done"):
                    dve.sem_inc(sm[n], 4)

    def layer(self, layer, weights_count, src, dst, A):
        nc, S, sm = self.core.nc, self.core, self.sm
        me = self

        def G(n):
            return layer * NT + n

        def steps(eng, before, step, after):
            before()
            with eng.Fori(0, B - 1) as b:
                for i in range(TT):
                    step(b * TT + i, b, i, True, True, True, True)
            for i in range(TT):
                step((B - 1) * TT + i, B - 1, i, False, i < TT - 3, i < TT - 2, i < TT - 1)
            after()

        with ExitStack() as ctx:
            pa = S.ps(ctx, "la_pa", [P, 4, BANK])
            ring = S.ps(ctx, "la_ring", [P, 4, BANK])
            with nc.Block() as block:
                @block.tensor
                def _(pe):
                    def project(n, b, i, k):
                        if k == 0:
                            pe.wait_ge(me.xs_ready[i], 32 * (layer * B + b) + 32)
                            pe.wait_ge(sm["x_ready"], G(n) + 1)
                        pe.wait_ge(sm["sin_ready"], 2 * G(n - 1) + k + 1 + 4)
                        for half in range(2):
                            at = INNER * k + BANK * half
                            mm = pe.matmul(pa[:, 2 * k + half, :], me.xs[:, i, WIN:], me.wqkv[:, at:at + BANK], start=True, stop=True)
                        mm.then_inc(sm["proj_done"], 1)

                    def turn(n, steady):
                        for u in range(4):
                            if u % 2 == 0:
                                pe.wait_ge(sm["qkn_ready"], 2 * G(n) + u // 2 + 1 + 2)
                            if steady:
                                if u < 2:
                                    pe.wait_ge(sm["sub_ready"], 2 * G(n - 1) + u + 1)
                                    pe.wait_ge(sm["o_taken"], 2 * (G(n) - 2) + u + 1 + 2)
                                elif u == 2:
                                    pe.wait_ge(sm["pt_taken"], 4 * (G(n) - 2) + 4 + 4)
                            for j in range(4):
                                at = (u % 2) * BANK + P * j
                                tr = pe.transpose(ring[:, u, P * j:P * j + P], me.qkn[:, u // 2, at:at + P], S.ident[:, :])
                            tr.then_inc(sm["turn_done"], 1)

                    def score(n, i, half):
                        s = i % 2
                        for u in half:
                            pe.wait_ge(sm["q_taken"], 4 * G(n) + 4)
                            pe.wait_ge(sm["k_taken"], 2 * G(n) + 2)
                            first = 1 if (i == 0 and u == 0) else 0
                            pe.matmul(ring[:, u, :], S.identb[:, :], me.mask[:, first, :, :].rearrange("p n m -> p (n m)"),
                                      start=True, stop=False, skip_group_check=True)
                            for w in (2 * u, 2 * u + 1):
                                r = 64 * (w % 2)
                                for p in range(NPAIR):
                                    mm = pe.matmul(ring[r:r + 64, u, 64 * p:64 * p + 64], me.qb[:, p, w, :],
                                                   me.kt[:, s, p, WIN * w:WIN * w + 64], start=False, stop=True,
                                                   skip_group_check=True)
                            mm.then_inc(sm["s_done"], 1)

                    def values(n, i, follows, windows):
                        wv = me.wqkv[:, 2 * INNER:3 * INNER].rearrange("p (j r m) -> p j r m", r=2, m=P)
                        for w in windows:
                            if w < 2:
                                if follows:
                                    pe.wait_ge(sm["k_taken"], 2 * G(n + 1) + 1 + w)
                                else:
                                    pe.wait_ge(sm["pt_taken"], 4 * G(n - 1) + 4 + 4)
                            else:
                                pe.wait_ge(sm["v_taken"], 4 * G(n) + w - 1 + 4)
                            for r in range(2):
                                mm = pe.matmul(ring[64 * r:64 * r + 64, 2 + w % 2, :], me.xs[:, i, WIN * w:WIN * w + 64],
                                               wv[:, :, r, :], start=True, stop=True)
                            mm.then_inc(sm["v_done"], 1)

                    def turn_weights(n):
                        for u in range(2):
                            pe.wait_ge(sm["v_taken"], 4 * G(n) + 3 + u + 4)
                            pe.wait_ge(sm["pn_ready"], 2 * G(n) + u + 1 + 4)
                            for j in range(NPAIR // 2):
                                tr = pe.transpose(ring[:, 2 + u, P * j:P * j + P],
                                                  me.pn[:, u, 2 * j:2 * j + 2, :].rearrange("p a k -> p (a k)"), S.ident[:, :])
                            tr.then_inc(sm["pt_done"], 1)

                    def weigh(n, follows, more3):
                        pe.wait_ge(sm["pt_taken"], 4 * G(n) + 4 + 4)
                        for half in range(2):
                            if follows:
                                pe.wait_ge(sm["sub_ready"], 2 * G(n + 1) + half + 1)
                            for h in range(2):
                                for j in (2 * half, 2 * half + 1):
                                    for w in range(NW):
                                        o = ring[64 * h:64 * h + 64, half, :].rearrange("p (a r t) -> p a r t", a=2, r=2)
                                        mm = pe.matmul(o[:, j % 2, :, WIN * w:WIN * w + WIN], me.vs[:, w, j, 64 * h:64 * h + 64],
                                                       me.pb[:, w // 2, j, 2 * (w % 2) + h, :, :], start=True, stop=True)
                            mm.then_inc(sm["o_done"], 1)
                        if more3:
                            pe.wait_ge(sm["sin_ready"], 2 * G(n + 3) + 1 + 4)
                        else:
                            pe.wait_ge(sm["x_ready"], G(n) + 4)
                        for p in range(NPAIR):
                            if p % 4 == 0:
                                pe.wait_ge(sm["o_taken"], 2 * G(n) + p // 4 + 1 + 2)
                            mm = pe.matmul(pa[:, 0, 0:P], me.wo[:, p, :], me.os[:, p, :], start=(p == 0), stop=(p == NPAIR - 1))
                        mm.then_inc(sm["y_done"], 1)

                    def before():
                        pe.wait_ge(S.weights_a, weights_count)
                        for n in range(3):
                            project(n, 0, n, 0)
                            project(n, 0, n, 1)
                            if n == 1:
                                turn(0, False)
                        score(0, 0, (0, 1))

                    def step(n, b, i, more4, more3, more2, more1):
                        ahead = (n + 3, b + 1 if i + 3 >= TT else b, (i + 3) % TT)
                        if more1:
                            turn(n + 1, True)
                        if more3:
                            project(*ahead, 0)
                        values(n, i, more1, (0, 1))
                        if more1:
                            score(n + 1, (i + 1) % TT, (0,))
                        values(n, i, more1, (2, 3))
                        if more1:
                            score(n + 1, (i + 1) % TT, (1,))
                        turn_weights(n)
                        if more3:
                            project(*ahead, 1)
                        weigh(n, more1, more3)

                    steps(pe, before, step, lambda: None)

                @block.sync
                def _(sp):
                    def shift(b, i):
                        for half in range(2):
                            r, at = slice(64 * half, 64 * half + 64), P * i + 1 - half
                            sp.dma_start(me.xs[r, i, :], src[r, b, at:at + P + WIN]).then_inc(me.xs_ready[i], 16)

                    def before():
                        for i in range(TT):
                            shift(0, i)

                    def step(n, b, i, more4, more3, more2, more1):
                        if more4:
                            sp.wait_ge(sm["v_done"], 4 * G(n) + 4)
                            shift(b + 1, i)

                    steps(sp, before, step, lambda: None)

                @block.gpsimd
                def _(pool):
                    def add_parts(n):
                        for k in range(2):
                            pool.wait_ge(sm["cos_ready"], 2 * G(n) + k + 1 + 2)
                            pool.wait_ge(sm["sin_ready"], 2 * G(n) + k + 1 + 4)
                            pool.tensor_tensor(me.t1[:, k, :], me.t1[:, k, :], me.t2[:, k, :], ALU.add).then_inc(sm["add_ready"], 1)

                    def scale(n):
                        for k in range(2):
                            pool.wait_ge(sm["add_ready"], 2 * G(n) + k + 1 + 2)
                            pool.wait_ge(sm["rn_ready"], 2 * G(n) + k + 1 + 4)
                            pool.wait_ge(sm["turn_done"], 4 * G(n) + 4 if k else 4 * G(n) + 2)
                            pool.tensor_tensor(me.qkn[:, k, :].rearrange("p (h d) -> p h d", h=H2),
                                               me.t1[:, k, :].rearrange("p (h d) -> p h d", h=H2),
                                               me.rn[:, k, :].unsqueeze(2).broadcast_to([P, H2, HD2]),
                                               ALU.mult).then_inc(sm["qkn_ready"], 1)

                    def normalize(n):
                        for u in range(2):
                            pool.wait_ge(sm["rsum_ready"], 2 * G(n) + u + 1)
                            pool.wait_ge(sm["pt_done"], 2 * G(n) + u - 1 + 4)
                            pool.tensor_tensor(me.pn[:, u, :, :], me.pr[:, u, :, :],
                                               me.rs[:, u, :].unsqueeze(2).broadcast_to([P, NPAIR, 2 * WIN]),
                                               ALU.mult).then_inc(sm["pn_ready"], 1)

                    def before():
                        add_parts(0)
                        scale(0)
                        add_parts(1)
                        scale(1)
                        add_parts(2)

                    def step(n, b, i, more4, more3, more2, more1):
                        if more2:
                            scale(n + 2)
                        normalize(n)
                        if more3:
                            add_parts(n + 3)

                    steps(pool, before, step, lambda: None)

                @block.scalar
                def _(act):
                    def squares(n, k):
                        act.wait_ge(sm["proj_done"], 2 * G(n) + k + 1 + 4)
                        act.wait_ge(sm["ssmax_ready"], 2 * G(n) + k - 1 + 4)
                        act.activation(me.sq[:, k, :], pa[:, 2 * k:2 * k + 2, :].rearrange("p a b -> p (a b)"),
                                       ACT.Square).then_inc(sm["sq_ready"], 1)

                    def inverse_norms(n, k):
                        act.wait_ge(sm["ssmax_ready"], 2 * G(n) + k + 1 + 4)
                        act.wait_ge(sm["qkn_ready"], 2 * G(n) + k - 1 + 2)
                        act.activation(me.rn[:, k, :], me.ss[:, k, :], ACT.Ln, scale=LN_RANGE).then_inc(sm["ln_step"], 1)
                        act.wait_ge(sm["ln_step"], 2 * G(n) + k + 1)
                        act.activation(me.rn[:, k, :], me.rn[:, k, :], ACT.Exp, scale=-0.5,
                                       bias=S.half_range[:, 0:1]).then_inc(sm["rn_ready"], 1)

                    def take_q(n):
                        for u in range(2):
                            act.wait_ge(sm["turn_done"], 4 * G(n) + u + 1 + 4)
                            act.wait_ge(sm["s_done"], 2 * G(n) + 4)
                            for half in range(2):
                                r = slice(64 * half, 64 * half + 64)
                                act.activation(me.qb[r, 4 * u:4 * u + 4, :, WIN * half:WIN * half + WIN],
                                               ring[r, u, :].rearrange("p (a w t) -> p a w t", a=4, w=NW),
                                               ACT.Identity).then_inc(sm["q_taken"], 1)

                    def exps(n):
                        for u in range(2):
                            act.wait_ge(sm["sub_ready"], 2 * G(n) + u + 1)
                            act.activation(me.pr[:, u, :, :], me.pr[:, u, :, :], ACT.Exp, scale=QK_SCALE).then_inc(sm["exp_ready"], 1)

                    def take_v(n, windows):
                        for w in windows:
                            act.wait_ge(sm["v_done"], 4 * G(n) + w + 1)
                            act.wait_ge(sm["o_done"], 2 * G(n) + 4)
                            act.activation(me.vs[:, w, :, :].rearrange("p j m -> p (j m)"), ring[:, 2 + w % 2, :],
                                           ACT.Identity).then_inc(sm["v_taken"], 1)

                    def take_turned_weights(n):
                        for u in range(2):
                            act.wait_ge(sm["pt_done"], 2 * G(n) + u + 1 + 4)
                            for half in range(2):
                                r = slice(64 * half, 64 * half + 64)
                                act.activation(me.pb[r, u, :, :, half, :],
                                               ring[r, 2 + u, :].rearrange("p (j x t) -> p j x t", j=4, x=4),
                                               ACT.Identity).then_inc(sm["pt_taken"], 1)

                    def take_weighted(n):
                        for half in range(2):
                            act.wait_ge(sm["o_done"], 2 * G(n) + half + 1 + 4)
                            act.wait_ge(sm["y_done"], G(n) + 4)
                            act.activation(me.os[:, 4 * half:4 * half + 4, :].rearrange("p a t -> p (a t)"), ring[:, half, :],
                                           ACT.Identity).then_inc(sm["o_taken"], 1)

                    def before():
                        act.preload_act_table_set("natural_log_exp_and_others")
                        for n in range(3):
                            for k in range(2):
                                squares(n, k)
                                inverse_norms(n, k)
                            if n == 1:
                                take_q(0)
                        exps(0)

                    def step(n, b, i, more4, more3, more2, more1):
                        if more1:
                            take_q(n + 1)
                        if more3:
                            squares(n + 3, 0)
                        take_v(n, (0, 1))
                        if more3:
                            inverse_norms(n + 3, 0)
                        take_v(n, (2, 3))
                        take_turned_weights(n)
                        if more3:
                            squares(n + 3, 1)
                        if more1:
                            exps(n + 1)
                        take_weighted(n)
                        if more3:
                            inverse_norms(n + 3, 1)

                    steps(act, before, step, lambda: None)

                @block.vector
                def _(dve):
                    def tables():
                        dve.wait_ge(S.weights_a, weights_count)
                        scales = me.qks[:, :, :]
                        cos, sin = me.cs[:, 0, :, :, :], me.cs[:, 1, :, :, :]
                        dve.tensor_tensor(cos, me.rope[:, 0, :, :, :], scales.unsqueeze(1).broadcast_to([P, TT, 2, HD2]), ALU.mult)
                        hd = HD2 // 2
                        for half in range(2):
                            to, other = slice(hd * half, hd * half + hd), slice(hd * (1 - half), hd * (1 - half) + hd)
                            ins = dve.tensor_tensor(sin[:, :, :, to], me.rope[:, 1, :, :, to],
                                                    scales[:, :, other].unsqueeze(1).broadcast_to([P, TT, 2, hd]), ALU.mult)
                        ins.then_inc(sm["table_step"], 1)
                        dve.wait_ge(sm["table_step"], layer + 1)

                    def sums(n, k):
                        dve.wait_ge(sm["sq_ready"], 2 * G(n) + k + 1)
                        dve.tensor_reduce(me.ss[:, k, :], me.sq[:, k, :].rearrange("p (h d) -> p h d", h=H2), AX_X,
                                          ALU.add).then_inc(sm["ss_ready"], 1)
                        dve.wait_ge(sm["ss_ready"], 2 * G(n) + k + 1)
                        dve.wait_ge(sm["rn_ready"], 2 * G(n) + k - 1 + 4)
                        dve.tensor_scalar(me.ss[:, k, :], me.ss[:, k, :], 1e-24, None, ALU.max).then_inc(sm["ssmax_ready"], 1)

                    def rope(n, i, k):
                        hd = HD2 // 2
                        raw = pa[:, 2 * k:2 * k + 2, :].rearrange("p a (h d) -> p (a h) d", d=HD2)
                        dve.wait_ge(sm["add_ready"], 2 * G(n) + k - 1 + 2)
                        dve.wait_ge(sm["qkn_ready"], 2 * G(n) + k - 1 + 2)
                        dve.tensor_tensor(me.t1[:, k, :].rearrange("p (h d) -> p h d", h=H2), raw,
                                          me.cs[:, 0, i, k, :].unsqueeze(1).broadcast_to([P, H2, HD2]),
                                          ALU.mult).then_inc(sm["cos_ready"], 1)
                        t2 = me.t2[:, k, :].rearrange("p (h d) -> p h d", h=H2)
                        for half in range(2):
                            to, other = slice(hd * half, hd * half + hd), slice(hd * (1 - half), hd * (1 - half) + hd)
                            ins = dve.tensor_tensor(t2[:, :, to], raw[:, :, other],
                                                    me.cs[:, 1, i, k, to].unsqueeze(1).broadcast_to([P, H2, hd]), ALU.mult)
                        ins.then_inc(sm["sin_ready"], 1)

                    def take_k(n, i):
                        s = i % 2
                        for u in range(2):
                            dve.wait_ge(sm["turn_done"], 4 * G(n) + 2 + u + 1 + 4)
                            bank = ring[:, 2 + u, :].rearrange("p (a t) -> p a t", a=4)
                            dve.tensor_copy(me.kt[:, s, 4 * u:4 * u + 4, WIN:], bank)
                            dve.tensor_copy(me.kt[:, 1 - s, 4 * u:4 * u + 4, 0:WIN], bank[:, :, P - WIN:]).then_inc(sm["k_taken"], 1)

                    def softmax(n, u):
                        dve.wait_ge(sm["s_done"], 2 * G(n) + u + 1 + 4)
                        sc = ring[:, u, :].rearrange("p (a k) -> p a k", a=NPAIR)
                        dve.tensor_reduce(me.mx[:, u, :], sc, AX_X, ALU.max).then_inc(sm["max_ready"], 1)
                        dve.wait_ge(sm["max_ready"], 2 * G(n) + u + 1)
                        dve.wait_ge(sm["pn_ready"], 2 * G(n) + u - 1 + 4)
                        dve.tensor_tensor(me.pr[:, u, :, :], sc, me.mx[:, u, :].unsqueeze(2).broadcast_to([P, NPAIR, 2 * WIN]),
                                          ALU.subtract).then_inc(sm["sub_ready"], 1)

                    def totals(n):
                        for u in range(2):
                            dve.wait_ge(sm["exp_ready"], 2 * G(n) + u + 1)
                            dve.tensor_reduce(me.su[:, u, :], me.pr[:, u, :, :], AX_X, ALU.add).then_inc(sm["sum_ready"], 1)
                            dve.wait_ge(sm["sum_ready"], 2 * G(n) + u + 1)
                            dve.reciprocal(me.rs[:, u, :], me.su[:, u, :]).then_inc(sm["rsum_ready"], 1)

                    def add_x(n, b, i):
                        dve.wait_ge(sm["y_done"], G(n) + 1 + 4)
                        at = slice(PADW + P * i, PADW + P * i + P)
                        dve.tensor_tensor(dst[:, b, at], pa[:, 0, 0:P], src[:, b, at], ALU.add).then_inc(sm["x_ready"], 1)

                    def before():
                        tables()
                        for n in range(3):
                            for k in range(2):
                                sums(n, k)
                                rope(n, n, k)
                            if n == 1:
                                take_k(0, 0)
                        softmax(0, 0)
                        softmax(0, 1)

                    def step(n, b, i, more4, more3, more2, more1):
                        if more1:
                            take_k(n + 1, (i + 1) % TT)
                        totals(n)
                        if more3:
                            sums(n + 3, 0)
                        if more1:
                            softmax(n + 1, 0)
                        if more3:
                            rope(n + 3, (i + 3) % TT, 0)
                        if more1:
                            softmax(n + 1, 1)
                        if more3:
                            sums(n + 3, 1)
                            rope(n + 3, (i + 3) % TT, 1)
                        add_x(n, b, i)

                    steps(dve, before, step, lambda: None)


def ffn_layer(core, F, layer, src, dst):
    nc, S, sm = core.nc, core, F.sm
    NC = 3
    sizes = [P, P, DI - 2 * P]
    with ExitStack() as ctx:
        pa = core.ps(ctx, "ff_pa", [P, NC, BANK])
        pg = core.ps(ctx, "ff_pg", [P, NC, BANK])
        py = core.ps(ctx, "ff_py", [P, 2, BANK])
        with nc.Block() as block:
            def loop(eng, one):
                with eng.Fori(0, B // 2) as r:
                    for u in range(2):
                        one(r * 2 + u, u)

            def G(b):
                return layer * B + b

            @block.tensor
            def _(pe):
                def one(b, u):
                    for c in range(NC):
                        pe.wait_ge(sm["gelu_ready"], NC * G(b) + c + 1)
                        pe.matmul(pg[0:sizes[c], c, :], F.w1[:, DI + P * c:DI + P * c + sizes[c]], S.h[:, b, :], start=True,
                                  stop=True).then_inc(sm["gate_done"], 1)
                        pe.wait_ge(sm["h_ready"], NC * G(b) + c + 1)
                        pe.matmul(pa[0:sizes[c], c, :], F.w1[:, P * c:P * c + sizes[c]], S.h[:, b, :], start=True,
                                  stop=True).then_inc(sm["a_done"], 1)
                    pe.wait_ge(sm["x_ready"], G(b) + 1)
                    for c in range(NC):
                        pe.wait_ge(sm["h_ready"], NC * G(b) + c + 4)
                        mm = pe.matmul(py[:, u, :], F.w2[0:sizes[c], c, :], F.hs[0:sizes[c], u, c, :], start=(c == 0),
                                       stop=(c == NC - 1))
                    mm.then_inc(sm["y_done"], 1)

                loop(pe, one)

            @block.scalar
            def _(act):
                def one(b, u):
                    for c in range(NC):
                        act.wait_ge(sm["gate_done"], NC * G(b) + c + 1)
                        act.wait_ge(sm["h_ready"], NC * G(b) + c + 1)
                        act.activation(F.gl[0:sizes[c], c, :], pg[0:sizes[c], c, :], ACT.Gelu,
                                       bias=F.b1[0:sizes[c], 3 + c:4 + c]).then_inc(sm["gelu_ready"], 1)

                act.preload_act_table_set("gelu_and_others")
                loop(act, one)

            @block.vector
            def _(dve):
                def one(b, u):
                    dve.wait_ge(sm["y_done"], G(b) + 1)
                    for c in range(NC):
                        dve.wait_ge(sm["a_done"], NC * G(b) + c + 1)
                        dve.wait_ge(sm["gelu_ready"], NC * G(b) + c + 4)
                        dve.scalar_tensor_tensor(out=F.hs[0:sizes[c], u, c, :], in0=pa[0:sizes[c], c, :],
                                                 scalar=F.b1[0:sizes[c], c:c + 1], in1=F.gl[0:sizes[c], c, :],
                                                 op0=ALU.add, op1=ALU.mult).then_inc(sm["h_ready"], 1)
                    dve.wait_ge(sm["y_done"], G(b) + 3)
                    dve.scalar_tensor_tensor(out=dst[:, b, PADW:], in0=py[:, u, :], scalar=F.b2[:, 0:1],
                                             in1=src[:, b, PADW:], op0=ALU.add, op1=ALU.add).then_inc(sm["x_ready"], 1)

                loop(dve, one)


class FeedForward:

    def __init__(self, core, ctx, work):
        self.sm = {n: core.sem("ff_" + n) for n in "gate_done a_done gelu_ready h_ready y_done x_ready shifted".split()}
        sb = lambda name, shape: core.sb(ctx, "ff_" + name, shape)
        self.w1, self.w2 = sb("w1", [P, 2 * DI]), sb("w2", [P, 3, P])
        self.b1, self.b2, self.lnp = sb("b1", [P, 6]), sb("b2", [P, 1]), sb("ln", [P, 2])
        flat = work[:, :, :, :].rearrange("p a b c -> p (a b c)")
        self.hs = flat[:, 0:6 * T].rearrange("p (u c t) -> p u c t", u=2, c=3)
        self.gl = flat[:, 6 * T:9 * T].rearrange("p (c t) -> p c t", c=3)


def shift_stage(core, F, layer, src):
    nc, S = core.nc, core
    with nc.Block() as block:
        @block.vector
        def _(dve):
            for b in range(B):
                dve.tensor_copy(S.h[0:64, b, :], src[0:64, b, PADW:])

        @block.scalar
        def _(act):
            for b in range(B):
                act.activation(S.h[64:P, b, :], src[64:P, b, PADW - 1:PADW - 1 + T], ACT.Identity)


def local_layers(core, A, C):
    nc, S = core.nc, core
    S.weights_a, S.weights_f = core.sem("weights_a"), core.sem("weights_f")
    added = core.sem("final_added")
    with ExitStack() as ctx:
        L = LocalAttention(core, ctx)
        F = FeedForward(core, ctx, L.work)

        def load_attention(sp, l):
            sp.dma_start(L.wqkv[:, :], A["L1_ffn_Wqkv"][l]).then_inc(S.weights_a, 16)
            sp.dma_start(L.wo[:, :, :], A["L1_ffn_Wo"][l].rearrange("(a p) d -> p a d", p=P)).then_inc(S.weights_a, 16)
            sp.dma_start(L.qks[:, 0, :], A["L1_ffn_q_scale"][l].partition_broadcast(P)).then_inc(S.weights_a, 16)
            sp.dma_start(L.qks[:, 1, :], A["L1_ffn_k_scale"][l].partition_broadcast(P)).then_inc(S.weights_a, 16)

        def load_feedforward(sp, l):
            sp.dma_start(F.w1[:, :], A["L1_ffn_W1"][l]).then_inc(S.weights_f, 16)
            sp.dma_start(F.w2[:, 0:2, :], A["L1_ffn_W2"][l][0:2 * P, :].rearrange("(a p) d -> p a d", p=P)).then_inc(S.weights_f, 16)
            sp.dma_start(F.w2[0:DI - 2 * P, 2, :], A["L1_ffn_W2"][l][2 * P:DI, :]).then_inc(S.weights_f, 16)
            for c in range(2):
                sp.dma_start(F.b1[:, 3 * c:3 * c + 2], A["L1_ffn_b1"][l][DI * c:DI * c + 2 * P].rearrange("(a p) -> p a", p=P)).then_inc(S.weights_f, 16)
                sp.dma_start(F.b1[0:DI - 2 * P, 3 * c + 2:3 * c + 3], column(A["L1_ffn_b1"][l][DI * c + 2 * P:DI * c + DI])).then_inc(S.weights_f, 16)
            for ap, n in ((F.b2[:, 0:1], "b2"), (F.lnp[:, 0:1], "ln_g"), (F.lnp[:, 1:2], "ln_b")):
                sp.dma_start(ap, column(A["L1_ffn_" + n][l])).then_inc(S.weights_f, 16)

        norm_stage(S, lambda b: S.xr[:, b, :], lambda b: S.xa[:, b, PADW:],
                   lambda b: S.mod[:, 1, 4, b:b + 1], lambda b: S.mod[:, 1, 3, b:b + 1])(5 * B)
        L.setup(A, C)
        norm = norm_stage(core, lambda b: S.h[:, b, :], lambda b: S.h[:, b, :], lambda b: F.lnp[:, 0:1], lambda b: F.lnp[:, 1:2])
        with nc.Block() as block:
            @block.sync
            def _(sp):
                load_attention(sp, 0)

            @block.vector
            def _(dve):
                for n, k in (("gelu_ready", 3), ("h_ready", 3), ("x_ready", 2), ("y_done", 2)):
                    dve.sem_inc(F.sm[n], k)
        with nc.Fori(0, DEPTH) as layer:
            with nc.Block() as block:
                @block.sync
                def _(sp):
                    with nc.allow_non_contiguous_dma("small vectors turned onto the partitions"):
                        load_feedforward(sp, layer)
            L.layer(layer, 64 * layer + 64, S.xa, S.xb, A)
            with nc.Block() as block:
                @block.sync
                def _(sp):
                    sp.wait_ge(S.weights_f, 160 * layer + 160)
                    load_attention(sp, (layer + 1) % DEPTH)
            shift_stage(core, F, layer, S.xb)
            norm((layer + 6) * B)
            ffn_layer(core, F, layer, S.xb, S.xa)
        with nc.Block() as block:
            @block.sync
            def _(sp):
                sp.wait_ge(S.weights_a, 64 * DEPTH + 64)

            @block.vector
            def _(dve):
                for b in range(B):
                    dve.scalar_tensor_tensor(out=S.xr[:, b, :], in0=S.xa[:, b, PADW:], scalar=S.mod[:, 1, 5, b:b + 1],
                                             in1=S.xr[:, b, :], op0=ALU.mult, op1=ALU.add)


def program(nc, A, C, out):
    with ExitStack() as ctx:
        nc.disable_value_cache = True
        S = Core(nc, ctx)
        S.xr = S.sb(ctx, "xr", [P, B, T])
        S.h = S.sb(ctx, "h", [P, B, T])
        S.xa = S.sb(ctx, "xa", [P, B, XW])
        S.xb = S.sb(ctx, "xb", [P, B, XW])
        S.ident, S.mean, S.center = (S.sb(ctx, n, [P, P]) for n in ("ident", "mean", "center"))
        S.identb = S.sb(ctx, "identb", [P, P], BF16)
        S.mod = S.sb(ctx, "mod", [P, 2, 6, B])
        S.eps = S.sb(ctx, "eps", [P, 1])
        S.half_range = S.sb(ctx, "half_range", [P, 1])
        l0 = ctx.enter_context(ExitStack())
        S.cos0, S.sin0 = (S.sb(l0, n, [P, T]) for n in ("cos0", "sin0"))
        S.swap0 = S.sb(l0, "swap0", [P, P])
        S.pick = S.sb(l0, "pick", [P, E0, P], BF16)
        S.bq = S.sb(l0, "bq", [P, 4])
        S.bo0 = S.sb(l0, "bo0", [P, 1])
        S.bv0 = S.sb(l0, "bv0", [P, P])
        S.w0 = S.sb(l0, "w0", [P, 6, P])
        S.norms = 0
        S.norm_sems = [S.sem("norm_" + n) for n in ("centered", "squared", "var", "ln", "rstd", "scaled", "done")]
        S.constants_set = S.sem("constants_set")
        with nc.Block() as block:
            @block.vector
            def _(dve):
                dve.memset(S.eps[:, :], EPS).then_inc(S.constants_set, 1)
                dve.memset(S.half_range[:, :], float(0.5 * np.log(LN_RANGE))).then_inc(S.constants_set, 1)
                dve.wait_ge(S.constants_set, 2)
        prelude(S, A, C)
        norm_stage(S, lambda b: S.xr[:, b, :], lambda b: S.h[:, b, :],
                   lambda b: S.mod[:, 0, 1, b:b + 1], lambda b: S.mod[:, 0, 0, b:b + 1])(0)
        attention0(S)
        ffn0(S, A, C)
        l0.close()
        norm_stage(S, lambda b: S.xr[:, b, :], lambda b: S.h[:, b, :],
                   lambda b: S.mod[:, 1, 1, b:b + 1], lambda b: S.mod[:, 1, 0, b:b + 1])(4 * B)
        attention1(S, A, C)
        local_layers(S, A, C)
        store(S, out, S.xr)


def store(core, out, src):
    nc, S = core.nc, core
    turned, taken, stored = core.sem("out_turned"), core.sem("out_taken"), core.sem("out_stored")
    with ExitStack() as ctx:
        px = core.ps(ctx, "out_px", [P, 4, BANK])
        xt = core.sb(ctx, "out_tokens", [P, B, T])
        with nc.Block() as block:
            @block.tensor
            def _(pe):
                for n in range(B):
                    if n >= 4:
                        pe.wait_ge(taken, n - 3)
                    for c in range(TT):
                        tr = pe.transpose(px[:, n % 4, P * c:P * c + P], src[:, n, P * c:P * c + P], S.ident[:, :])
                    tr.then_inc(turned, 1)

            @block.scalar
            def _(act):
                for n in range(B):
                    act.wait_ge(turned, n + 1)
                    act.activation(xt[:, n, :], px[:, n % 4, :], ACT.Identity).then_inc(taken, 1)

            @block.sync
            def _(sp):
                for n in range(B):
                    sp.wait_ge(taken, n + 1)
                    sp.dma_start(out[n].rearrange("(c p) d -> p c d", p=P),
                                 xt[:, n, :].rearrange("p (c d) -> p c d", c=TT)).then_inc(stored, 16)
                sp.wait_ge(stored, 16 * B)


INPUTS = ['L0_attn_x', 'L0_attn_Wq', 'L0_attn_bq', 'L0_attn_Wk', 'L0_attn_bk', 'L0_attn_Wv', 'L0_attn_bv', 'L0_attn_Wo',
          'L0_attn_bo', 'L0_ffn_g1', 'L0_ffn_be1', 'L0_ffn_mix_w', 'L0_ffn_mix_b', 'L0_ffn_g2', 'L0_ffn_be2',
          'L0_ffn_router_w', 'L0_ffn_w1', 'L0_ffn_b1', 'L0_ffn_w2', 'L0_ffn_b2', 'L0_c', 'L0_wmod', 'L1_attn_phase',
          'L1_attn_Wq', 'L1_attn_bq', 'L1_attn_Wk', 'L1_attn_bk', 'L1_attn_Wv', 'L1_attn_bv', 'L1_attn_Wo', 'L1_attn_bo',
          'L1_ffn_Wqkv', 'L1_ffn_q_scale', 'L1_ffn_k_scale', 'L1_ffn_Wo', 'L1_ffn_ln_g', 'L1_ffn_ln_b', 'L1_ffn_W1',
          'L1_ffn_b1', 'L1_ffn_W2', 'L1_ffn_b2', 'L1_c', 'L1_wmod']


def kernel(**inputs):
    import concourse.bacc as bacc
    from concourse.bass_utils import run_bass_kernel_spmd

    nc = bacc.Bacc("TRN2", target_bir_lowering=False, num_devices=1)
    arrays, args, tables = {}, {}, {}
    for name in INPUTS:
        a = np.ascontiguousarray(inputs[name])
        arrays[f"in_{name}"] = a
        args[name] = nc.dram_tensor(f"in_{name}", a.shape, mybir.dt.from_np(a.dtype), kind="ExternalInput").ap()
    for name, a in constants().items():
        a = np.ascontiguousarray(a)
        arrays[f"const_{name}"] = a
        tables[name] = nc.dram_tensor(f"const_{name}", a.shape, mybir.dt.from_np(a.dtype), kind="ExternalInput").ap()
    out = nc.dram_tensor("out", (B, T, D), F32, kind="ExternalOutput").ap()
    program(nc, args, tables, out)
    r = run_bass_kernel_spmd(nc, [arrays], core_ids=[0])
    return r.results[0]["out"]
```

```python
from contextlib import ExitStack

import numpy as np

import concourse.bass as bass
from concourse import mybir

F32 = mybir.dt.float32
BF16 = mybir.dt.bfloat16
ACT = mybir.ActivationFunctionType
ALU = mybir.AluOpType
AX_X = mybir.AxisListType.X

B, T, D = 8, 512, 128
P = 128
TT = T // P
EPS = 1e-5
BANK = 512
NEG = -1e30

H0, HD0 = 16, 8
E0, F0 = 8, 512
H1, HD1, TB = 4, 128, 32
DEPTH, H2, HD2, WIN = 6, 16, 64, 32
INNER = H2 * HD2
QK_SCALE = 8.0
DI = 341
PADW = WIN + 1
XW = PADW + T
LN_RANGE = 2.0 ** 20


def constants():
    f = np.float32
    c = {}
    c["ident"] = np.eye(P, dtype=f)
    c["mean"] = np.full((P, P), 1.0 / P, f)
    c["center"] = (np.eye(P) - 1.0 / P).astype(f)
    half = HD0 // 2
    inv = (1.0 / f(10000.0) ** (np.arange(0, HD0, 2, dtype=f) / f(HD0))).astype(f)
    ang = (np.arange(T, dtype=f)[:, None] * inv[None, :]).astype(f)
    d = np.arange(P) % HD0
    c["cos0"] = np.cos(ang).astype(f).T[d % half].copy()
    c["sin0"] = (np.sin(ang).astype(f).T[d % half] * np.where(d < half, -1, 1)[:, None]).astype(f)
    other = np.arange(P) + np.where(d < half, half, -half)
    swap = np.zeros((P, P), f)
    swap[other, np.arange(P)] = 1
    c["swap0"] = swap
    pick = np.zeros((P, E0, P), f)
    for part in range(3):
        for h in range(E0):
            pick[32 * part + h, h, :] = 1
    c["pick"] = pick.reshape(P, E0 * P)
    c["lower"] = np.broadcast_to(np.tril(np.ones((E0, E0), f), -1).reshape(1, -1), (P, E0 * E0)).copy()
    t = np.arange(P) % TB
    c["mask1"] = np.where(t[:, None] == t[None, :], 0, NEG).astype(f)
    q = (np.arange(P) % WIN)[:, None]
    k = np.arange(2 * WIN)[None, :]
    ok = (q <= k) & (q >= k - WIN)
    first = ok & ((np.arange(P)[:, None] >= 64) | (k >= WIN))
    c["mask2"] = np.concatenate([np.where(ok, 0, NEG), np.where(first, 0, NEG)], 1).astype(f)
    hf = np.arange(0, HD2, 2, dtype=f)
    inv = (1.0 / f(10000.0) ** (hf / f(HD2))).astype(f)
    tok = np.arange(T, dtype=f)
    ang = (tok[:, None] * inv[None, :]).astype(f)
    ang = np.concatenate([ang, ang], 1)
    base = ((hf + f(0.4 * HD2)) / f(1.4 * HD2)).astype(f)
    power = ((tok - T // 2) / f(WIN // 2)).astype(f)
    scale = (base[None, :] ** power[:, None]).astype(f)
    scale = np.concatenate([scale, scale], 1)
    sign = np.where(np.arange(HD2) < HD2 // 2, -1, 1).astype(f)
    cos, sin = np.cos(ang).astype(f), (np.sin(ang) * sign).astype(f)
    co = np.stack([cos * scale, cos / scale], 1).reshape(TT, P, 2, HD2).transpose(1, 0, 2, 3)
    si = np.stack([sin * scale, sin / scale], 1).reshape(TT, P, 2, HD2).transpose(1, 0, 2, 3)
    c["cos2"] = np.ascontiguousarray(co.reshape(P, -1)).astype(f)
    c["sin2"] = np.ascontiguousarray(si.reshape(P, -1)).astype(f)
    return c


def column(v):
    return v.rearrange("(p one) -> p one", one=1)


def across(v, n=P):
    return v.partition_broadcast(n)


class Core:

    def __init__(self, nc, ctx):
        self.nc, self.ctx = nc, ctx

    def sb(self, ctx, name, shape, dt=F32):
        return ctx.enter_context(self.nc.sbuf_tensor(name, shape, dt))

    def ps(self, ctx, name, shape, dt=F32):
        return ctx.enter_context(self.nc.psum_tensor(name, shape, dt))

    def sem(self, name):
        return self.ctx.enter_context(self.nc.semaphore(name))


def prelude(core, A, C):
    nc = core.nc
    loaded, small, cast = core.sem("x_loaded"), core.sem("small_loaded"), core.sem("pick_loaded")
    turned, taken = core.sem("x_turned"), core.sem("x_taken")
    silu_ready, silu_turned, silu_t_ready = core.sem("silu_ready"), core.sem("silu_turned"), core.sem("silu_t_ready")
    mod_done, gate_step = core.sem("mod_done"), core.sem("gate_step")
    w_turned, w_taken = core.sem("w_turned"), core.sem("w_taken")
    bias_turned = core.sem("bias_turned")
    S = core
    with ExitStack() as ctx:
        xt = core.sb(ctx, "x_tokens", [P, B * TT, P])
        cc = core.sb(ctx, "cond", [B, 2, P])
        sc = core.sb(ctx, "cond_silu", [B, 2, P])
        sct = core.sb(ctx, "cond_silu_t", [P, 2, B])
        wmod = core.sb(ctx, "wmod", [P, 2, 6 * P])
        w4 = core.sb(ctx, "w_l0", [P, 4, P])
        sg = core.sb(ctx, "gate_sign", [P, 2 * B])
        ab = core.sb(ctx, "gate_size", [P, 2 * B])
        ra = core.sb(ctx, "gate_raw", [P, 2 * B])
        px = core.ps(ctx, "px", [P, 4, BANK])
        pm = core.ps(ctx, "pm", [P, 2, BANK])
        pw = core.ps(ctx, "pw", [P, 2, BANK])
        names = ["L0_attn_Wq", "L0_attn_Wk", "L0_attn_Wv", "L0_attn_Wo"]
        NSMALL = 6 + 2 + 2 + 4 + 4
        with nc.Block() as block:
            @block.sync
            def _(sp):
                for g in range(4):
                    sp.dma_start(xt[:, 8 * g:8 * g + 8, :],
                                 A["L0_attn_x"].rearrange("b t d -> (b t) d")[1024 * g:1024 * g + 1024, :]
                                 .rearrange("(n p) d -> p n d", p=P)).then_inc(loaded, 16)
                for n, ap in (("L0_attn_bk", S.bq[:, 1:2]), ("L0_attn_bq", S.bq[:, 0:1]), ("L0_attn_bo", S.bo0[:, :])):
                    sp.dma_start(ap, column(A[n])).then_inc(small, 16)
                sp.dma_start(S.bv0[:, :], across(A["L0_attn_bv"])).then_inc(small, 16)
                sp.wait_ge(loaded, 64)
                sp.wait_ge(small, 16 * NSMALL)

            @block.gpsimd
            def _(pool):
                pool.dma_start(S.pick[:, :, :].rearrange("p h m -> p (h m)"), C["pick"]).then_inc(cast, 16)
                pool.dma_start(S.identb[:, :], C["ident"]).then_inc(cast, 16)
                pool.memset(S.xa[:, :, 0:PADW], 0.0)
                pool.memset(S.xb[:, :, 0:PADW], 0.0)
                pool.wait_ge(cast, 32)

            @block.tensor
            def _(pe):
                pe.wait_ge(small, 16 * NSMALL)
                pe.wait_ge(silu_ready, 1)
                for l in range(2):
                    tr = pe.transpose(pm[:, 0, 8 * l:8 * l + 8], sc[:, l, :], S.ident[0:B, 0:B])
                tr.then_inc(silu_turned, 1)
                pe.transpose(pw[:, 0, 0:128], w4[:, 0, :], S.ident[:, :])
                pe.transpose(pw[:, 0, 128:256], w4[:, 1, :], S.ident[:, :])
                pe.transpose(pw[:, 0, 256:384], w4[:, 2, :], S.ident[:, :])
                pe.transpose(pw[:, 0, 384:512], w4[:, 3, :], S.ident[:, :]).then_inc(w_turned, 1)
                pe.matmul(pw[:, 1, 0:128], w4[:, 0, :], S.swap0[:, :], start=True, stop=True)
                pe.matmul(pw[:, 1, 128:256], w4[:, 1, :], S.swap0[:, :], start=True, stop=True)
                pe.matmul(pw[:, 1, 256:258], S.swap0[:, :], S.bq[:, 0:2], start=True, stop=True).then_inc(w_turned, 1)
                pe.wait_ge(silu_t_ready, 1)
                for l in range(2):
                    for j in range(6):
                        at = (l * 6 + j) * B
                        mm = pe.matmul(pm[:, 1, at:at + B], wmod[:, l, P * j:P * j + P], sct[:, l, :],
                                       start=True, stop=True)
                mm.then_inc(mod_done, 1)
                pe.wait_ge(loaded, 64)
                for n in range(B * TT // 4):
                    if n >= 4:
                        pe.wait_ge(taken, n - 3)
                    for c in range(4):
                        tr = pe.transpose(px[:, n % 4, P * c:P * c + P], xt[:, 4 * n + c, :], S.ident[:, :])
                    tr.then_inc(turned, 1)

            @block.scalar
            def _(act):
                for n, ap in (("ident", S.ident), ("mean", S.mean), ("center", S.center), ("cos0", S.cos0),
                              ("sin0", S.sin0), ("swap0", S.swap0)):
                    act.dma_start(ap[:, :], C[n]).then_inc(small, 16)
                for l in range(2):
                    act.dma_start(cc[:, l, :], A[f"L{l}_c"]).then_inc(small, 16)
                    act.dma_start(wmod[:, l, :], A[f"L{l}_wmod"]).then_inc(small, 16)
                for i, n in enumerate(names):
                    act.dma_start(w4[:, i, :], A[n]).then_inc(small, 16)
                act.wait_ge(small, 16 * NSMALL)
                act.activation(sc[:, :, :], cc[:, :, :], ACT.Silu).then_inc(silu_ready, 1)
                for n in range(B * TT // 4):
                    act.wait_ge(turned, n + 1)
                    act.activation(S.xr[:, n, :], px[:, n % 4, :], ACT.Identity).then_inc(taken, 1)

            @block.vector
            def _(dve):
                dve.wait_ge(silu_turned, 1)
                dve.tensor_copy(sct[:, :, :].rearrange("p l b -> p (l b)"), pm[:, 0, 0:2 * B]).then_inc(silu_t_ready, 1)
                dve.wait_ge(w_turned, 1)
                dve.tensor_copy(S.w0[:, 0:4, :].rearrange("p n m -> p (n m)"), pw[:, 0, :])
                dve.wait_ge(w_turned, 2)
                dve.tensor_copy(S.w0[:, 4:6, :].rearrange("p n m -> p (n m)"), pw[:, 1, 0:256])
                dve.tensor_copy(S.bq[:, 2:4], pw[:, 1, 256:258])
                dve.wait_ge(mod_done, 1)
                m = pm[:, 1, 0:12 * B].rearrange("p (l j b) -> p l j b", l=2, j=6)
                for j in (0, 3):
                    dve.tensor_copy(S.mod[:, :, j, :], m[:, :, j, :])
                for j in (1, 4):
                    dve.tensor_scalar(S.mod[:, :, j, :], m[:, :, j, :], 1.0, None, ALU.add)
                n = 0
                for j in (2, 5):
                    raw = ra[:, :].rearrange("p (l b) -> p l b", l=2)
                    sgn, size = sg[:, :].rearrange("p (l b) -> p l b", l=2), ab[:, :].rearrange("p (l b) -> p l b", l=2)
                    for ins in (lambda: dve.tensor_scalar(sgn, m[:, :, j, :], 0.0, 2.0, ALU.is_ge, ALU.mult),
                                lambda: dve.tensor_scalar(sgn, sgn, 1.0, None, ALU.subtract),
                                lambda: dve.tensor_copy(raw, m[:, :, j, :]),
                                lambda: dve.scalar_tensor_tensor(out=size, in0=raw, scalar=-1.0, in1=raw, op0=ALU.mult, op1=ALU.max),
                                lambda: dve.tensor_scalar(size, size, 0.25, None, ALU.max),
                                lambda: dve.tensor_tensor(S.mod[:, :, j, :], sgn, size, ALU.mult)):
                        ins().then_inc(gate_step, 1)
                        n += 1
                        dve.wait_ge(gate_step, n)


def norm_stage(core, source, target, scale, shift, batches=B, shifted_from=None, beside=None):
    nc, S = core.nc, core
    U = 4
    S.norms += 1
    tag = f"norm{S.norms}"
    centered, squared, var_done, ln_step, rstd_ready, scaled, done = S.norm_sems

    def stage(before):
        with ExitStack() as ctx:
            pc = core.ps(ctx, tag + "_pc", [P, U, BANK])
            pv = core.ps(ctx, tag + "_pv", [P, U, BANK])
            work = core.sb(ctx, tag + "_work", [P, U, T])
            with nc.Block() as block:
                @block.tensor
                def _(pe):
                    for n in range(batches + 1):
                        if n < batches:
                            if shifted_from is not None:
                                pe.wait_ge(S.shifted, before + n + 1)
                            if n >= U:
                                pe.wait_ge(scaled, before + n - U + 1)
                            pe.matmul(pc[:, n % U, :], S.center[:, :], source(n), start=True, stop=True).then_inc(centered, 1)
                        if n:
                            b = n - 1
                            pe.wait_ge(squared, before + b + 1)
                            if b >= U:
                                pe.wait_ge(rstd_ready, before + b - U + 1)
                            pe.matmul(pv[:, b % U, :], S.mean[:, :], work[:, b % U, :], start=True, stop=True).then_inc(var_done, 1)

                @block.scalar
                def _(act):
                    act.preload_act_table_set("natural_log_exp_and_others")
                    for n in range(batches + 1):
                        if n < batches:
                            act.wait_ge(centered, before + n + 1)
                            if n >= U:
                                act.wait_ge(done, before + n - U + 1)
                            act.activation(work[:, n % U, :], pc[:, n % U, :], ACT.Square).then_inc(squared, 1)
                        if n:
                            b = n - 1
                            u = b % U
                            act.wait_ge(var_done, before + b + 1)
                            act.activation(work[:, u, :], pv[:, u, :], ACT.Ln, bias=S.eps[:, 0:1]).then_inc(ln_step, 1)
                            act.wait_ge(ln_step, before + b + 1)
                            act.activation(work[:, u, :], work[:, u, :], ACT.Exp, scale=-0.5).then_inc(rstd_ready, 1)

                @block.vector
                def _(dve):
                    if shifted_from is not None:
                        for b in range(batches):
                            dve.tensor_copy(S.h[0:64, b, :], shifted_from[0:64, b, PADW:])
                            dve.tensor_copy(S.h[64:P, b, :], shifted_from[64:P, b, PADW - 1:PADW - 1 + T]).then_inc(S.shifted, 1)
                    for b in range(batches):
                        u = b % U
                        dve.wait_ge(rstd_ready, before + b + 1)
                        dve.tensor_tensor(work[:, u, :], pc[:, u, :], work[:, u, :], ALU.mult).then_inc(scaled, 1)
                        dve.wait_ge(scaled, before + b + 1)
                        dve.tensor_scalar(target(b), work[:, u, :], scale(b), shift(b), ALU.mult, ALU.add).then_inc(done, 1)

                if beside is not None:
                    beside(block)

    return stage


def attention0(core):
    nc, S = core.nc, core
    names = ("proj_done rope_step q_ready parts_step v_done v_ready spilled stacked_low stacked_high score_done max_ready "
             "maxt_done part_step rows_ready gated st_done exp_done pv_done o_ready ot_done onorm_step of_done of_ready "
             "y_done hs_ready zeroed ones_set ones_ready").split()
    sm = {n: core.sem("a0_" + n) for n in names}
    NS = H0 * TT
    QB = 4
    NQ = NS // QB
    GH = 4
    GQ = GH * TT // QB
    NG = H0 // GH
    NP = 3
    KR = NP * NP * HD0
    KM = KR + NP
    NPT = 2 * QB
    HH = H0 // 2
    LAY = 2 * NP * NP * 16
    with ExitStack() as ctx:
        hs = core.sb(ctx, "a0_hs", [P, T])
        ta, tb, qk, rest = (S.xb[:, i:i + 2, PADW:] for i in (0, 2, 4, 6))
        pt = S.xa[:, 0:NPT, PADW:]
        scratch = nc.dram_tensor("a0_scratch", (P, 2, NP, 2, T), BF16, kind="Internal").ap()
        parts = core.sb(ctx, "a0_parts", [P, NP, 2, T], BF16)
        ones = core.sb(ctx, "a0_ones", [NP, T], BF16)
        qs = core.sb(ctx, "a0_stacked", [P, 2, 2, H0, T], BF16)
        vv = core.sb(ctx, "a0_v", [P, 2, TT, H0, 32])
        mx = core.sb(ctx, "a0_max", [P, 2, TT, HH])
        rem = core.sb(ctx, "a0_rem", [HH, 2, T])
        mid = core.sb(ctx, "a0_mid", [HH, T], BF16)
        mb = core.sb(ctx, "a0_maxparts", [96, T], BF16)
        os_ = core.sb(ctx, "a0_o", [P, 2, T])
        rc = core.sb(ctx, "a0_rsum", [P, TT, GH])
        on = core.sb(ctx, "a0_onorm", [P, TT, P])
        of = core.sb(ctx, "a0_of", [P, T])
        tx = core.sb(ctx, "a0_tx", [P, T])
        ring = core.ps(ctx, "a0_ring", [P, 4, BANK])
        og = core.ps(ctx, "a0_og", [P, 2, BANK])
        t1 = core.ps(ctx, "a0_t1", [P, BANK])
        t2 = core.ps(ctx, "a0_t2", [P, BANK])
        with nc.Block() as block:
            def steps(eng, step):
                def flags(b):
                    return {"prepared": b + 2 < B, "maxima": b + 1 < B, "weighed": b >= 0, "tail": b >= 1, "first": b == 0}
                step(-1, 1, flags(-1))
                step(0, 0, flags(0))
                with eng.Fori(0, B // 2 - 2) as r:
                    step(r * 2 + 1, 1, flags(1))
                    step(r * 2 + 2, 0, flags(2))
                for b in range(B - 3, B):
                    step(b, b % 2, flags(b))

            def head_of(n):
                return n // (GH * TT), n // GH % TT, n % GH

            @block.gpsimd
            def _(pool):
                pool.tensor_copy(hs[:, :], S.h[:, 0, :]).then_inc(sm["hs_ready"], 1)
                pool.memset(vv[:, :, :, :, :].rearrange("p u c h m -> p (u c h m)"), 0.0).then_inc(sm["zeroed"], 1)
                pool.wait_ge(sm["zeroed"], 1)
                pool.memset(vv[:, :, :, :, HD0:HD0 + 1].rearrange("p u c h m -> p (u c) h m"), 1.0).then_inc(sm["zeroed"], 1)
                with pool.Fori(0, B - 1) as b:
                    pool.wait_ge(sm["v_done"], b + 1)
                    pool.tensor_copy(hs[:, :], S.h[:, b + 1, :]).then_inc(sm["hs_ready"], 1)

            @block.sync
            def _(sp):
                def lay(i, u, heads, done):
                    for x in range(2):
                        for j in range(NP):
                            row = HD0 * (NP * i + j if x == 0 else NP * j + i)
                            rows = scratch[:, u, i, x, :].rearrange("(h d) t -> d h t", h=H0)
                            sp.dma_start(qs[row:row + HD0, u, x, heads, :], rows[:, heads, :]).then_inc(sm[done], 16)

                low, high = slice(0, HH), slice(HH, H0)

                def spill(s, u, i):
                    sp.wait_ge(sm["parts_step"], s * 4 + (1, 3, 4)[i])
                    sp.dma_start(scratch[:, u, i, :, :], parts[:, i, :, :]).then_inc(sm["spilled"], 16)

                def lay_low(s, u, i):
                    sp.wait_ge(sm["spilled"], (s * NP + i + 1) * 16)
                    lay(i, u, low, "stacked_low")

                def rows(s, u, half):
                    sp.wait_ge(sm["part_step"], s * 12 + 6 * half + 6)
                    for i in range(NP):
                        sp.dma_start(qs[KR + i:KR + i + 1, u, 0, HH * half:HH * half + HH, :],
                                     mb[32 * i:32 * i + HH, :]).then_inc(sm["rows_ready"], 16)

                def step(b, u, has):
                    if has["maxima"]:
                        if has["tail"]:
                            sp.wait_ge(sm["st_done"], b * NS)
                        for i in range(NP):
                            lay(i, 1 - u, high, "stacked_high")
                    if has["weighed"]:
                        rows(b, u, 1)
                    if has["prepared"]:
                        if has["weighed"]:
                            sp.wait_ge(sm["stacked_high"], (b + 1) * LAY)
                        for i in range(NP):
                            spill(b + 2, u, i)
                            if has["weighed"] and i == 0:
                                sp.wait_ge(sm["st_done"], b * NS + NS // 2)
                            lay_low(b + 2, u, i)
                    if has["maxima"]:
                        if has["weighed"]:
                            sp.wait_ge(sm["rows_ready"], (2 * b + 2) * 16 * NP)
                        rows(b + 1, 1 - u, 0)

                for i in range(NP):
                    spill(0, 0, i)
                sp.wait_ge(sm["spilled"], NP * 16)
                for i in range(NP):
                    lay(i, 0, low, "stacked_low")
                sp.wait_ge(sm["ones_set"], 1)
                for u in range(2):
                    sp.dma_start(qs[KR:KM, u, 1, :, :], ones[:, :].unsqueeze(1).broadcast_to([NP, H0, T])).then_inc(sm["ones_ready"], 16)
                steps(sp, step)

            @block.tensor
            def _(pe):
                def project_first(i):
                    if i == 0:
                        pe.wait_ge(sm["hs_ready"], 1)
                    pe.matmul(ring[:, i, :], S.w0[:, (0, 4, 1, 5)[i], :], hs[:, :], start=True, stop=True).then_inc(sm["proj_done"], 1)

                def project(s, i, has):
                    if i == 0:
                        pe.wait_ge(sm["hs_ready"], s + 1)
                        if has["tail"]:
                            pe.wait_ge(sm["gated"], s - 2)
                        elif has["weighed"]:
                            pe.wait_ge(sm["part_step"], 8)
                    else:
                        pe.wait_ge(sm["rope_step"], s * 4 + i)
                    pe.matmul(t2[:, :], S.w0[:, (0, 4, 1, 5)[i], :], hs[:, :], start=True, stop=True).then_inc(sm["proj_done"], 1)

                def values(a, has):
                    if has["tail"]:
                        pe.wait_ge(sm["onorm_step"], (a - 1) * 8)
                    elif has["weighed"]:
                        pe.wait_ge(sm["v_ready"], 1)
                    for c in range(TT):
                        mm = pe.matmul(t1[:, P * c:P * c + P], hs[:, P * c:P * c + P], S.w0[:, 2, :], start=True, stop=True)
                    mm.then_inc(sm["v_done"], 1)

                def turn_maxima(s, half, has):
                    pe.wait_ge(sm["max_ready"], s * NS + NS // 2 * (half + 1))
                    if half:
                        pe.wait_ge(sm["part_step"], s * 12 + 6)
                    elif has["prepared"]:
                        pe.wait_ge(sm["rope_step"], s * 4 + 8)
                    else:
                        pe.wait_ge(sm["gated"], s - 1)
                    for c in range(TT):
                        tr = pe.transpose(t2[0:HH, P * c:P * c + P], mx[:, half, c, :], S.ident[:, :])
                    tr.then_inc(sm["maxt_done"], 1)

                def turn_out(b, g, has):
                    pe.wait_ge(sm["o_ready"], b * NG + g + 1)
                    if g:
                        pe.wait_ge(sm["onorm_step"], b * 8 + 2 * g)
                    elif has["maxima"]:
                        pe.wait_ge(sm["v_ready"], b + 2)
                    else:
                        pe.wait_ge(sm["onorm_step"], b * 8)
                    for c in range(TT):
                        tr = pe.transpose(t1[:, P * c:P * c + P], os_[:, g % 2, P * c:P * c + P], S.ident[:, :])
                    tr.then_inc(sm["ot_done"], 1)

                def turn_normed(b):
                    pe.wait_ge(sm["onorm_step"], b * 8 + 8)
                    pe.wait_ge(sm["part_step"], min(b * 12 + 20, 12 * B) if isinstance(b, int) else b * 12 + 20)
                    for c in range(TT):
                        tr = pe.transpose(t2[:, P * c:P * c + P], on[:, c, :], S.ident[:, :])
                    tr.then_inc(sm["of_done"], 1)

                def project_out(b):
                    pe.wait_ge(sm["of_ready"], b + 1)
                    pe.matmul(t2[:, :], S.w0[:, 3, :], of[:, :], start=True, stop=True).then_inc(sm["y_done"], 1)

                def largest(a, u, n):
                    if n >= 2 or not isinstance(a, int) or a:
                        pe.wait_ge(sm["max_ready"], a * NS + n - 1)
                    pe.matmul(ring[:, n % 2, :], qs[0:KR, u, 0, n // TT, P * (n % TT):P * (n % TT) + P],
                              qs[0:KR, u, 1, n // TT, :], start=True, stop=True).then_inc(sm["score_done"], 1)

                def scores(b, u, n, has):
                    g, c, j = head_of(n)
                    if n in (0, NS // 2):
                        pe.wait_ge(sm["rows_ready"], (2 * b + n // (NS // 2) + 1) * 16 * NP)
                    if n >= 2 or not has["first"]:
                        pe.wait_ge(sm["exp_done"], b * NS + n - 1)
                    pe.matmul(ring[:, 2 + n % 2, :], qs[0:KM, u, 1, GH * g + j, P * c:P * c + P], qs[0:KM, u, 0, GH * g + j, :],
                              start=True, stop=True).then_inc(sm["st_done"], 1)

                def weighted(b, u, q, has):
                    g, c, _ = head_of(QB * q)
                    if q == 0:
                        pe.wait_ge(sm["v_ready"], b + 1)
                    if c == 0 and not (has["first"] and g < 2):
                        pe.wait_ge(sm["o_ready"], b * NG + g - 1)
                    for n in range(QB * q, QB * q + QB):
                        j = n % GH
                        pe.wait_ge(sm["exp_done"], b * NS + n + 1)
                        pe.matmul(og[32 * j:32 * j + 32, g % 2, :], vv[:, u, c, GH * g + j, :], pt[:, n % NPT, :],
                                  start=(c == 0), stop=(c == TT - 1)).then_inc(sm["pv_done"], 1)

                def step(b, u, has):
                    for q in range(NQ):
                        for k in range(QB):
                            n = QB * q + k
                            if has["maxima"]:
                                if n == 0:
                                    pe.wait_ge(sm["stacked_low"], (b + 2) * LAY)
                                elif n == NS // 2:
                                    pe.wait_ge(sm["stacked_high"], (b + 2) * LAY)
                                largest(b + 1, 1 - u, n)
                            if has["weighed"]:
                                scores(b, u, n, has)
                            if k == 1 and has["weighed"] and q:
                                weighted(b, u, q - 1, has)
                            if k != QB - 1:
                                continue
                            if has["weighed"] and q == 0:
                                turn_maxima(b, 1, has)
                            if has["tail"]:
                                if q == 0:
                                    turn_out(b - 1, NG - 1, has)
                                elif q == 2:
                                    turn_normed(b - 1)
                                elif q == 4:
                                    project_out(b - 1)
                            if has["maxima"] and q == 3:
                                values(b + 1, has)
                            if has["prepared"] and 5 <= q < 9:
                                project(b + 2, q - 5, has)
                            if has["weighed"] and q in (6, 10, 14):
                                turn_out(b, (q - 6) // GQ, has)
                            if has["maxima"] and q == 10:
                                turn_maxima(b + 1, 0, has)
                    if has["weighed"]:
                        weighted(b, u, NQ - 1, has)

                for i in range(4):
                    project_first(i)
                pe.wait_ge(sm["rope_step"], 4)
                pe.wait_ge(sm["ones_ready"], 32)
                steps(pe, step)
                turn_out(B - 1, NG - 1, {})
                turn_normed(B - 1)
                project_out(B - 1)

            @block.scalar
            def _(act):
                def exp(b, n):
                    act.wait_ge(sm["st_done"], b * NS + n + 1)
                    if n >= NPT:
                        act.wait_ge(sm["pv_done"], b * NS + n - NPT + 1)
                    act.activation(pt[:, n % NPT, :], ring[:, 2 + n % 2, :], ACT.Exp, scale=float(HD0) ** -0.5).then_inc(sm["exp_done"], 1)

                def copy_out(b, g, has):
                    act.wait_ge(sm["pv_done"], b * NS + GH * TT * (g + 1))
                    if not (has["first"] and g < 2):
                        act.wait_ge(sm["ot_done"], b * NG + g - 1)
                    act.activation(os_[:, g % 2, :], og[:, g % 2, :], ACT.Identity).then_inc(sm["o_ready"], 1)

                def copy_normed(b):
                    act.wait_ge(sm["of_done"], b + 1)
                    act.activation(of[:, :], t2[:, :], ACT.Identity).then_inc(sm["of_ready"], 1)

                def step(b, u, has):
                    if not has["weighed"]:
                        return
                    for q in range(NQ):
                        for n in range(QB * q, QB * q + QB):
                            exp(b, n)
                        if has["tail"] and q == 2:
                            copy_normed(b - 1)
                        if q and q % GQ == 0:
                            copy_out(b, q // GQ - 1, has)
                    copy_out(b, NG - 1, has)

                act.preload_act_table_set("natural_log_exp_and_others")
                steps(act, step)
                copy_normed(B - 1)

            @block.vector
            def _(dve):
                def rope(s, i, bank):
                    table, out = ((S.cos0, ta), (S.sin0, tb))[i % 2]
                    dve.wait_ge(sm["proj_done"], s * 4 + i + 1)
                    at = 2 * (i % 2) + i // 2
                    dve.scalar_tensor_tensor(out=out[:, i // 2, :], in0=bank, scalar=S.bq[:, at:at + 1], in1=table[:, :],
                                             op0=ALU.add, op1=ALU.mult).then_inc(sm["rope_step"], 1)

                def split(s, i):
                    if i == 0:
                        dve.wait_ge(sm["rope_step"], s * 4 + 4)
                        dve.tensor_tensor(qk, ta, tb, ALU.add).then_inc(sm["q_ready"], 1)
                    elif i == 1:
                        dve.wait_ge(sm["q_ready"], s + 1)
                        if not (isinstance(s, int) and s == 0):
                            dve.wait_ge(sm["spilled"], s * NP * 16)
                        dve.tensor_copy(parts[:, 0, :, :], qk).then_inc(sm["parts_step"], 1)
                    elif i == 2:
                        dve.wait_ge(sm["parts_step"], s * 4 + 1)
                        dve.tensor_tensor(rest, qk, parts[:, 0, :, :], ALU.subtract).then_inc(sm["parts_step"], 1)
                    elif i == 3:
                        dve.wait_ge(sm["parts_step"], s * 4 + 2)
                        dve.tensor_copy(parts[:, 1, :, :], rest).then_inc(sm["parts_step"], 1)
                    else:
                        dve.wait_ge(sm["parts_step"], s * 4 + 3)
                        dve.tensor_tensor(parts[:, 2, :, :], rest, parts[:, 1, :, :], ALU.subtract).then_inc(sm["parts_step"], 1)

                def maximum(a, n):
                    h, c = n // TT, n % TT
                    dve.wait_ge(sm["score_done"], a * NS + n + 1)
                    dve.tensor_reduce(mx[:, h // HH, c, h % HH:h % HH + 1], ring[:, n % 2, :], AX_X, ALU.max,
                                      negate=True).then_inc(sm["max_ready"], 1)

                def split_maxima(s, half, i, first):
                    k = s * 12 + 6 * half
                    if i == 0:
                        dve.wait_ge(sm["maxt_done"], s * 2 + half + 1)
                        if not first:
                            dve.wait_ge(sm["rows_ready"], (s * 2 + half) * 16 * NP)
                        op = dve.tensor_copy(mb[0:HH, :], t2[0:HH, :])
                    elif i == 1:
                        dve.wait_ge(sm["part_step"], k + 1)
                        op = dve.tensor_tensor(rem[:, 0, :], t2[0:HH, :], mb[0:HH, :], ALU.subtract)
                    elif i == 2:
                        dve.wait_ge(sm["part_step"], k + 2)
                        op = dve.tensor_copy(mid[:, :], rem[:, 0, :])
                    elif i == 3:
                        dve.wait_ge(sm["part_step"], k + 3)
                        op = dve.tensor_copy(mb[32:32 + HH, :], mid[:, :])
                    elif i == 4:
                        op = dve.tensor_tensor(rem[:, 1, :], rem[:, 0, :], mid[:, :], ALU.subtract)
                    else:
                        dve.wait_ge(sm["part_step"], k + 5)
                        op = dve.tensor_copy(mb[64:64 + HH, :], rem[:, 1, :])
                    op.then_inc(sm["part_step"], 1)

                def invert_sums(b, g):
                    dve.wait_ge(sm["ot_done"], b * NG + g + 1)
                    t = t1[:, :].rearrange("p (c j m) -> p c j m", c=TT, j=GH)
                    dve.reciprocal(rc[:, :, :], t[:, :, :, HD0]).then_inc(sm["onorm_step"], 1)

                def normalize(b, g):
                    dve.wait_ge(sm["onorm_step"], b * 8 + 2 * g + 1)
                    t = t1[:, :].rearrange("p (c j m) -> p c j m", c=TT, j=GH)
                    o = on[:, :, GH * HD0 * g:GH * HD0 * (g + 1)].rearrange("p c (j d) -> p c j d", j=GH)
                    dve.tensor_tensor(o, t[:, :, :, 0:HD0], rc[:, :, :].unsqueeze(3).broadcast_to([P, TT, GH, HD0]),
                                      ALU.mult).then_inc(sm["onorm_step"], 1)

                def gate(b):
                    dve.wait_ge(sm["y_done"], b + 1)
                    dve.tensor_scalar(tx[:, :], t2[:, :], S.bo0[:, 0:1], S.mod[:, 0, 2, bass.ds(b, 1)], ALU.add,
                                      ALU.mult).then_inc(sm["gated"], 1)

                def add_gated(b):
                    dve.wait_ge(sm["gated"], b + 1)
                    dve.tensor_tensor(S.xr[:, b, :], S.xr[:, b, :], tx[:, :], ALU.add)

                def add_bias(a, u):
                    dve.wait_ge(sm["v_done"], a + 1)
                    dve.tensor_tensor(vv[:, u, :, :, 0:HD0], t1[:, :].rearrange("p (c h d) -> p c h d", c=TT, h=H0),
                                      S.bv0[:, :].rearrange("p (h d) -> p h d", h=H0).unsqueeze(1).broadcast_to([P, TT, H0, HD0]),
                                      ALU.add).then_inc(sm["v_ready"], 1)

                def step(b, u, has):
                    for n in range(NS):
                        if has["maxima"]:
                            maximum(b + 1, n)
                        if has["weighed"]:
                            if n in (3, 5, 7, 9, 10, 12):
                                split_maxima(b, 1, (3, 5, 7, 9, 10, 12).index(n), False)
                            elif n in (30, 45, 61):
                                invert_sums(b, (n - 30) // (QB * GQ - 1))
                            elif n in (32, 47, 63):
                                normalize(b, (n - 32) // (QB * GQ - 1))
                        if has["tail"]:
                            if n == 4:
                                invert_sums(b - 1, NG - 1)
                            elif n == 6:
                                normalize(b - 1, NG - 1)
                            elif n == 21:
                                gate(b - 1)
                            elif n == 22:
                                add_gated(b - 1)
                        if has["maxima"]:
                            if n == 17:
                                add_bias(b + 1, 1 - u)
                            elif n in (50, 52, 54, 56, 57, 59):
                                split_maxima(b + 1, 0, (50, 52, 54, 56, 57, 59).index(n), not has["weighed"])
                        if has["prepared"]:
                            if n in (25, 29, 33, 37):
                                rope(b + 2, (n - 25) // QB, t2[:, :])
                            elif n in (39, 41, 43, 46, 48):
                                split(b + 2, (39, 41, 43, 46, 48).index(n))

                dve.memset(ones[:, :], 1.0).then_inc(sm["ones_set"], 1)
                for i in range(4):
                    rope(0, i, ring[:, i, :])
                for i in range(5):
                    split(0, i)
                dve.wait_ge(sm["zeroed"], 2)
                steps(dve, step)
                invert_sums(B - 1, NG - 1)
                normalize(B - 1, NG - 1)
                gate(B - 1)
                add_gated(B - 1)


def mix_stage(core, A, w, bias, loaded):
    nc, S = core.nc, core
    mixed, step, done = core.sem("mix_done"), core.sem("mix_step"), core.sem("mix_added")
    with ExitStack() as ctx:
        tmp = core.sb(ctx, "mix_tmp", [P, 4, T])
        pm = core.ps(ctx, "mix_ps", [P, 4, BANK])
        with nc.Block() as block:
            @block.tensor
            def _(pe):
                pe.wait_ge(loaded, 32)
                for b in range(B):
                    if b >= 4:
                        pe.wait_ge(step, b - 3)
                    pe.matmul(pm[:, b % 4, :], w[:, :], S.xa[:, b, PADW:], start=True, stop=True).then_inc(mixed, 1)

            @block.vector
            def _(dve):
                dve.wait_ge(loaded, 32)
                for b in range(B):
                    dve.wait_ge(mixed, b + 1)
                    dve.scalar_tensor_tensor(out=tmp[:, b % 4, :], in0=pm[:, b % 4, :], scalar=bias[:, 0:1],
                                             in1=S.xa[:, b, PADW:], op0=ALU.add, op1=ALU.add).then_inc(step, 1)
                    dve.wait_ge(step, b + 1)
                    dve.tensor_tensor(S.h[:, b, :], S.h[:, b, :], tmp[:, b % 4, :], ALU.add).then_inc(done, 1)


def router_stage(core, w, b1, b2, low, loaded, comb, b1t, b2t):
    nc, S = core.nc, core
    logits, biases, step = core.sem("rt_logits"), core.sem("rt_biases"), core.sem("rt_step")
    exp_done, turned, taken = core.sem("rt_exp"), core.sem("rt_turned"), core.sem("rt_taken")
    zeroed = core.sem("rt_zeroed")
    N = B * TT
    with ExitStack() as ctx:
        pr = core.sb(ctx, "rt_probs", [P, N, E0])
        mx, sm = core.sb(ctx, "rt_max", [P, N]), core.sb(ctx, "rt_sum", [P, N])
        gt, eq = core.sb(ctx, "rt_gt", [P, N, E0 * E0]), core.sb(ctx, "rt_eq", [P, N, E0 * E0])
        rank = core.sb(ctx, "rt_rank", [P, N, E0])
        part = core.sb(ctx, "rt_part", [P, 2, N, E0], BF16)
        parts = core.sb(ctx, "rt_parts", [P, N, 96])
        pl = core.ps(ctx, "rt_pl", [P, BANK])
        pb = core.ps(ctx, "rt_pb", [P, BANK])
        pt = core.ps(ctx, "rt_pt", [P, 4, BANK])
        with nc.Block() as block:
            @block.tensor
            def _(pe):
                pe.wait_ge(loaded, 64)
                for n in range(N):
                    b, c = n // TT, n % TT
                    mm = pe.matmul(pl[:, E0 * n:E0 * n + E0], S.xa[:, b, PADW + P * c:PADW + P * c + P], w[:, :],
                                   start=True, stop=True)
                mm.then_inc(logits, 1)
                pe.transpose(pb[:, 0:32], b1[:, :], S.ident[0:32, 0:32])
                pe.transpose(pb[:, 32:40], b2[:, :], S.ident[0:8, 0:8]).then_inc(biases, 1)
                pe.wait_ge(step, 19)
                for b in range(B):
                    if b >= 4:
                        pe.wait_ge(taken, b - 3)
                    for c in range(TT):
                        tr = pe.transpose(pt[0:96, b % 4, P * c:P * c + P], parts[:, TT * b + c, :], S.ident[:, :])
                    tr.then_inc(turned, 1)

            @block.scalar
            def _(act):
                act.preload_act_table_set("natural_log_exp_and_others")
                act.wait_ge(step, 2)
                act.activation(pr[:, :, :], pr[:, :, :], ACT.Exp).then_inc(exp_done, 1)
                for b in range(B):
                    act.wait_ge(turned, b + 1)
                    act.activation(comb[:, b, :], pt[0:96, b % 4, :], ACT.Identity).then_inc(taken, 1)

            @block.gpsimd
            def _(pool):
                pool.memset(parts[:, :, :], 0.0).then_inc(zeroed, 1)

            @block.vector
            def _(dve):
                n = 0

                def ordered(ins):
                    nonlocal n
                    n += 1
                    ins.then_inc(step, 1)
                    dve.wait_ge(step, n)

                lg = pl[:, 0:N * E0].rearrange("p (n e) -> p n e", e=E0)

                def wide(ap):
                    return ap[:, :].unsqueeze(2).broadcast_to([P, N, E0])

                def pairs(ap):
                    return ap[:, :, :].rearrange("p n (e o) -> p n e o", e=E0)

                def by_expert():
                    return pr[:, :, :].unsqueeze(3).broadcast_to([P, N, E0, E0])

                def by_other():
                    return pr[:, :, :].unsqueeze(2).broadcast_to([P, N, E0, E0])

                dve.wait_ge(logits, 1)
                ordered(dve.tensor_reduce(mx[:, :], lg, AX_X, ALU.max))
                ordered(dve.tensor_tensor(pr[:, :, :], lg, wide(mx), ALU.subtract))
                dve.wait_ge(exp_done, 1)
                ordered(dve.tensor_reduce(sm[:, :], pr[:, :, :], AX_X, ALU.add))
                ordered(dve.reciprocal(sm[:, :], sm[:, :]))
                ordered(dve.tensor_tensor(pr[:, :, :], pr[:, :, :], wide(sm), ALU.mult))
                ordered(dve.tensor_tensor(pairs(gt), by_other(), by_expert(), ALU.is_gt))
                ordered(dve.tensor_tensor(pairs(eq), by_other(), by_expert(), ALU.is_equal))
                dve.wait_ge(loaded, 64)
                ordered(dve.tensor_tensor(eq[:, :, :], eq[:, :, :], low[:, :].unsqueeze(1).broadcast_to([P, N, E0 * E0]),
                                          ALU.mult))
                ordered(dve.tensor_tensor(gt[:, :, :], gt[:, :, :], eq[:, :, :], ALU.add))
                ordered(dve.tensor_reduce(rank[:, :, :], pairs(gt), AX_X, ALU.add))
                ordered(dve.tensor_scalar(rank[:, :, :], rank[:, :, :], 2.0, None, ALU.is_lt))
                ordered(dve.tensor_tensor(pr[:, :, :], pr[:, :, :], rank[:, :, :], ALU.mult))
                dve.wait_ge(zeroed, 1)
                ordered(dve.tensor_copy(part[:, 0, :, :], pr[:, :, :]))
                ordered(dve.tensor_copy(parts[:, :, 0:E0], part[:, 0, :, :]))
                ordered(dve.tensor_tensor(pr[:, :, :], pr[:, :, :], part[:, 0, :, :], ALU.subtract))
                ordered(dve.tensor_copy(part[:, 1, :, :], pr[:, :, :]))
                ordered(dve.tensor_copy(parts[:, :, 32:32 + E0], part[:, 1, :, :]))
                ordered(dve.tensor_tensor(pr[:, :, :], pr[:, :, :], part[:, 1, :, :], ALU.subtract))
                ordered(dve.tensor_copy(parts[:, :, 64:64 + E0], pr[:, :, :]))
                dve.wait_ge(biases, 1)
                dve.tensor_copy(b1t[:, :], pb[:, 0:32])
                dve.tensor_copy(b2t[:, :], pb[:, 32:40])


def experts_stage(core, comb, w1, w2, b1t, b2t):
    nc, S = core.nc, core
    FC = F0 // P
    NH = E0 * FC
    sm = {n: core.sem("ex_" + n) for n in "h_done h_ready y_done c_done c_ready y_ready acc_ready x_ready".split()}
    with ExitStack() as ctx:
        hs = core.sb(ctx, "ex_hs", [P, 2 * FC, T])
        cs = core.sb(ctx, "ex_cs", [P, 2, T])
        ys = core.sb(ctx, "ex_ys", [P, 2, T])
        acc = core.sb(ctx, "ex_acc", [P, T])
        ph = core.ps(ctx, "ex_ph", [P, 4, BANK])
        py = core.ps(ctx, "ex_py", [P, 2, BANK])
        pc = core.ps(ctx, "ex_pc", [P, 2, BANK])
        with nc.Block() as block:
            @block.tensor
            def _(pe):
                pe.wait_ge(S.experts_loaded, 32)
                with pe.Fori(0, B) as b:
                    def up(e):
                        for f in range(FC):
                            n = e * FC + f
                            pe.wait_ge(sm["h_ready"], b * NH + n + 1)
                            pe.matmul(ph[:, n % 4, :], w1[:, e, P * f:P * f + P], S.xa[:, b, PADW:], start=True,
                                      stop=True).then_inc(sm["h_done"], 1)
                        pe.wait_ge(sm["c_ready"], b * E0 + e + 1)
                        pe.matmul(pc[:, e % 2, :], S.pick[0:96, e, :], comb[:, b, :], start=True,
                                  stop=True).then_inc(sm["c_done"], 1)

                    def down(e):
                        pe.wait_ge(sm["y_ready"], b * E0 + e + 1)
                        for f in range(FC):
                            n = e * FC + f
                            pe.wait_ge(sm["h_ready"], b * NH + n + 5)
                            mm = pe.matmul(py[:, e % 2, :], w2[:, e, f, :], hs[:, n % (2 * FC), :], start=(f == 0),
                                           stop=(f == FC - 1))
                        mm.then_inc(sm["y_done"], 1)

                    for e in range(E0 + 1):
                        if e < E0:
                            up(e)
                        if e:
                            down(e - 1)

            @block.scalar
            def _(act):
                act.preload_act_table_set("silu_and_others")
                act.sem_inc(sm["h_ready"], 4)
                act.sem_inc(sm["c_ready"], 2)
                with act.Fori(0, B) as b:
                    for e in range(E0):
                        act.wait_ge(sm["y_done"], b * E0 + e + 1)
                        for f in range(FC):
                            n = e * FC + f
                            act.wait_ge(sm["h_done"], b * NH + n + 1)
                            act.activation(hs[:, n % (2 * FC), :], ph[:, n % 4, :], ACT.Silu,
                                           bias=b1t[:, n:n + 1]).then_inc(sm["h_ready"], 1)
                        act.wait_ge(sm["c_done"], b * E0 + e + 1)
                        act.wait_ge(sm["y_ready"], b * E0 + e + 1)
                        act.activation(cs[:, e % 2, :], pc[:, e % 2, :], ACT.Identity).then_inc(sm["c_ready"], 1)

            @block.vector
            def _(dve):
                dve.sem_inc(sm["y_ready"], 2)
                dve.sem_inc(sm["y_done"], 2)
                dve.sem_inc(sm["x_ready"], 1)
                with dve.Fori(0, B) as b:
                    for e in range(E0):
                        dve.wait_ge(sm["y_done"], b * E0 + e + 3)
                        dve.wait_ge(sm["c_ready"], b * E0 + e + 3)
                        dve.wait_ge(sm["acc_ready"], b * E0 + e + 1)
                        dve.scalar_tensor_tensor(out=ys[:, e % 2, :], in0=py[:, e % 2, :], scalar=b2t[:, e:e + 1],
                                                 in1=cs[:, e % 2, :], op0=ALU.add, op1=ALU.mult).then_inc(sm["y_ready"], 1)
                    dve.wait_ge(sm["acc_ready"], b * E0 + E0 + 2)
                    dve.scalar_tensor_tensor(out=S.xr[:, b, :], in0=acc[:, :], scalar=S.mod[:, 0, 5, bass.ds(b, 1)],
                                             in1=S.xr[:, b, :], op0=ALU.mult, op1=ALU.add).then_inc(sm["x_ready"], 1)

            @block.gpsimd
            def _(pool):
                pool.sem_inc(sm["acc_ready"], 2)
                with pool.Fori(0, B) as b:
                    pool.wait_ge(sm["x_ready"], b + 1)
                    for e in range(E0):
                        pool.wait_ge(sm["y_ready"], b * E0 + e + 3)
                        if e:
                            pool.wait_ge(sm["acc_ready"], b * E0 + e + 2)
                        pool.tensor_tensor(acc[:, :], acc[:, :] if e else S.h[:, b, :], ys[:, e % 2, :],
                                           ALU.add).then_inc(sm["acc_ready"], 1)


def ffn0(core, A, C):
    nc, S = core.nc, core
    with ExitStack() as ctx:
        w1 = core.sb(ctx, "moe_w1", [P, E0, F0])
        w2 = core.sb(ctx, "moe_w2", [P, E0, F0 // P, P])
        comb = core.sb(ctx, "moe_comb", [96, B, T], BF16)
        b1t, b2t = core.sb(ctx, "moe_b1", [P, 32]), core.sb(ctx, "moe_b2", [P, 8])
        gb = core.sb(ctx, "moe_norms", [P, 4])
        mix_w, mix_b = core.sb(ctx, "mix_w", [P, P]), core.sb(ctx, "mix_b", [P, 1])
        rw, low = core.sb(ctx, "rt_w", [P, E0]), core.sb(ctx, "rt_lower", [P, E0 * E0])
        b1, b2 = core.sb(ctx, "rt_b1", [4 * E0, P]), core.sb(ctx, "rt_b2", [E0, P])
        mix_loaded, router_loaded = core.sem("mix_loaded"), core.sem("rt_loaded")
        S.experts_loaded, gains = core.sem("experts_loaded"), core.sem("gains_loaded")
        def loads(block):
            @block.sync
            def _(sp):
                for i, n in enumerate(("g1", "be1", "g2", "be2")):
                    sp.dma_start(gb[:, i:i + 1], column(A["L0_ffn_" + n])).then_inc(gains, 16)
                sp.dma_start(mix_w[:, :], A["L0_ffn_mix_w"]).then_inc(mix_loaded, 16)
                sp.dma_start(mix_b[:, :], column(A["L0_ffn_mix_b"])).then_inc(mix_loaded, 16)
                sp.dma_start(rw[:, :], A["L0_ffn_router_w"]).then_inc(router_loaded, 16)
                sp.dma_start(b1[:, :], A["L0_ffn_b1"].rearrange("e (c p) -> (e c) p", p=P)).then_inc(router_loaded, 16)
                sp.dma_start(b2[:, :], A["L0_ffn_b2"]).then_inc(router_loaded, 16)
                sp.dma_start(low[:, :], C["lower"]).then_inc(router_loaded, 16)
                sp.dma_start(w1[:, :, :], A["L0_ffn_w1"].rearrange("e d f -> d e f")).then_inc(S.experts_loaded, 16)
                sp.dma_start(w2[:, :, :, :], A["L0_ffn_w2"].rearrange("e (c p) d -> p e c d", p=P)).then_inc(S.experts_loaded, 16)
                sp.wait_ge(gains, 64)

        norm_stage(core, lambda b: S.xr[:, b, :], lambda b: S.h[:, b, :],
                   lambda b: S.mod[:, 0, 4, b:b + 1], lambda b: S.mod[:, 0, 3, b:b + 1], beside=loads)(B)
        norm_stage(core, lambda b: S.h[:, b, :], lambda b: S.xa[:, b, PADW:], lambda b: gb[:, 0:1], lambda b: gb[:, 1:2])(2 * B)
        mix_stage(core, A, mix_w, mix_b, mix_loaded)
        norm_stage(core, lambda b: S.h[:, b, :], lambda b: S.xa[:, b, PADW:], lambda b: gb[:, 2:3], lambda b: gb[:, 3:4])(3 * B)
        router_stage(core, rw, b1, b2, low, router_loaded, comb, b1t, b2t)
        experts_stage(core, comb, w1, w2, b1t, b2t)


def attention1(core, A, C):
    nc, S = core.nc, core
    sm = {n: core.sem("a1_" + n) for n in ("loaded loaded_cast trig_step trig_ready sin_done hs_ready proj_done act_ready dve_ready s_done v_done "
                                           "max_ready sub_ready exp_done sum_ready rsum_ready norm_ready t_done t_ready "
                                           "v_ready o_done o_ready y_done gated x_ready start setup").split()}
    NB = T // TB
    NG = NB // 4
    SCALE = float(HD1) ** -0.5
    TWO_PI = 2 * np.pi
    TP_HI = float(np.float32(6.28125))
    TP_LO = float(TWO_PI - 6.28125)
    MAGIC = 1.5 * 2.0 ** 23
    with ExitStack() as ctx:
        wq, wk, wv = (core.sb(ctx, "a1_w" + n, [P, H1 * HD1]) for n in "qkv")
        wo = core.sb(ctx, "a1_wo", [P, H1, P])
        bqk = core.sb(ctx, "a1_bqk", [P, 2, H1])
        bo = core.sb(ctx, "a1_bo", [P, 1])
        bv = core.sb(ctx, "a1_bv", [P, HD1])
        mask = core.sb(ctx, "a1_mask", [P, P], BF16)
        mask4 = core.sb(ctx, "a1_mask4", [P, 4, P], BF16)
        ph = core.sb(ctx, "a1_phase", [P, H1])
        rnd = core.sb(ctx, "a1_round", [P, 2, H1])
        red = core.sb(ctx, "a1_reduced", [P, 2, H1])
        trig = core.sb(ctx, "a1_trig", [P, 2, H1])
        tbias = core.sb(ctx, "a1_tbias", [P, 2, H1])
        hs = core.sb(ctx, "a1_hs", [P, T])
        qp = core.sb(ctx, "a1_q", [P, 2, NB, H1, TB])
        kp = core.sb(ctx, "a1_k", [P, 2, NB, H1, TB])
        vs = core.sb(ctx, "a1_v", [P, 2, 4, HD1])
        pr = core.sb(ctx, "a1_p", [P, 2, 4, P])
        pn = core.sb(ctx, "a1_pn", [P, 2, 4, P])
        at = core.sb(ctx, "a1_pt", [P, 2, 4, P])
        mx, su, rs = (core.sb(ctx, "a1_" + n, [P, 2, 4]) for n in ("max", "sum", "rsum"))
        ot = core.sb(ctx, "a1_o", [P, H1, T])
        tx = core.sb(ctx, "a1_tx", [P, T])

        def loads(block):
            @block.sync
            def _(sp):
                for n, ap in (("L1_attn_Wq", wq), ("L1_attn_Wk", wk), ("L1_attn_Wv", wv)):
                    sp.dma_start(ap[:, :], A[n]).then_inc(sm["loaded"], 16)
                sp.dma_start(wo[:, :, :], A["L1_attn_Wo"].rearrange("(h d) o -> d h o", d=HD1)).then_inc(sm["loaded"], 16)
                with nc.allow_non_contiguous_dma("small vectors turned onto the partitions"):
                    sp.dma_start(bqk[:, 0, :], A["L1_attn_bq"].rearrange("(h d) -> d h", d=HD1)).then_inc(sm["loaded"], 16)
                    sp.dma_start(bqk[:, 1, :], A["L1_attn_bk"].rearrange("(h d) -> d h", d=HD1)).then_inc(sm["loaded"], 16)
                    sp.dma_start(ph[:, :], A["L1_attn_phase"].rearrange("h d -> d h")).then_inc(sm["loaded"], 16)
                sp.dma_start(bo[:, :], column(A["L1_attn_bo"])).then_inc(sm["loaded"], 16)
                for g in range(H1):
                    sp.dma_start(bv[TB * g:TB * g + TB, :],
                                 A["L1_attn_bv"][HD1 * g:HD1 * g + HD1].partition_broadcast(TB)).then_inc(sm["loaded"], 16)

            @block.gpsimd
            def _(pool):
                pool.dma_start(mask[:, :], C["mask1"]).then_inc(sm["loaded_cast"], 16)

        NLOAD = 16 * 12
        norm_stage(S, lambda b: S.xr[:, b, :], lambda b: S.h[:, b, :],
                   lambda b: S.mod[:, 1, 1, b:b + 1], lambda b: S.mod[:, 1, 0, b:b + 1], beside=loads)(4 * B)
        ring = core.ps(ctx, "a1_ring", [P, 4, BANK])
        ps = core.ps(ctx, "a1_s", [P, 2, BANK])
        po = core.ps(ctx, "a1_po", [P, BANK])
        py = core.ps(ctx, "a1_py", [P, BANK])
        with nc.Block() as block:
            @block.gpsimd
            def _(pool):
                pool.wait_ge(sm["loaded_cast"], 16)
                with pool.Fori(0, B) as b:
                    pool.wait_ge(sm["v_done"], b * NG + 1)
                    pool.tensor_copy(hs[:, :], S.h[:, b, :]).then_inc(sm["hs_ready"], 1)
                    for g in range(NG):
                        pool.wait_ge(sm["rsum_ready"], b * NG + g + 1)
                        pool.wait_ge(sm["t_done"], b * NG + g + 1)
                        pool.tensor_tensor(pn[:, g % 2, :, :], pr[:, g % 2, :, :],
                                           rs[:, g % 2, :].unsqueeze(2).broadcast_to([P, 4, P]),
                                           ALU.mult).then_inc(sm["norm_ready"], 1)

            @block.tensor
            def _(pe):
                pe.wait_ge(sm["loaded"], NLOAD)
                pe.wait_ge(sm["setup"], 1)
                pe.sem_inc(sm["v_done"], 1)
                pe.sem_inc(sm["t_done"], 2)
                with pe.Fori(0, B) as b:
                    pe.wait_ge(sm["hs_ready"], b + 1)
                    for n in range(2 * H1):
                        h, k = n // 2, n % 2
                        w = wk if k else wq
                        if h >= 2:
                            pe.wait_ge(sm["dve_ready" if k else "act_ready"], b * 2 * H1 + 2 * (h - 1))
                        elif k:
                            pe.wait_ge(sm["t_ready"], b * NG + 1)
                        else:
                            pe.wait_ge(sm["v_ready"], b * NG + 1)
                        pe.matmul(ring[:, 2 * k + h % 2, :], w[:, HD1 * h:HD1 * h + HD1], hs[:, :], start=True,
                                  stop=True).then_inc(sm["proj_done"], 1)

                    def scores(g):
                        pe.wait_ge(sm["sub_ready"], b * NG + g + 1)
                        if g == 0:
                            pe.wait_ge(sm["act_ready"], b * 2 * H1 + 2 * H1)
                            pe.wait_ge(sm["dve_ready"], b * 2 * H1 + 2 * H1)
                        pe.matmul(ps[:, g % 2, :], S.identb[:, :], mask4[:, :, :].rearrange("p n m -> p (n m)"), start=True,
                                  stop=False, skip_group_check=True)
                        for i in range(4):
                            for part in range(2):
                                mm = pe.matmul(ps[:, g % 2, P * i:P * i + P],
                                               qp[:, part, 4 * g + i, :, :].rearrange("p h t -> p (h t)"),
                                               kp[:, part, 4 * g + i, :, :].rearrange("p h t -> p (h t)"),
                                               start=False, stop=(part == 1), skip_group_check=True)
                        mm.then_inc(sm["s_done"], 1)
                        if g >= 2:
                            pe.wait_ge(sm["v_ready"], b * NG + g)
                        for h in range(H1):
                            for i in range(4):
                                at_ = TB * (4 * g + i)
                                mm = pe.matmul(ring[TB * h:TB * h + TB, g % 2, P * i:P * i + P], hs[:, at_:at_ + TB],
                                               wv[:, HD1 * h:HD1 * h + HD1], start=True, stop=True)
                        mm.then_inc(sm["v_done"], 1)

                    def turn(g):
                        pe.wait_ge(sm["norm_ready"], b * NG + g + 3)
                        if g >= 2:
                            pe.wait_ge(sm["t_ready"], b * NG + g)
                        for i in range(4):
                            tr = pe.transpose(ring[:, 2 + g % 2, P * i:P * i + P], pn[:, g % 2, i, :], S.ident[:, :])
                        tr.then_inc(sm["t_done"], 1)

                    def weighted(g):
                        pe.wait_ge(sm["t_ready"], b * NG + g + 2)
                        pe.wait_ge(sm["v_ready"], b * NG + g + 2)
                        pe.wait_ge(sm["o_ready"], b * NG + g + 1)
                        for i in range(4):
                            mm = pe.matmul(po[:, P * i:P * i + P], vs[:, g % 2, i, :], at[:, g % 2, i, :], start=True, stop=True)
                        mm.then_inc(sm["o_done"], 1)

                    for s in range(NG + 2):
                        if s < NG:
                            scores(s)
                        if 1 <= s < NG:
                            turn(s - 1)
                        if s >= 2:
                            weighted(s - 2)
                        if s == NG:
                            turn(s - 1)
                    pe.wait_ge(sm["o_ready"], b * NG + NG + 1)
                    pe.wait_ge(sm["x_ready"], b + 1)
                    for j in range(H1):
                        mm = pe.matmul(py[:, :], wo[:, j, :], ot[:, :, :].rearrange("p h (r j) -> p h r j", j=H1)[:, :, :, j],
                                       start=(j == 0), stop=(j == H1 - 1))
                    mm.then_inc(sm["y_done"], 1)

            @block.scalar
            def _(act):
                act.sem_inc(sm["t_ready"], 1)
                act.wait_ge(sm["trig_ready"], 1)
                act.activation(trig[:, :, :], red[:, :, :], ACT.Sin).then_inc(sm["sin_done"], 1)
                act.wait_ge(sm["setup"], 1)
                act.preload_act_table_set("natural_log_exp_and_others")
                with act.Fori(0, B) as b:
                    for h in range(H1):
                        act.wait_ge(sm["proj_done"], b * 2 * H1 + 2 * h + 1)
                        if h == 0:
                            act.wait_ge(sm["s_done"], b * NG + 1)
                        for part in range(2):
                            act.activation(qp[:, part, :, h, :], ring[:, h % 2, :].rearrange("p (n t) -> p n t", t=TB),
                                           ACT.Identity, bias=tbias[:, part, h:h + 1],
                                           scale=trig[:, part, h:h + 1]).then_inc(sm["act_ready"], 1)
                    for s in range(NG + 1):
                        if s < NG:
                            act.wait_ge(sm["sub_ready"], b * NG + s + 3)
                            act.activation(pr[:, s % 2, :, :], pr[:, s % 2, :, :], ACT.Exp, scale=SCALE).then_inc(sm["exp_done"], 1)
                        if s:
                            g = s - 1
                            act.wait_ge(sm["t_done"], b * NG + g + 3)
                            act.wait_ge(sm["o_done"], b * NG + g + 1)
                            act.activation(at[:, g % 2, :, :].rearrange("p n m -> p (n m)"), ring[:, 2 + g % 2, :],
                                           ACT.Identity).then_inc(sm["t_ready"], 1)

            @block.vector
            def _(dve):
                dve.sem_inc(sm["v_ready"], 1)
                dve.sem_inc(sm["sub_ready"], 2)
                dve.sem_inc(sm["o_ready"], 1)
                dve.sem_inc(sm["x_ready"], 1)
                dve.sem_inc(sm["s_done"], 1)
                dve.sem_inc(sm["o_done"], 2)
                dve.sem_inc(sm["norm_ready"], 2)
                dve.sem_inc(sm["y_done"], 1)
                dve.wait_ge(sm["loaded"], NLOAD)
                n = 0

                def ordered(ins):
                    nonlocal n
                    n += 1
                    ins.then_inc(sm["trig_step"], 1)
                    dve.wait_ge(sm["trig_step"], n)

                for part in range(2):
                    ordered(dve.tensor_scalar(rnd[:, part, :], ph[:, :], 1.0 / TWO_PI, 0.25 if part == 0 else 0.0,
                                              ALU.mult, ALU.add))
                    ordered(dve.tensor_scalar(rnd[:, part, :], rnd[:, part, :], MAGIC, None, ALU.add))
                    ordered(dve.tensor_scalar(rnd[:, part, :], rnd[:, part, :], MAGIC, None, ALU.subtract))
                    ordered(dve.scalar_tensor_tensor(out=red[:, part, :], in0=rnd[:, part, :], scalar=-TP_HI, in1=ph[:, :],
                                                     op0=ALU.mult, op1=ALU.add))
                    ordered(dve.scalar_tensor_tensor(out=red[:, part, :], in0=rnd[:, part, :], scalar=-TP_LO,
                                                     in1=red[:, part, :], op0=ALU.mult, op1=ALU.add))
                    if part == 0:
                        ordered(dve.tensor_scalar(red[:, part, :], red[:, part, :], float(np.pi / 2), None, ALU.add))
                    ordered(dve.tensor_scalar(red[:, part, :], red[:, part, :], 3.1415925, -3.1415925, ALU.min, ALU.max))
                dve.sem_inc(sm["trig_ready"], 1)
                dve.wait_ge(sm["sin_done"], 1)
                for part in range(2):
                    ordered(dve.tensor_tensor(tbias[:, part, :], trig[:, part, :], bqk[:, 0, :], ALU.mult))
                dve.wait_ge(sm["loaded_cast"], 16)
                dve.tensor_copy(mask4[:, :, :], mask[:, :].unsqueeze(1).broadcast_to([P, 4, P])).then_inc(sm["setup"], 1)
                with dve.Fori(0, B) as b:
                    for h in range(H1):
                        dve.wait_ge(sm["proj_done"], b * 2 * H1 + 2 * h + 2)
                        for part in range(2):
                            dve.tensor_scalar(kp[:, part, :, h, :], ring[:, 2 + h % 2, :].rearrange("p (n t) -> p n t", t=TB),
                                              bqk[:, 1, h:h + 1], trig[:, part, h:h + 1], ALU.add,
                                              ALU.mult).then_inc(sm["dve_ready"], 1)
                    for s in range(NG + 2):
                        if s < NG:
                            g, i = s, s % 2
                            dve.wait_ge(sm["s_done"], b * NG + g + 2)
                            S4 = ps[:, i, :].rearrange("p (n m) -> p n m", m=P)
                            dve.tensor_reduce(mx[:, i, :], S4, AX_X, ALU.max).then_inc(sm["max_ready"], 1)
                            dve.wait_ge(sm["max_ready"], b * NG + g + 1)
                            dve.wait_ge(sm["norm_ready"], b * NG + g + 1)
                            dve.tensor_tensor(pr[:, i, :, :], S4, mx[:, i, :].unsqueeze(2).broadcast_to([P, 4, P]),
                                              ALU.subtract).then_inc(sm["sub_ready"], 1)
                            dve.wait_ge(sm["v_done"], b * NG + g + 2)
                            if g >= 2:
                                dve.wait_ge(sm["o_done"], b * NG + g + 1)
                            dve.tensor_tensor(vs[:, i, :, :], ring[:, i, :].rearrange("p (n m) -> p n m", m=HD1),
                                              bv[:, :].unsqueeze(1).broadcast_to([P, 4, HD1]), ALU.add).then_inc(sm["v_ready"], 1)
                            dve.wait_ge(sm["exp_done"], b * NG + g + 1)
                            dve.tensor_reduce(su[:, i, :], pr[:, i, :, :], AX_X, ALU.add).then_inc(sm["sum_ready"], 1)
                            dve.wait_ge(sm["sum_ready"], b * NG + g + 1)
                            dve.reciprocal(rs[:, i, :], su[:, i, :]).then_inc(sm["rsum_ready"], 1)
                        if s >= 2:
                            g = s - 2
                            dve.wait_ge(sm["o_done"], b * NG + g + 3)
                            if g == 0:
                                dve.wait_ge(sm["y_done"], b + 1)
                            dve.tensor_copy(ot[:, :, P * g:P * g + P].rearrange("p h (n t) -> p n h t", t=TB),
                                            po[:, :].rearrange("p (n h t) -> p n h t", n=4, h=H1)).then_inc(sm["o_ready"], 1)
                    dve.wait_ge(sm["y_done"], b + 2)
                    dve.tensor_scalar(tx[:, :], py[:, :], bo[:, 0:1], S.mod[:, 1, 2, bass.ds(b, 1)], ALU.add,
                                      ALU.mult).then_inc(sm["gated"], 1)
                    dve.wait_ge(sm["gated"], b + 1)
                    dve.tensor_tensor(S.xr[:, b, :], S.xr[:, b, :], tx[:, :], ALU.add).then_inc(sm["x_ready"], 1)


NPAIR = H2 // 2
NT = B * TT
NW = P // WIN


class LocalAttention:

    NAMES = ("proj_done sq_ready ss_ready ssmax_ready ln_step rn_ready cos_ready sin_ready add_ready qkn_ready "
             "turn_done q_taken k_taken s_done max_ready sub_ready exp_ready sum_ready rsum_ready pn_ready "
             "v_done v_taken tail_ready pt_done pt_taken o_done o_taken y_done x_ready table_step table_ready").split()

    def __init__(self, core, ctx):
        self.core = core
        self.sm = {n: core.sem("la_" + n) for n in self.NAMES}
        self.xs_ready = [core.sem("la_xs%d_ready" % i) for i in range(TT)]
        sb = lambda name, shape, dt=F32: core.sb(ctx, "la_" + name, shape, dt)
        self.wqkv = sb("wqkv", [P, 3 * INNER])
        self.wo = sb("wo", [P, NPAIR, P])
        self.qks = sb("qks", [P, 2, HD2])
        self.rope = sb("rope", [P, 2, TT, 2, HD2])
        self.cs = sb("cs", [P, 2, TT, 2, HD2])
        self.maskf = sb("maskf", [P, 2, 2 * WIN], BF16)
        self.mask = sb("mask", [P, 2, NPAIR, 2 * WIN], BF16)
        self.xs = sb("xs", [P, TT, P])
        self.work = sb("work", [P, 3, 2, INNER])
        self.sq, self.t1, self.t2 = (self.work[:, i, :, :] for i in range(3))
        self.ss = sb("ss", [P, 2, H2])
        self.rn = sb("rn", [P, 2, H2])
        self.qkn = sb("qkn", [P, 2, INNER])
        self.kt = sb("kt", [P, 2, NPAIR, P + WIN])
        self.qb = sb("qb", [P, NPAIR, NW, 2 * WIN])
        self.pr = sb("pr", [P, 2, NPAIR, 2 * WIN])
        self.pn = sb("pn", [P, 2, NPAIR, 2 * WIN])
        self.mx, self.su, self.rs = (sb(n, [P, 2, NPAIR]) for n in ("max", "sum", "rsum"))
        self.pb = sb("pb", [P, 2, NPAIR // 2, 2, 2, 2 * WIN])
        self.vs = sb("vs", [P, 2, 2, BANK])
        self.vf = sb("vf", [P, 2, BANK])
        self.os = sb("os", [P, NPAIR, P])

    def setup(self, C):
        nc, S, sm = self.core.nc, self.core, self.sm
        loaded, cast, ready = S.sem("la_tables"), S.sem("la_masks"), S.sem("la_zeroed")

        def beside(block):
            @block.sync
            def _(sp):
                for i, n in enumerate(("cos2", "sin2")):
                    sp.dma_start(self.rope[:, i, :, :, :].rearrange("p t k d -> p (t k d)"), C[n]).then_inc(loaded, 16)
                sp.wait_ge(loaded, 32)
                sp.wait_ge(ready, 1)
                sp.dma_start(self.vf[96:P, :, :], self.vs[96:P, 1, :, :]).then_inc(sm["tail_ready"], 16)

            @block.gpsimd
            def _(pool):
                pool.dma_start(self.maskf[:, :, :].rearrange("p n m -> p (n m)"), C["mask2"]).then_inc(cast, 16)
                pool.memset(self.qb[:, :, :, :].rearrange("p a b c -> p (a b c)"), 0.0)
                pool.memset(self.pb[:, :, :, :, :, :].rearrange("p a b c d e -> p (a b c d e)"), 0.0)
                pool.memset(self.vf[:, :, :].rearrange("p a b -> p (a b)"), 0.0)
                pool.memset(self.vs[:, :, :, :].rearrange("p a b c -> p (a b c)"), 0.0).then_inc(ready, 1)
                pool.memset(self.kt[:, 0, :, 0:WIN], 0.0)
                pool.wait_ge(cast, 16)

        def counts(dve):
            dve.wait_ge(cast, 16)
            dve.tensor_copy(self.mask[:, :, :, :], self.maskf[:, :, :].unsqueeze(2).broadcast_to([P, 2, NPAIR, 2 * WIN]))
            for n in ("qkn_ready", "cos_ready", "o_taken", "add_ready"):
                dve.sem_inc(sm[n], 2)
            for n in ("proj_done", "s_done", "pt_done", "o_done", "y_done", "pt_taken", "x_ready", "sin_ready", "ssmax_ready",
                      "rn_ready", "pn_ready", "turn_done"):
                dve.sem_inc(sm[n], 4)

        return beside, counts

    def layer(self, layer, weights_count, src, dst, load_next):
        nc, S, sm = self.core.nc, self.core, self.sm
        me = self

        def G(n):
            return layer * NT + n

        def steps(eng, before, step, after):
            before()
            with eng.Fori(0, B - 1) as b:
                for i in range(TT):
                    step(b * TT + i, b, i, True, True, True, True)
            for i in range(TT):
                step((B - 1) * TT + i, B - 1, i, False, i < TT - 3, i < TT - 2, i < TT - 1)
            after()

        with ExitStack() as ctx:
            pa = S.ps(ctx, "la_pa", [P, 4, BANK])
            ring = S.ps(ctx, "la_ring", [P, 4, BANK])
            with nc.Block() as block:
                @block.tensor
                def _(pe):
                    def project(n, b, i, k):
                        if k == 0:
                            pe.wait_ge(me.xs_ready[i], 32 * (layer * B + b) + 32)
                            pe.wait_ge(sm["x_ready"], G(n) + 1)
                        pe.wait_ge(sm["sin_ready"], 2 * G(n - 1) + k + 1 + 4)
                        for half in range(2):
                            at = INNER * k + BANK * half
                            mm = pe.matmul(pa[:, 2 * k + half, :], me.xs[:, i, :], me.wqkv[:, at:at + BANK], start=True, stop=True)
                        mm.then_inc(sm["proj_done"], 1)

                    def turn(n, steady):
                        for u in range(4):
                            if u % 2 == 0:
                                pe.wait_ge(sm["qkn_ready"], 2 * G(n) + u // 2 + 1 + 2)
                            if steady:
                                if u < 2:
                                    pe.wait_ge(sm["sub_ready"], 2 * G(n - 1) + u + 1)
                                    pe.wait_ge(sm["o_taken"], 2 * (G(n) - 2) + u + 1 + 2)
                                elif u == 2:
                                    pe.wait_ge(sm["pt_taken"], 4 * (G(n) - 2) + 4 + 4)
                            for j in range(4):
                                at = (u % 2) * BANK + P * j
                                tr = pe.transpose(ring[:, u, P * j:P * j + P], me.qkn[:, u // 2, at:at + P], S.ident[:, :])
                            tr.then_inc(sm["turn_done"], 1)

                    def score(n, i, half):
                        s = i % 2
                        for u in half:
                            pe.wait_ge(sm["q_taken"], 4 * G(n) + 4)
                            pe.wait_ge(sm["k_taken"], 2 * G(n) + 2)
                            first = 1 if (i == 0 and u == 0) else 0
                            pe.matmul(ring[:, u, :], S.identb[:, :], me.mask[:, first, :, :].rearrange("p n m -> p (n m)"),
                                      start=True, stop=False, skip_group_check=True)
                            for w in (2 * u, 2 * u + 1):
                                r = 64 * (w % 2)
                                for p in range(NPAIR):
                                    mm = pe.matmul(ring[r:r + 64, u, 64 * p:64 * p + 64], me.qb[:, p, w, :],
                                                   me.kt[:, s, p, WIN * w:WIN * w + 64], start=False, stop=True,
                                                   skip_group_check=True)
                            mm.then_inc(sm["s_done"], 1)

                    def values(n, i, follows):
                        for x in range(2):
                            if follows:
                                pe.wait_ge(sm["k_taken"], 2 * G(n + 1) + 1 + x)
                            else:
                                pe.wait_ge(sm["pt_taken"], 4 * G(n - 1) + 4 + 4)
                            at = 2 * INNER + BANK * x
                            pe.matmul(ring[:, 2 + x, :], me.xs[:, i, :], me.wqkv[:, at:at + BANK], start=True,
                                      stop=True).then_inc(sm["v_done"], 1)

                    def turn_weights(n):
                        for u in range(2):
                            pe.wait_ge(sm["v_taken"], 2 * G(n) + u + 1)
                            pe.wait_ge(sm["pn_ready"], 2 * G(n) + u + 1 + 4)
                            for j in range(NPAIR // 2):
                                tr = pe.transpose(ring[:, 2 + u, P * j:P * j + P],
                                                  me.pn[:, u, 2 * j:2 * j + 2, :].rearrange("p a k -> p (a k)"), S.ident[:, :])
                            tr.then_inc(sm["pt_done"], 1)

                    def weigh(n, i, follows, more3):
                        pe.wait_ge(sm["tail_ready"], 16 * G(n) + 16)
                        for half in range(2):
                            if follows:
                                pe.wait_ge(sm["sub_ready"], 2 * G(n + 1) + half + 1)
                            for u in range(2):
                                v = me.vs[:, i % 2, :, :] if u else me.vf[:, :, :]
                                pe.wait_ge(sm["pt_taken"], 4 * G(n) + 2 * u + 2 + 4)
                                for h in range(2):
                                    for p in range(4 * half, 4 * half + 4):
                                        at, a = 64 * (2 * (p % 4) + h), P * (p % 4)
                                        o = ring[64 * h:64 * h + 64, half, :]
                                        mm = pe.matmul(o[:, a + 64 * u:a + 64 * u + 64], v[:, half, at:at + 64],
                                                       me.pb[:, u, p // 2, p % 2, h, :], start=True, stop=True,
                                                       skip_group_check=True)
                            mm.then_inc(sm["o_done"], 1)
                        if more3:
                            pe.wait_ge(sm["sin_ready"], 2 * G(n + 3) + 1 + 4)
                        else:
                            pe.wait_ge(sm["x_ready"], G(n) + 4)
                        for p in range(NPAIR):
                            if p % 4 == 0:
                                pe.wait_ge(sm["o_taken"], 2 * G(n) + p // 4 + 1 + 2)
                            mm = pe.matmul(pa[:, 0, 0:P], me.wo[:, p, :], me.os[:, p, :], start=(p == 0), stop=(p == NPAIR - 1))
                        mm.then_inc(sm["y_done"], 1)

                    def before():
                        pe.wait_ge(S.weights_a, weights_count)
                        for n in range(3):
                            project(n, 0, n, 0)
                            project(n, 0, n, 1)
                            if n == 1:
                                turn(0, False)
                        score(0, 0, (0, 1))

                    def step(n, b, i, more4, more3, more2, more1):
                        ahead = (n + 3, b + 1 if i + 3 >= TT else b, (i + 3) % TT)
                        if more1:
                            turn(n + 1, True)
                        if more3:
                            project(*ahead, 0)
                        values(n, i, more1)
                        if more1:
                            score(n + 1, (i + 1) % TT, (0,))
                        turn_weights(n)
                        if more1:
                            score(n + 1, (i + 1) % TT, (1,))
                        if more3:
                            project(*ahead, 1)
                        weigh(n, i, more1, more3)

                    steps(pe, before, step, lambda: None)

                @block.sync
                def _(sp):
                    def shift(b, i):
                        for half in range(2):
                            r, at = slice(64 * half, 64 * half + 64), PADW + P * i - half
                            sp.dma_start(me.xs[r, i, :], src[r, b, at:at + P]).then_inc(me.xs_ready[i], 16)

                    def before():
                        for i in range(TT):
                            shift(0, i)
                        with nc.allow_non_contiguous_dma("small vectors turned onto the partitions"):
                            load_next(sp, layer)

                    def step(n, b, i, more4, more3, more2, more1):
                        if more4:
                            sp.wait_ge(sm["v_done"], 2 * G(n) + 2)
                            shift(b + 1, i)
                        sp.wait_ge(sm["o_done"], 2 * G(n) + 2 + 4)
                        sp.dma_start(me.vf[96:P, :, :], me.vs[96:P, i % 2, :, :]).then_inc(sm["tail_ready"], 16)

                    steps(sp, before, step, lambda: None)

                @block.gpsimd
                def _(pool):
                    def add_parts(n):
                        for k in range(2):
                            pool.wait_ge(sm["cos_ready"], 2 * G(n) + k + 1 + 2)
                            pool.wait_ge(sm["sin_ready"], 2 * G(n) + k + 1 + 4)
                            pool.tensor_tensor(me.t1[:, k, :], me.t1[:, k, :], me.t2[:, k, :], ALU.add).then_inc(sm["add_ready"], 1)

                    def scale(n, parts):
                        for k in parts:
                            pool.wait_ge(sm["add_ready"], 2 * G(n) + k + 1 + 2)
                            pool.wait_ge(sm["rn_ready"], 2 * G(n) + k + 1 + 4)
                            pool.wait_ge(sm["turn_done"], 4 * G(n) + 4 if k else 4 * G(n) + 2)
                            pool.tensor_tensor(me.qkn[:, k, :].rearrange("p (h d) -> p h d", h=H2),
                                               me.t1[:, k, :].rearrange("p (h d) -> p h d", h=H2),
                                               me.rn[:, k, :].unsqueeze(2).broadcast_to([P, H2, HD2]),
                                               ALU.mult).then_inc(sm["qkn_ready"], 1)

                    def normalize(n):
                        for u in range(2):
                            pool.wait_ge(sm["rsum_ready"], 2 * G(n) + u + 1)
                            pool.wait_ge(sm["pt_done"], 2 * G(n) + u - 1 + 4)
                            pool.tensor_tensor(me.pn[:, u, :, :], me.pr[:, u, :, :],
                                               me.rs[:, u, :].unsqueeze(2).broadcast_to([P, NPAIR, 2 * WIN]),
                                               ALU.mult).then_inc(sm["pn_ready"], 1)

                    def before():
                        add_parts(0)
                        scale(0, (0, 1))
                        add_parts(1)
                        scale(1, (0, 1))
                        add_parts(2)

                    def step(n, b, i, more4, more3, more2, more1):
                        if more2:
                            scale(n + 2, (0,))
                        normalize(n)
                        if more2:
                            scale(n + 2, (1,))
                        if more3:
                            add_parts(n + 3)

                    steps(pool, before, step, lambda: None)

                @block.scalar
                def _(act):
                    def squares(n, k):
                        act.wait_ge(sm["proj_done"], 2 * G(n) + k + 1 + 4)
                        act.wait_ge(sm["ssmax_ready"], 2 * G(n) + k - 1 + 4)
                        act.activation(me.sq[:, k, :], pa[:, 2 * k:2 * k + 2, :].rearrange("p a b -> p (a b)"),
                                       ACT.Square).then_inc(sm["sq_ready"], 1)

                    def inverse_norms(n, k):
                        act.wait_ge(sm["ssmax_ready"], 2 * G(n) + k + 1 + 4)
                        act.wait_ge(sm["qkn_ready"], 2 * G(n) + k - 1 + 2)
                        act.activation(me.rn[:, k, :], me.ss[:, k, :], ACT.Ln, scale=LN_RANGE).then_inc(sm["ln_step"], 1)
                        act.wait_ge(sm["ln_step"], 2 * G(n) + k + 1)
                        act.activation(me.rn[:, k, :], me.rn[:, k, :], ACT.Exp, scale=-0.5,
                                       bias=S.half_range[:, 0:1]).then_inc(sm["rn_ready"], 1)

                    def take_q(n):
                        for u in range(2):
                            act.wait_ge(sm["turn_done"], 4 * G(n) + u + 1 + 4)
                            act.wait_ge(sm["s_done"], 2 * G(n) + 4)
                            for half in range(2):
                                r = slice(64 * half, 64 * half + 64)
                                act.activation(me.qb[r, 4 * u:4 * u + 4, :, WIN * half:WIN * half + WIN],
                                               ring[r, u, :].rearrange("p (a w t) -> p a w t", a=4, w=NW),
                                               ACT.Identity).then_inc(sm["q_taken"], 1)

                    def exps(n):
                        for u in range(2):
                            act.wait_ge(sm["sub_ready"], 2 * G(n) + u + 1)
                            act.activation(me.pr[:, u, :, :], me.pr[:, u, :, :], ACT.Exp, scale=QK_SCALE).then_inc(sm["exp_ready"], 1)

                    def take_v(n, i):
                        for x in range(2):
                            act.wait_ge(sm["v_done"], 2 * G(n) + x + 1)
                            act.wait_ge(sm["o_done"], 2 * G(n) + 4)
                            act.activation(me.vs[:, i % 2, x, :], ring[:, 2 + x, :], ACT.Identity)
                            act.activation(me.vf[0:64, x, :], ring[0:64, 2 + x, :], ACT.Identity).then_inc(sm["v_taken"], 1)

                    def take_turned_weights(n):
                        for u in range(2):
                            act.wait_ge(sm["pt_done"], 2 * G(n) + u + 1 + 4)
                            turned = ring[:, 2 + u, :].rearrange("p (j w h t) -> p j w h t", j=4, w=2, h=2)
                            for parity in range(2):
                                at = 64 * parity
                                if u == 0:
                                    moves = ((me.pb[96:P, 0, :, parity, :, 0:WIN], at, 32, 0),
                                             (me.pb[0:32, 0, :, parity, :, 0:WIN], at + 32, 32, 0),
                                             (me.pb[0:64, 0, :, parity, :, WIN:], at, 64, 1))
                                else:
                                    moves = ((me.pb[32:64, 1, :, parity, :, 0:WIN], at, 32, 0),
                                             (me.pb[64:96, 1, :, parity, :, 0:WIN], at + 32, 32, 0),
                                             (me.pb[64:P, 1, :, parity, :, WIN:], at, 64, 1))
                                for to, row, rows, w in moves:
                                    ins = act.activation(to, turned[row:row + rows, :, w, :, :], ACT.Identity)
                                ins.then_inc(sm["pt_taken"], 1)

                    def take_weighted(n):
                        for half in range(2):
                            act.wait_ge(sm["o_done"], 2 * G(n) + half + 1 + 4)
                            act.wait_ge(sm["y_done"], G(n) + 4)
                            act.activation(me.os[:, 4 * half:4 * half + 4, :].rearrange("p a t -> p (a t)"), ring[:, half, :],
                                           ACT.Identity).then_inc(sm["o_taken"], 1)

                    def before():
                        act.preload_act_table_set("natural_log_exp_and_others")
                        for n in range(3):
                            for k in range(2):
                                squares(n, k)
                                inverse_norms(n, k)
                            if n == 1:
                                take_q(0)
                        exps(0)

                    def step(n, b, i, more4, more3, more2, more1):
                        if more1:
                            take_q(n + 1)
                        if more3:
                            squares(n + 3, 0)
                        take_v(n, i)
                        if more3:
                            inverse_norms(n + 3, 0)
                        take_turned_weights(n)
                        if more3:
                            squares(n + 3, 1)
                        if more1:
                            exps(n + 1)
                        take_weighted(n)
                        if more3:
                            inverse_norms(n + 3, 1)

                    steps(act, before, step, lambda: None)

                @block.vector
                def _(dve):
                    def tables():
                        dve.wait_ge(S.weights_a, weights_count)
                        scales = me.qks[:, :, :]
                        cos, sin = me.cs[:, 0, :, :, :], me.cs[:, 1, :, :, :]
                        dve.tensor_tensor(cos, me.rope[:, 0, :, :, :], scales.unsqueeze(1).broadcast_to([P, TT, 2, HD2]), ALU.mult)
                        hd = HD2 // 2
                        for half in range(2):
                            to, other = slice(hd * half, hd * half + hd), slice(hd * (1 - half), hd * (1 - half) + hd)
                            ins = dve.tensor_tensor(sin[:, :, :, to], me.rope[:, 1, :, :, to],
                                                    scales[:, :, other].unsqueeze(1).broadcast_to([P, TT, 2, hd]), ALU.mult)
                        ins.then_inc(sm["table_step"], 1)
                        dve.wait_ge(sm["table_step"], layer + 1)

                    def sums(n, k):
                        dve.wait_ge(sm["sq_ready"], 2 * G(n) + k + 1)
                        dve.tensor_reduce(me.ss[:, k, :], me.sq[:, k, :].rearrange("p (h d) -> p h d", h=H2), AX_X,
                                          ALU.add).then_inc(sm["ss_ready"], 1)
                        dve.wait_ge(sm["ss_ready"], 2 * G(n) + k + 1)
                        dve.wait_ge(sm["rn_ready"], 2 * G(n) + k - 1 + 4)
                        dve.tensor_scalar(me.ss[:, k, :], me.ss[:, k, :], 1e-24, None, ALU.max).then_inc(sm["ssmax_ready"], 1)

                    def rope(n, i, k):
                        hd = HD2 // 2
                        raw = pa[:, 2 * k:2 * k + 2, :].rearrange("p a (h d) -> p (a h) d", d=HD2)
                        dve.wait_ge(sm["add_ready"], 2 * G(n) + k - 1 + 2)
                        dve.wait_ge(sm["qkn_ready"], 2 * G(n) + k - 1 + 2)
                        dve.tensor_tensor(me.t1[:, k, :].rearrange("p (h d) -> p h d", h=H2), raw,
                                          me.cs[:, 0, i, k, :].unsqueeze(1).broadcast_to([P, H2, HD2]),
                                          ALU.mult).then_inc(sm["cos_ready"], 1)
                        t2 = me.t2[:, k, :].rearrange("p (h d) -> p h d", h=H2)
                        for half in range(2):
                            to, other = slice(hd * half, hd * half + hd), slice(hd * (1 - half), hd * (1 - half) + hd)
                            ins = dve.tensor_tensor(t2[:, :, to], raw[:, :, other],
                                                    me.cs[:, 1, i, k, to].unsqueeze(1).broadcast_to([P, H2, hd]), ALU.mult)
                        ins.then_inc(sm["sin_ready"], 1)

                    def take_k(n, i):
                        s = i % 2
                        for u in range(2):
                            dve.wait_ge(sm["turn_done"], 4 * G(n) + 2 + u + 1 + 4)
                            bank = ring[:, 2 + u, :].rearrange("p (a t) -> p a t", a=4)
                            dve.tensor_copy(me.kt[:, s, 4 * u:4 * u + 4, WIN:], bank)
                            dve.tensor_copy(me.kt[:, 1 - s, 4 * u:4 * u + 4, 0:WIN], bank[:, :, P - WIN:]).then_inc(sm["k_taken"], 1)

                    def softmax(n, u):
                        dve.wait_ge(sm["s_done"], 2 * G(n) + u + 1 + 4)
                        sc = ring[:, u, :].rearrange("p (a k) -> p a k", a=NPAIR)
                        dve.tensor_reduce(me.mx[:, u, :], sc, AX_X, ALU.max).then_inc(sm["max_ready"], 1)
                        dve.wait_ge(sm["max_ready"], 2 * G(n) + u + 1)
                        dve.wait_ge(sm["pn_ready"], 2 * G(n) + u - 1 + 4)
                        dve.tensor_tensor(me.pr[:, u, :, :], sc, me.mx[:, u, :].unsqueeze(2).broadcast_to([P, NPAIR, 2 * WIN]),
                                          ALU.subtract).then_inc(sm["sub_ready"], 1)

                    def totals(n):
                        for u in range(2):
                            dve.wait_ge(sm["exp_ready"], 2 * G(n) + u + 1)
                            dve.tensor_reduce(me.su[:, u, :], me.pr[:, u, :, :], AX_X, ALU.add).then_inc(sm["sum_ready"], 1)
                            dve.wait_ge(sm["sum_ready"], 2 * G(n) + u + 1)
                            dve.reciprocal(me.rs[:, u, :], me.su[:, u, :]).then_inc(sm["rsum_ready"], 1)

                    def add_x(n, b, i):
                        dve.wait_ge(sm["y_done"], G(n) + 1 + 4)
                        at = slice(PADW + P * i, PADW + P * i + P)
                        dve.tensor_tensor(dst[:, b, at], pa[:, 0, 0:P], src[:, b, at], ALU.add).then_inc(sm["x_ready"], 1)

                    def before():
                        tables()
                        for n in range(2):
                            for k in range(2):
                                sums(n, k)
                                rope(n, n, k)
                        take_k(0, 0)
                        sums(2, 0)
                        softmax(0, 0)
                        softmax(0, 1)
                        rope(2, 2, 0)
                        sums(2, 1)
                        rope(2, 2, 1)

                    def step(n, b, i, more4, more3, more2, more1):
                        if more1:
                            take_k(n + 1, (i + 1) % TT)
                        totals(n)
                        if more3:
                            sums(n + 3, 0)
                        if more1:
                            softmax(n + 1, 0)
                        if more3:
                            rope(n + 3, (i + 3) % TT, 0)
                        if more1:
                            softmax(n + 1, 1)
                        if more3:
                            sums(n + 3, 1)
                            rope(n + 3, (i + 3) % TT, 1)
                        add_x(n, b, i)

                    steps(dve, before, step, lambda: None)


def ffn_layer(core, F, layer, src, dst):
    nc, S, sm = core.nc, core, F.sm
    NC = 3
    sizes = [P, P, DI - 2 * P]
    with ExitStack() as ctx:
        pa = core.ps(ctx, "ff_pa", [P, NC, BANK])
        pg = core.ps(ctx, "ff_pg", [P, NC, BANK])
        py = core.ps(ctx, "ff_py", [P, 2, BANK])
        with nc.Block() as block:
            def loop(eng, one):
                with eng.Fori(0, B // 2) as r:
                    for u in range(2):
                        one(r * 2 + u, u)

            def G(b):
                return layer * B + b

            @block.tensor
            def _(pe):
                def one(b, u):
                    for c in range(NC):
                        pe.wait_ge(sm["gelu_ready"], NC * G(b) + c + 1)
                        pe.matmul(pg[0:sizes[c], c, :], F.w1[:, DI + P * c:DI + P * c + sizes[c]], S.h[:, b, :], start=True,
                                  stop=True).then_inc(sm["gate_done"], 1)
                        pe.wait_ge(sm["h_ready"], NC * G(b) + c + 1)
                        pe.matmul(pa[0:sizes[c], c, :], F.w1[:, P * c:P * c + sizes[c]], S.h[:, b, :], start=True,
                                  stop=True).then_inc(sm["a_done"], 1)
                    pe.wait_ge(sm["x_ready"], G(b) + 1)
                    for c in range(NC):
                        pe.wait_ge(sm["h_ready"], NC * G(b) + c + 4)
                        mm = pe.matmul(py[:, u, :], F.w2[0:sizes[c], c, :], F.hs[0:sizes[c], u, c, :], start=(c == 0),
                                       stop=(c == NC - 1))
                    mm.then_inc(sm["y_done"], 1)

                loop(pe, one)

            @block.scalar
            def _(act):
                def one(b, u):
                    for c in range(NC):
                        act.wait_ge(sm["gate_done"], NC * G(b) + c + 1)
                        act.wait_ge(sm["h_ready"], NC * G(b) + c + 1)
                        act.activation(F.gl[0:sizes[c], c, :], pg[0:sizes[c], c, :], ACT.Gelu,
                                       bias=F.b1[0:sizes[c], 3 + c:4 + c]).then_inc(sm["gelu_ready"], 1)

                act.preload_act_table_set("gelu_and_others")
                loop(act, one)

            @block.vector
            def _(dve):
                def one(b, u):
                    dve.wait_ge(sm["y_done"], G(b) + 1)
                    for c in range(NC):
                        dve.wait_ge(sm["a_done"], NC * G(b) + c + 1)
                        dve.wait_ge(sm["gelu_ready"], NC * G(b) + c + 4)
                        dve.scalar_tensor_tensor(out=F.hs[0:sizes[c], u, c, :], in0=pa[0:sizes[c], c, :],
                                                 scalar=F.b1[0:sizes[c], c:c + 1], in1=F.gl[0:sizes[c], c, :],
                                                 op0=ALU.add, op1=ALU.mult).then_inc(sm["h_ready"], 1)
                    dve.wait_ge(sm["y_done"], G(b) + 3)
                    dve.scalar_tensor_tensor(out=dst[:, b, PADW:], in0=py[:, u, :], scalar=F.b2[:, 0:1],
                                             in1=src[:, b, PADW:], op0=ALU.add, op1=ALU.add).then_inc(sm["x_ready"], 1)

                loop(dve, one)


class FeedForward:

    def __init__(self, core, ctx, work):
        self.sm = {n: core.sem("ff_" + n) for n in "gate_done a_done gelu_ready h_ready y_done x_ready".split()}
        sb = lambda name, shape: core.sb(ctx, "ff_" + name, shape)
        self.w1, self.w2 = sb("w1", [P, 2 * DI]), sb("w2", [P, 3, P])
        self.b1, self.b2, self.lnp = sb("b1", [P, 6]), sb("b2", [P, 1]), sb("ln", [P, 2])
        flat = work[:, :, :, :].rearrange("p a b c -> p (a b c)")
        self.hs = flat[:, 0:6 * T].rearrange("p (u c t) -> p u c t", u=2, c=3)
        self.gl = flat[:, 6 * T:9 * T].rearrange("p (c t) -> p c t", c=3)


def local_layers(core, A, C):
    nc, S = core.nc, core
    S.weights_a, S.weights_f, S.shifted = core.sem("weights_a"), core.sem("weights_f"), core.sem("shifted")
    added = core.sem("final_added")
    with ExitStack() as ctx:
        L = LocalAttention(core, ctx)
        F = FeedForward(core, ctx, L.work)

        def load_attention(sp, l):
            sp.dma_start(L.wqkv[:, :], A["L1_ffn_Wqkv"][l]).then_inc(S.weights_a, 16)
            sp.dma_start(L.wo[:, :, :], A["L1_ffn_Wo"][l].rearrange("(a p) d -> p a d", p=P)).then_inc(S.weights_a, 16)
            sp.dma_start(L.qks[:, 0, :], A["L1_ffn_q_scale"][l].partition_broadcast(P)).then_inc(S.weights_a, 16)
            sp.dma_start(L.qks[:, 1, :], A["L1_ffn_k_scale"][l].partition_broadcast(P)).then_inc(S.weights_a, 16)

        def load_feedforward(sp, l):
            sp.dma_start(F.w1[:, :], A["L1_ffn_W1"][l]).then_inc(S.weights_f, 16)
            sp.dma_start(F.w2[:, 0:2, :], A["L1_ffn_W2"][l][0:2 * P, :].rearrange("(a p) d -> p a d", p=P)).then_inc(S.weights_f, 16)
            sp.dma_start(F.w2[0:DI - 2 * P, 2, :], A["L1_ffn_W2"][l][2 * P:DI, :]).then_inc(S.weights_f, 16)
            for c in range(2):
                sp.dma_start(F.b1[:, 3 * c:3 * c + 2], A["L1_ffn_b1"][l][DI * c:DI * c + 2 * P].rearrange("(a p) -> p a", p=P)).then_inc(S.weights_f, 16)
                sp.dma_start(F.b1[0:DI - 2 * P, 3 * c + 2:3 * c + 3], column(A["L1_ffn_b1"][l][DI * c + 2 * P:DI * c + DI])).then_inc(S.weights_f, 16)
            for ap, n in ((F.b2[:, 0:1], "b2"), (F.lnp[:, 0:1], "ln_g"), (F.lnp[:, 1:2], "ln_b")):
                sp.dma_start(ap, column(A["L1_ffn_" + n][l])).then_inc(S.weights_f, 16)

        beside, counts = L.setup(C)
        norm_stage(S, lambda b: S.xr[:, b, :], lambda b: S.xa[:, b, PADW:],
                   lambda b: S.mod[:, 1, 4, b:b + 1], lambda b: S.mod[:, 1, 3, b:b + 1], beside=beside)(5 * B)
        norm = norm_stage(core, lambda b: S.h[:, b, :], lambda b: S.h[:, b, :], lambda b: F.lnp[:, 0:1], lambda b: F.lnp[:, 1:2],
                          shifted_from=S.xb)
        with nc.Block() as block:
            @block.sync
            def _(sp):
                load_attention(sp, 0)

            @block.vector
            def _(dve):
                counts(dve)
                dve.sem_inc(S.shifted, 6 * B)
                for n, k in (("gelu_ready", 3), ("h_ready", 3), ("x_ready", 2), ("y_done", 2)):
                    dve.sem_inc(F.sm[n], k)
        with nc.Fori(0, DEPTH) as layer:
            L.layer(layer, 64 * layer + 64, S.xa, S.xb, load_feedforward)
            with nc.Block() as block:
                @block.sync
                def _(sp):
                    sp.wait_ge(S.weights_f, 160 * layer + 160)
                    load_attention(sp, (layer + 1) % DEPTH)
            norm((layer + 6) * B)
            ffn_layer(core, F, layer, S.xb, S.xa)
        with nc.Block() as block:
            @block.sync
            def _(sp):
                sp.wait_ge(S.weights_a, 64 * DEPTH + 64)

            @block.vector
            def _(dve):
                for b in range(B):
                    dve.scalar_tensor_tensor(out=S.xr[:, b, :], in0=S.xa[:, b, PADW:], scalar=S.mod[:, 1, 5, b:b + 1],
                                             in1=S.xr[:, b, :], op0=ALU.mult, op1=ALU.add)


def program(nc, A, C, out):
    with ExitStack() as ctx:
        nc.disable_value_cache = True
        S = Core(nc, ctx)
        S.xr = S.sb(ctx, "xr", [P, B, T])
        S.h = S.sb(ctx, "h", [P, B, T])
        S.xa = S.sb(ctx, "xa", [P, B, XW])
        S.xb = S.sb(ctx, "xb", [P, B, XW])
        S.ident, S.mean, S.center = (S.sb(ctx, n, [P, P]) for n in ("ident", "mean", "center"))
        S.identb = S.sb(ctx, "identb", [P, P], BF16)
        S.mod = S.sb(ctx, "mod", [P, 2, 6, B])
        S.eps = S.sb(ctx, "eps", [P, 1])
        S.half_range = S.sb(ctx, "half_range", [P, 1])
        l0 = ctx.enter_context(ExitStack())
        S.cos0, S.sin0 = (S.sb(l0, n, [P, T]) for n in ("cos0", "sin0"))
        S.swap0 = S.sb(l0, "swap0", [P, P])
        S.pick = S.sb(l0, "pick", [P, E0, P], BF16)
        S.bq = S.sb(l0, "bq", [P, 4])
        S.bo0 = S.sb(l0, "bo0", [P, 1])
        S.bv0 = S.sb(l0, "bv0", [P, P])
        S.w0 = S.sb(l0, "w0", [P, 6, P])
        S.norms = 0
        S.norm_sems = [S.sem("norm_" + n) for n in ("centered", "squared", "var", "ln", "rstd", "scaled", "done")]
        S.constants_set = S.sem("constants_set")
        with nc.Block() as block:
            @block.vector
            def _(dve):
                dve.memset(S.eps[:, :], EPS).then_inc(S.constants_set, 1)
                dve.memset(S.half_range[:, :], float(0.5 * np.log(LN_RANGE))).then_inc(S.constants_set, 1)
                dve.wait_ge(S.constants_set, 2)
        prelude(S, A, C)
        norm_stage(S, lambda b: S.xr[:, b, :], lambda b: S.h[:, b, :],
                   lambda b: S.mod[:, 0, 1, b:b + 1], lambda b: S.mod[:, 0, 0, b:b + 1])(0)
        attention0(S)
        ffn0(S, A, C)
        l0.close()
        attention1(S, A, C)
        local_layers(S, A, C)
        store(S, out, S.xr)


def store(core, out, src):
    nc, S = core.nc, core
    turned, taken, stored = core.sem("out_turned"), core.sem("out_taken"), core.sem("out_stored")
    with ExitStack() as ctx:
        px = core.ps(ctx, "out_px", [P, 4, BANK])
        xt = core.sb(ctx, "out_tokens", [P, B, T])
        with nc.Block() as block:
            @block.tensor
            def _(pe):
                for n in range(B):
                    if n >= 4:
                        pe.wait_ge(taken, n - 3)
                    for c in range(TT):
                        tr = pe.transpose(px[:, n % 4, P * c:P * c + P], src[:, n, P * c:P * c + P], S.ident[:, :])
                    tr.then_inc(turned, 1)

            @block.scalar
            def _(act):
                for n in range(B):
                    act.wait_ge(turned, n + 1)
                    act.activation(xt[:, n, :], px[:, n % 4, :], ACT.Identity).then_inc(taken, 1)

            @block.sync
            def _(sp):
                for n in range(B):
                    sp.wait_ge(taken, n + 1)
                    sp.dma_start(out[n].rearrange("(c p) d -> p c d", p=P),
                                 xt[:, n, :].rearrange("p (c d) -> p c d", c=TT)).then_inc(stored, 16)
                sp.wait_ge(stored, 16 * B)


INPUTS = ['L0_attn_x', 'L0_attn_Wq', 'L0_attn_bq', 'L0_attn_Wk', 'L0_attn_bk', 'L0_attn_Wv', 'L0_attn_bv', 'L0_attn_Wo',
          'L0_attn_bo', 'L0_ffn_g1', 'L0_ffn_be1', 'L0_ffn_mix_w', 'L0_ffn_mix_b', 'L0_ffn_g2', 'L0_ffn_be2',
          'L0_ffn_router_w', 'L0_ffn_w1', 'L0_ffn_b1', 'L0_ffn_w2', 'L0_ffn_b2', 'L0_c', 'L0_wmod', 'L1_attn_phase',
          'L1_attn_Wq', 'L1_attn_bq', 'L1_attn_Wk', 'L1_attn_bk', 'L1_attn_Wv', 'L1_attn_bv', 'L1_attn_Wo', 'L1_attn_bo',
          'L1_ffn_Wqkv', 'L1_ffn_q_scale', 'L1_ffn_k_scale', 'L1_ffn_Wo', 'L1_ffn_ln_g', 'L1_ffn_ln_b', 'L1_ffn_W1',
          'L1_ffn_b1', 'L1_ffn_W2', 'L1_ffn_b2', 'L1_c', 'L1_wmod']


def kernel(**inputs):
    import concourse.bacc as bacc
    from concourse.bass_utils import run_bass_kernel_spmd

    nc = bacc.Bacc("TRN2", target_bir_lowering=False, num_devices=1)
    arrays, args, tables = {}, {}, {}
    for name in INPUTS:
        a = np.ascontiguousarray(inputs[name])
        arrays[f"in_{name}"] = a
        args[name] = nc.dram_tensor(f"in_{name}", a.shape, mybir.dt.from_np(a.dtype), kind="ExternalInput").ap()
    for name, a in constants().items():
        a = np.ascontiguousarray(a)
        arrays[f"const_{name}"] = a
        tables[name] = nc.dram_tensor(f"const_{name}", a.shape, mybir.dt.from_np(a.dtype), kind="ExternalInput").ap()
    out = nc.dram_tensor("out", (B, T, D), F32, kind="ExternalOutput").ap()
    program(nc, args, tables, out)
    r = run_bass_kernel_spmd(nc, [arrays], core_ids=[0])
    return r.results[0]["out"]
```
